# Optimizing a Trainium2 kernel written in Bass

```python
import numpy as np
import jax
import jax.numpy as jnp

def _softmax(x, axis=-1):
    return jax.nn.softmax(x, axis=axis)

def _gelu(x):
    return jax.nn.gelu(x, approximate=True)

def _silu(x):
    return jax.nn.silu(x)

def _sigmoid(x):
    return jax.nn.sigmoid(x)

def _layernorm(x, axis=-1, eps=1e-05):
    m = jnp.mean(x, axis=axis, keepdims=True)
    v = jnp.var(x, axis=axis, keepdims=True)
    return (x - m) / jnp.sqrt(v + eps)

def _scatter_add(tgt, idx, src, axis=0):
    return tgt.at[idx].add(src)

def _segment_sum(src, seg, n):
    return jax.ops.segment_sum(src, seg, n)
kernel_name = 'mk_perceiver_d2_seqx_r8_5e2497'

def setup_inputs(seed: int=0):
    np.random.seed(seed)
    _w = jnp.asarray

    def _rec_inputs():
        import jax
        import jax.numpy as jnp
        _rk = jax.random.key(seed)
        x = -0.0002928 + 1 * jax.random.normal(jax.random.fold_in(_rk, 1), (1, 128, 512), jnp.float32)
        _lenS = 128 - jax.random.randint(jax.random.fold_in(_rk, 7), (1,), 0, max(1, 128 // 4) + 1, jnp.int32)
        _lenS2 = 2048 - jax.random.randint(jax.random.fold_in(_rk, 8), (1,), 0, max(1, 2048 // 4) + 1, jnp.int32)
        _ctx_4096P = jax.random.normal(jax.random.fold_in(_rk, 11), (1, 16, 512), jnp.float32)
        _ctx_4096c = jax.random.dirichlet(jax.random.fold_in(_rk, 511), 0.3 * jnp.ones((16,), jnp.float32), (1, 2048))
        _ctx_4096t = jnp.einsum('bsk,bkd->bsd', _ctx_4096c, _ctx_4096P)
        _ctx_4096t = _ctx_4096t * jax.lax.rsqrt(jnp.mean(jnp.square(_ctx_4096t)) + 1e-12) * 0.953939
        ctx_4096 = -2.8382e-05 + 0.999851 * (_ctx_4096t + 0.3 * jax.random.normal(jax.random.fold_in(_rk, 611), (1, 2048, 512), jnp.float32))
        _validS = jnp.arange(128)[None, :] < _lenS[:, None]
        _validS2 = jnp.arange(2048)[None, :] < _lenS2[:, None]
        _causal = jnp.tril(jnp.ones((128, 128), dtype=bool))
        mask_1x1xSxS2_ff0 = jnp.where(jnp.ones((1, 1, 128, 2048), dtype=bool), 0.0, -1000000000.0).astype(jnp.float32)
        return (x, ctx_4096, mask_1x1xSxS2_ff0)
    x, ctx_4096, mask_1x1xSxS2_ff0 = _rec_inputs()

    def _L0_xattn_setup():
        import jax, jax.numpy as jnp
        import numpy as np
        NUM_HEADS = 32
        NUM_KV_HEADS = 8
        HEAD_DIM = 128
        HIDDEN = 512
        EPS = 1e-05

        def rmsnorm(x, w, eps=EPS):
            xf = x.astype(jnp.float32)
            var = jnp.mean(xf * xf, axis=-1, keepdims=True)
            return w * (xf * jax.lax.rsqrt(var + eps)).astype(x.dtype)
        key = jax.random.key(seed)
        ks = jax.random.split(key, 10)
        B, Q, KV = (1, 128, 6404)
        s = 1.0 / np.sqrt(HIDDEN)
        return {'hidden_states': jax.random.normal(ks[0], (B, Q, HIDDEN), jnp.float32), 'cross_attention_states': jax.random.normal(ks[1], (B, KV, HIDDEN), jnp.float32), 'attention_mask': jnp.zeros((B, 1, Q, KV), jnp.float32), 'q_proj_w': jax.random.normal(ks[2], (NUM_HEADS * HEAD_DIM, HIDDEN), jnp.float32) * s, 'k_proj_w': jax.random.normal(ks[3], (NUM_KV_HEADS * HEAD_DIM, HIDDEN), jnp.float32) * s, 'v_proj_w': jax.random.normal(ks[4], (NUM_KV_HEADS * HEAD_DIM, HIDDEN), jnp.float32) * s, 'o_proj_w': jax.random.normal(ks[5], (HIDDEN, NUM_HEADS * HEAD_DIM), jnp.float32) * s, 'q_norm_w': jnp.ones((HEAD_DIM,), jnp.float32), 'k_norm_w': jnp.ones((HEAD_DIM,), jnp.float32)}
    _L0_xattn_all = _L0_xattn_setup()
    _L0_xattn_in = {k: v for k, v in _L0_xattn_all.items() if k in ('q_proj_w', 'k_proj_w', 'v_proj_w', 'o_proj_w', 'q_norm_w', 'k_norm_w')}
    del _L0_xattn_all

    def _L0_attn_setup():
        import jax, jax.numpy as jnp
        import numpy as np
        D_MODEL = 512
        N_Q = 32
        N_KV = 8
        HD = 128
        SLIDE = 64

        def _gqa_swa_attention(q, k, v, slide):
            B, Hq, N, D = q.shape
            Hkv = k.shape[1]
            G = Hq // Hkv
            qg = q.reshape(B, Hkv, G, N, D)
            scale = 1.0 / jnp.sqrt(jnp.asarray(D, q.dtype))
            s = jnp.einsum('bhgnd,bhmd->bhgnm', qg, k) * scale
            i = jnp.arange(N)[:, None]
            j = jnp.arange(N)[None, :]
            mask = j <= i
            if slide > 0:
                mask = mask & (i - j < slide)
            s = jnp.where(mask[None, None, None], s, jnp.asarray(-jnp.inf, s.dtype))
            p = jax.nn.softmax(s, axis=-1)
            o = jnp.einsum('bhgnm,bhmd->bhgnd', p, v)
            return o.reshape(B, Hq, N, D)
        key = jax.random.key(seed)
        ks = jax.random.split(key, 5)
        std = 0.01
        x = jax.random.normal(ks[0], (2, 256, D_MODEL), dtype=jnp.float32)
        wq = jax.random.normal(ks[1], (N_Q * HD, D_MODEL), dtype=jnp.float32) * std
        wk = jax.random.normal(ks[2], (N_KV * HD, D_MODEL), dtype=jnp.float32) * std
        wv = jax.random.normal(ks[3], (N_KV * HD, D_MODEL), dtype=jnp.float32) * std
        wo = jax.random.normal(ks[4], (D_MODEL, N_Q * HD), dtype=jnp.float32) * std
        return {'x': x, 'wq': wq, 'wk': wk, 'wv': wv, 'wo': wo}
    _L0_attn_all = _L0_attn_setup()
    _L0_attn_in = {k: v for k, v in _L0_attn_all.items() if k in ('wq', 'wk', 'wv', 'wo')}
    del _L0_attn_all

    def _L0_ffn_setup():
        import jax, jax.numpy as jnp
        import numpy as np
        K_TOP = 8
        key = jax.random.key(seed)
        k1, k2, k3 = jax.random.split(key, 3)
        B, S, H, E = (4, 512, 512, 64)
        hidden_states = jax.random.normal(k1, (B, S, H), dtype=jnp.float32)
        router_weight = jax.random.normal(k2, (E, H), dtype=jnp.float32)
        router_bias = jnp.zeros((E,), dtype=jnp.float32)
        expert_bias = jax.random.normal(k3, (E, H), dtype=jnp.float32) * 0.1
        return {'hidden_states': hidden_states, 'router_weight': router_weight, 'router_bias': router_bias, 'expert_bias': expert_bias}
    _L0_ffn_all = _L0_ffn_setup()
    _L0_ffn_in = {k: v for k, v in _L0_ffn_all.items() if k in ('router_weight', 'router_bias', 'expert_bias')}
    del _L0_ffn_all

    def _L1_xattn_setup():
        import jax, jax.numpy as jnp
        import numpy as np
        TEXT_DIM = 512
        FEATURE_DIM = 512

        def _xavier_uniform(key, shape):
            fan_in, fan_out = (shape[1], shape[0])
            limit = float(np.sqrt(6.0 / (fan_in + fan_out)))
            return jax.random.uniform(key, shape, jnp.float32, -limit, limit)
        key = jax.random.key(seed)
        k1, k2, k3, k4 = jax.random.split(key, 4)
        text = jax.random.normal(k1, (8, 256, TEXT_DIM), jnp.float32)
        features = jax.random.normal(k2, (8, 72, FEATURE_DIM), jnp.float32)
        Wq = _xavier_uniform(k3, (FEATURE_DIM, TEXT_DIM))
        bq = jnp.zeros((FEATURE_DIM,), jnp.float32)
        Wk = _xavier_uniform(k4, (FEATURE_DIM, FEATURE_DIM))
        bk = jnp.zeros((FEATURE_DIM,), jnp.float32)
        return {'text': text, 'features': features, 'Wq': Wq, 'bq': bq, 'Wk': Wk, 'bk': bk}
    _L1_xattn_all = _L1_xattn_setup()
    _L1_xattn_in = {k: v for k, v in _L1_xattn_all.items() if k in ('Wq', 'bq', 'Wk', 'bk')}
    del _L1_xattn_all

    def _L1_attn_setup():
        import jax, jax.numpy as jnp
        import numpy as np
        H_SIZE = 512
        NH = 128
        HD = 64
        SS = 128
        K = 4
        NG = 8
        CHUNK = 128
        INTER = NH * HD
        CONV_DIM = INTER + 2 * NG * SS
        PROJ = INTER + CONV_DIM + NH
        DT_MIN, DT_MAX = (0.001, 100.0)
        EPS = 1e-05
        GROUP = INTER // NG

        def _ssd(x, Bm, Cm, D, dt, dt_bias):
            Bsz, S, H, P = x.shape
            N = Bm.shape[-1]
            A = -jnp.arange(1, H + 1, dtype=jnp.float32)
            dt = jnp.clip(jax.nn.softplus(dt + dt_bias), DT_MIN, DT_MAX)
            rep = H // Bm.shape[2]
            Bh = jnp.repeat(Bm, rep, axis=2)
            Ch = jnp.repeat(Cm, rep, axis=2)
            nc, L = (S // CHUNK, CHUNK)
            xc = x.reshape(Bsz, nc, L, H, P)
            dtc = dt.reshape(Bsz, nc, L, H)
            Bc = Bh.reshape(Bsz, nc, L, H, N)
            Cc = Ch.reshape(Bsz, nc, L, H, N)
            dA = jnp.swapaxes(dtc, 2, 3) * A[None, None, :, None]
            cs = jnp.cumsum(dA, axis=-1)
            seg = cs[..., :, None] - cs[..., None, :]
            tri = jnp.tril(jnp.ones((L, L), dtype=bool))
            Lmat = jnp.where(tri, jnp.exp(seg), 0.0)
            xdt = xc * dtc[..., None]
            scores = jnp.einsum('bclhn,bcshn->bchls', Cc, Bc) * Lmat
            Ydiag = jnp.einsum('bchls,bcshp->bclhp', scores, xdt)
            decay_states = jnp.exp(cs[..., -1:] - cs)
            states = jnp.einsum('bclhn,bchl,bclhp->bchpn', Bc, decay_states, xdt)
            chunk_decay = jnp.exp(cs[..., -1])

            def step(carry, inp):
                st, cd = inp
                new = carry * cd[:, :, None, None] + st
                return (new, carry)
            st_seq = jnp.moveaxis(states, 1, 0)
            cd_seq = jnp.moveaxis(chunk_decay, 1, 0)
            init = jnp.zeros_like(st_seq[0])
            _, prev = jax.lax.scan(step, init, (st_seq, cd_seq))
            prev = jnp.moveaxis(prev, 0, 1)
            Yoff = jnp.einsum('bclhn,bchpn,bchl->bclhp', Cc, prev, jnp.exp(cs))
            Y = (Ydiag + Yoff).reshape(Bsz, S, H, P) + x * D[None, None, :, None]
            return Y
        key = jax.random.key(seed)
        ks = jax.random.split(key, 5)
        s = 0.02
        return {'hidden_states': jax.random.normal(ks[0], (1, 256, H_SIZE), jnp.float32), 'in_proj_w': jax.random.normal(ks[1], (PROJ, H_SIZE), jnp.float32) * s, 'conv_w': jax.random.normal(ks[2], (CONV_DIM, 1, K), jnp.float32) * 0.1, 'conv_b': jnp.zeros((CONV_DIM,), jnp.float32), 'dt_bias': jnp.ones((NH,), jnp.float32), 'D': jnp.ones((NH,), jnp.float32), 'norm_w': jnp.ones((INTER,), jnp.float32), 'out_proj_w': jax.random.normal(ks[3], (H_SIZE, INTER), jnp.float32) * s}
    _L1_attn_all = _L1_attn_setup()
    _L1_attn_in = {k: v for k, v in _L1_attn_all.items() if k in ('in_proj_w', 'conv_w', 'conv_b', 'dt_bias', 'D', 'norm_w', 'out_proj_w')}
    del _L1_attn_all

    def _L1_ffn_setup():
        import jax, jax.numpy as jnp
        import numpy as np
        TOP_K = 2
        key = jax.random.key(seed)
        k1, k2, k3 = jax.random.split(key, 3)
        B, S, H, O, E = (1024, 1, 512, 512, 8)
        x = jax.random.normal(k1, (B, S, H), dtype=jnp.float32)
        gate_w = jax.random.normal(k2, (H, E), dtype=jnp.float32) * 0.02
        expert_w = jax.random.normal(k3, (E, H, O), dtype=jnp.float32) * 0.02
        return {'x': x, 'gate_w': gate_w, 'expert_w': expert_w}
    _L1_ffn_all = _L1_ffn_setup()
    _L1_ffn_in = {k: v for k, v in _L1_ffn_all.items() if k in ('gate_w', 'expert_w')}
    del _L1_ffn_all
    return {'x': x, 'ctx_4096': ctx_4096, 'mask_1x1xSxS2_ff0': mask_1x1xSxS2_ff0, 'L0_xattn_q_proj_w': _L0_xattn_in['q_proj_w'], 'L0_xattn_k_proj_w': _L0_xattn_in['k_proj_w'], 'L0_xattn_v_proj_w': _L0_xattn_in['v_proj_w'], 'L0_xattn_o_proj_w': _L0_xattn_in['o_proj_w'], 'L0_xattn_q_norm_w': _L0_xattn_in['q_norm_w'], 'L0_xattn_k_norm_w': _L0_xattn_in['k_norm_w'], 'L0_attn_wq': _L0_attn_in['wq'], 'L0_attn_wk': _L0_attn_in['wk'], 'L0_attn_wv': _L0_attn_in['wv'], 'L0_attn_wo': _L0_attn_in['wo'], 'L0_ffn_router_weight': _L0_ffn_in['router_weight'], 'L0_ffn_router_bias': _L0_ffn_in['router_bias'], 'L0_ffn_expert_bias': _L0_ffn_in['expert_bias'], 'L1_xattn_Wq': _L1_xattn_in['Wq'], 'L1_xattn_bq': _L1_xattn_in['bq'], 'L1_xattn_Wk': _L1_xattn_in['Wk'], 'L1_xattn_bk': _L1_xattn_in['bk'], 'L1_attn_in_proj_w': _L1_attn_in['in_proj_w'], 'L1_attn_conv_w': _L1_attn_in['conv_w'], 'L1_attn_conv_b': _L1_attn_in['conv_b'], 'L1_attn_dt_bias': _L1_attn_in['dt_bias'], 'L1_attn_D': _L1_attn_in['D'], 'L1_attn_norm_w': _L1_attn_in['norm_w'], 'L1_attn_out_proj_w': _L1_attn_in['out_proj_w'], 'L1_ffn_gate_w': _L1_ffn_in['gate_w'], 'L1_ffn_expert_w': _L1_ffn_in['expert_w']}

def reference(x, ctx_4096, mask_1x1xSxS2_ff0, L0_xattn_q_proj_w, L0_xattn_k_proj_w, L0_xattn_v_proj_w, L0_xattn_o_proj_w, L0_xattn_q_norm_w, L0_xattn_k_norm_w, L0_attn_wq, L0_attn_wk, L0_attn_wv, L0_attn_wo, L0_ffn_router_weight, L0_ffn_router_bias, L0_ffn_expert_bias, L1_xattn_Wq, L1_xattn_bq, L1_xattn_Wk, L1_xattn_bk, L1_attn_in_proj_w, L1_attn_conv_w, L1_attn_conv_b, L1_attn_dt_bias, L1_attn_D, L1_attn_norm_w, L1_attn_out_proj_w, L1_ffn_gate_w, L1_ffn_expert_w):
    import jax
    import jax.numpy as jnp

    def _L0_xattn_ref(hidden_states, cross_attention_states, attention_mask, q_proj_w, k_proj_w, v_proj_w, o_proj_w, q_norm_w, k_norm_w):
        import jax, jax.numpy as jnp
        import numpy as np
        NUM_HEADS = 32
        NUM_KV_HEADS = 8
        HEAD_DIM = 128
        HIDDEN = 512
        EPS = 1e-05

        def rmsnorm(x, w, eps=EPS):
            xf = x.astype(jnp.float32)
            var = jnp.mean(xf * xf, axis=-1, keepdims=True)
            return w * (xf * jax.lax.rsqrt(var + eps)).astype(x.dtype)
        B, Q, _ = hidden_states.shape
        KV = cross_attention_states.shape[1]
        n_rep = NUM_HEADS // NUM_KV_HEADS
        q = (hidden_states @ q_proj_w.T).reshape(B, Q, NUM_HEADS, HEAD_DIM).transpose(0, 2, 1, 3)
        k = (cross_attention_states @ k_proj_w.T).reshape(B, KV, NUM_KV_HEADS, HEAD_DIM).transpose(0, 2, 1, 3)
        v = (cross_attention_states @ v_proj_w.T).reshape(B, KV, NUM_KV_HEADS, HEAD_DIM).transpose(0, 2, 1, 3)
        q = rmsnorm(q, q_norm_w)
        k = jnp.repeat(k, n_rep, axis=1)
        v = jnp.repeat(v, n_rep, axis=1)
        k = rmsnorm(k, k_norm_w)
        scale = 1.0 / np.sqrt(HEAD_DIM)
        scores = jnp.einsum('bhqd,bhkd->bhqk', q, k) * scale + attention_mask
        attn = jax.nn.softmax(scores.astype(jnp.float32), axis=-1).astype(q.dtype)
        out = jnp.einsum('bhqk,bhkd->bhqd', attn, v)
        out = out.transpose(0, 2, 1, 3).reshape(B, Q, NUM_HEADS * HEAD_DIM)
        return out @ o_proj_w.T

    def _L0_attn_ref(x, wq, wk, wv, wo):
        import jax, jax.numpy as jnp
        import numpy as np
        D_MODEL = 512
        N_Q = 32
        N_KV = 8
        HD = 128
        SLIDE = 64

        def _gqa_swa_attention(q, k, v, slide):
            B, Hq, N, D = q.shape
            Hkv = k.shape[1]
            G = Hq // Hkv
            qg = q.reshape(B, Hkv, G, N, D)
            scale = 1.0 / jnp.sqrt(jnp.asarray(D, q.dtype))
            s = jnp.einsum('bhgnd,bhmd->bhgnm', qg, k) * scale
            i = jnp.arange(N)[:, None]
            j = jnp.arange(N)[None, :]
            mask = j <= i
            if slide > 0:
                mask = mask & (i - j < slide)
            s = jnp.where(mask[None, None, None], s, jnp.asarray(-jnp.inf, s.dtype))
            p = jax.nn.softmax(s, axis=-1)
            o = jnp.einsum('bhgnm,bhmd->bhgnd', p, v)
            return o.reshape(B, Hq, N, D)
        B, N, _ = x.shape
        q = (x @ wq.T).reshape(B, N, N_Q, HD).transpose(0, 2, 1, 3)
        k = (x @ wk.T).reshape(B, N, N_KV, HD).transpose(0, 2, 1, 3)
        v = (x @ wv.T).reshape(B, N, N_KV, HD).transpose(0, 2, 1, 3)
        o = _gqa_swa_attention(q, k, v, SLIDE)
        o = o.transpose(0, 2, 1, 3).reshape(B, N, N_Q * HD)
        return o @ wo.T

    def _L0_ffn_ref(hidden_states, router_weight, router_bias, expert_bias):
        import jax, jax.numpy as jnp
        import numpy as np
        K_TOP = 8
        B, S, H = hidden_states.shape
        E = router_weight.shape[0]
        T = B * S
        flat = hidden_states.reshape(T, H)
        logits = jnp.einsum('th,eh->te', flat, router_weight) + router_bias
        scores = jax.nn.softmax(logits, axis=-1)
        topk_w, topk_idx = jax.lax.top_k(scores, K_TOP)
        w_sum = topk_w.sum(axis=-1, keepdims=True)
        w_dense = jnp.zeros((T, E), dtype=scores.dtype).at[jnp.arange(T)[:, None], topk_idx].add(topk_w)
        bias_mix = jnp.einsum('te,eh->th', w_dense, expert_bias)
        out = flat * w_sum + bias_mix
        return out.reshape(B, S, H)

    def _L1_xattn_ref(text, features, Wq, bq, Wk, bk):
        import jax, jax.numpy as jnp
        import numpy as np
        TEXT_DIM = 512
        FEATURE_DIM = 512

        def _xavier_uniform(key, shape):
            fan_in, fan_out = (shape[1], shape[0])
            limit = float(np.sqrt(6.0 / (fan_in + fan_out)))
            return jax.random.uniform(key, shape, jnp.float32, -limit, limit)
        Q = jnp.einsum('btx,dx->btd', text, Wq) + bq
        K = jnp.einsum('bpx,dx->bpd', features, Wk) + bk
        scale = 1.0 / jnp.sqrt(jnp.asarray(K.shape[-1], K.dtype))
        scores = jnp.einsum('btd,bpd->btp', Q, K) * scale
        attn = jax.nn.softmax(scores, axis=-1)
        attended = jnp.einsum('btp,bpd->btd', attn, features)
        return attended

    def _L1_attn_ref(hidden_states, in_proj_w, conv_w, conv_b, dt_bias, D, norm_w, out_proj_w):
        import jax, jax.numpy as jnp
        import numpy as np
        H_SIZE = 512
        NH = 128
        HD = 64
        SS = 128
        K = 4
        NG = 8
        CHUNK = 128
        INTER = NH * HD
        CONV_DIM = INTER + 2 * NG * SS
        PROJ = INTER + CONV_DIM + NH
        DT_MIN, DT_MAX = (0.001, 100.0)
        EPS = 1e-05
        GROUP = INTER // NG

        def _ssd(x, Bm, Cm, D, dt, dt_bias):
            Bsz, S, H, P = x.shape
            N = Bm.shape[-1]
            A = -jnp.arange(1, H + 1, dtype=jnp.float32)
            dt = jnp.clip(jax.nn.softplus(dt + dt_bias), DT_MIN, DT_MAX)
            rep = H // Bm.shape[2]
            Bh = jnp.repeat(Bm, rep, axis=2)
            Ch = jnp.repeat(Cm, rep, axis=2)
            nc, L = (S // CHUNK, CHUNK)
            xc = x.reshape(Bsz, nc, L, H, P)
            dtc = dt.reshape(Bsz, nc, L, H)
            Bc = Bh.reshape(Bsz, nc, L, H, N)
            Cc = Ch.reshape(Bsz, nc, L, H, N)
            dA = jnp.swapaxes(dtc, 2, 3) * A[None, None, :, None]
            cs = jnp.cumsum(dA, axis=-1)
            seg = cs[..., :, None] - cs[..., None, :]
            tri = jnp.tril(jnp.ones((L, L), dtype=bool))
            Lmat = jnp.where(tri, jnp.exp(seg), 0.0)
            xdt = xc * dtc[..., None]
            scores = jnp.einsum('bclhn,bcshn->bchls', Cc, Bc) * Lmat
            Ydiag = jnp.einsum('bchls,bcshp->bclhp', scores, xdt)
            decay_states = jnp.exp(cs[..., -1:] - cs)
            states = jnp.einsum('bclhn,bchl,bclhp->bchpn', Bc, decay_states, xdt)
            chunk_decay = jnp.exp(cs[..., -1])

            def step(carry, inp):
                st, cd = inp
                new = carry * cd[:, :, None, None] + st
                return (new, carry)
            st_seq = jnp.moveaxis(states, 1, 0)
            cd_seq = jnp.moveaxis(chunk_decay, 1, 0)
            init = jnp.zeros_like(st_seq[0])
            _, prev = jax.lax.scan(step, init, (st_seq, cd_seq))
            prev = jnp.moveaxis(prev, 0, 1)
            Yoff = jnp.einsum('bclhn,bchpn,bchl->bclhp', Cc, prev, jnp.exp(cs))
            Y = (Ydiag + Yoff).reshape(Bsz, S, H, P) + x * D[None, None, :, None]
            return Y
        Bsz, S, _ = hidden_states.shape
        proj = hidden_states @ in_proj_w.T
        gate, xBC, dt = jnp.split(proj, [INTER, INTER + CONV_DIM], axis=-1)
        xBC_t = jnp.swapaxes(xBC, 1, 2)
        conv = jax.lax.conv_general_dilated(xBC_t, conv_w, window_strides=(1,), padding=[(K - 1, 0)], feature_group_count=CONV_DIM)
        conv = conv + conv_b[None, :, None]
        xBC = jax.nn.silu(jnp.swapaxes(conv, 1, 2))
        x, Bm, Cm = jnp.split(xBC, [INTER, INTER + NG * SS], axis=-1)
        y = _ssd(x.reshape(Bsz, S, NH, HD), Bm.reshape(Bsz, S, NG, SS), Cm.reshape(Bsz, S, NG, SS), D, dt, dt_bias)
        y = y.reshape(Bsz, S, INTER)
        yg = y * jax.nn.silu(gate)
        yg_g = yg.reshape(Bsz, S, NG, GROUP)
        rstd = jax.lax.rsqrt(jnp.mean(jnp.square(yg_g), axis=-1, keepdims=True) + EPS)
        out = (yg_g * rstd).reshape(Bsz, S, INTER) * norm_w
        return out @ out_proj_w.T

    def _L1_ffn_ref(x, gate_w, expert_w):
        import jax, jax.numpy as jnp
        import numpy as np
        TOP_K = 2
        E = gate_w.shape[-1]
        logits = jnp.einsum('bsh,he->bse', x, gate_w)
        topv, topi = jax.lax.top_k(logits, TOP_K)
        w = jax.nn.softmax(topv, axis=-1)
        onehot = jax.nn.one_hot(topi, E, dtype=x.dtype)
        w_e = jnp.einsum('bske,bsk->bse', onehot, w)
        out = jnp.einsum('bsh,eho,bse->bso', x, expert_w, w_e)
        return out
    x = x + _L0_xattn_ref(_layernorm(x, axis=-1), ctx_4096, mask_1x1xSxS2_ff0, L0_xattn_q_proj_w, L0_xattn_k_proj_w, L0_xattn_v_proj_w, L0_xattn_o_proj_w, L0_xattn_q_norm_w, L0_xattn_k_norm_w)
    x = x + _L0_attn_ref(_layernorm(x, axis=-1), L0_attn_wq, L0_attn_wk, L0_attn_wv, L0_attn_wo)
    x = x + _L0_ffn_ref(_layernorm(x, axis=-1), L0_ffn_router_weight, L0_ffn_router_bias, L0_ffn_expert_bias)
    x = x + _L1_xattn_ref(_layernorm(x, axis=-1), ctx_4096, L1_xattn_Wq, L1_xattn_bq, L1_xattn_Wk, L1_xattn_bk)
    x = x + _L1_attn_ref(_layernorm(x, axis=-1), L1_attn_in_proj_w, L1_attn_conv_w, L1_attn_conv_b, L1_attn_dt_bias, L1_attn_D, L1_attn_norm_w, L1_attn_out_proj_w)
    x = x + _L1_ffn_ref(_layernorm(x, axis=-1), L1_ffn_gate_w, L1_ffn_expert_w)
    return x

_drawn_inputs = setup_inputs


def setup_inputs(seed=0):
    import zlib

    import numpy as np

    out = dict(_drawn_inputs(seed))
    spreads = {'L0_xattn_q_norm_w': (1.0, 0.2),
     'L0_xattn_k_norm_w': (1.0, 0.2),
     'L0_ffn_router_bias': (0.0, 0.8),
     'L1_xattn_bq': (0.0, 0.632),
     'L1_xattn_bk': (0.0, 0.8),
     'L1_attn_conv_b': (0.0, 0.1),
     'L1_attn_dt_bias': (1.0, 0.6),
     'L1_attn_D': (1.0, 0.2),
     'L1_attn_norm_w': (1.0, 0.2)}
    factors = {'L0_attn_wq': 8.0, 'L0_attn_wk': 8.0}
    for name, (base, spread) in spreads.items():
        noise = np.random.default_rng([zlib.crc32(name.encode()), seed]).standard_normal(out[name].shape)
        drawn = base * np.exp(spread * noise) if base else spread * noise
        out[name] = jnp.asarray(drawn.astype(out[name].dtype))
    for name, factor in factors.items():
        out[name] = (out[name] * factor).astype(out[name].dtype)
    return out
```

```python
from contextlib import ExitStack

import concourse.bass as bass
from concourse import mybir

F32 = mybir.dt.float32
F32R = mybir.dt.float32r
ALU = mybir.AluOpType
ACT = mybir.ActivationFunctionType
AX = mybir.AxisListType

P = 128
D = 512
KC = D // P
EPS = 1e-5
NEG = -3.0e38
DMA = 16

T = 2048
TT = T // P
TB = T // 512
HD = 128
NG = 8
R = 4
SCALE = HD ** -0.5
SLIDE = 64
E = 64
TOP = 8
MH = 16
MP = 64
MC = MH * MP
MCC = MC // P
NCH = MCC + 2
TAPS = 4
STEPS = NCH * (TAPS - 1)
DT_STEPS = 11
DT_MIN, DT_MAX = 1e-3, 100.0
NE = 8
TOP2 = 2
PR = 3

SBUF0 = 16512
SBUF_BYTES = 212832


def perceiver(nc, ins, out):
    ctx = ExitStack()
    with ctx:
        starts = {}

        def place(name, shape, dt, at):
            size = 4
            for n in shape[1:]:
                size *= n
            assert at + size <= SBUF_BYTES, (name, at + size)
            starts[name] = at
            return nc.alloc_sbuf_tensor_at(name, shape, dt, offset=SBUF0 + at)

        def stack(at, *arrays):
            made = []
            for name, shape, dt in arrays:
                made.append(place(name, shape, dt, at))
                size = 4
                for n in shape[1:]:
                    size *= n
                at += -(-size // 32) * 32
            return made, at

        def sem(name):
            return ctx.enter_context(nc.semaphore(name))

        bank = [ctx.enter_context(nc.psum_tensor(f"bank{i}", [P, 512], F32)) for i in range(8)]

        (x, xn, xnT, ident, ones, stats, mv, var_eps, rstd, powm), at_a = stack(
            0,
            ("x", [P, D], F32),
            ("xn", [P, D], F32),
            ("xnT", [P, KC, P], F32),
            ("ident", [P, P], F32),
            ("ones", [P, P], F32),
            ("stats", [P, 6], F32),
            ("mv", [P, 2], F32),
            ("var_eps", [P, 1], F32),
            ("rstd", [P, 1], F32),
            ("powm", [P, 4], F32),
        )
        (ctx_hi, ctx_lo), at_w = stack(
            at_a, ("ctx_hi", [P, TB, KC, 512], F32R), ("ctx_lo", [P, TB, KC, 512], F32R))

        ((kv_raw, kvw, kvw_hi, kvw_lo, wq, wo, kt_hi, kt_lo, v_hi, v_lo, qt_hi, qt_lo, q_sb, scores,
          mask, pt_hi, pt_lo, a_xnT_hi, kj, kssq, kms, krstd, qssq, qms, qrstd, mx, nm, sums, rs, qkw, qkv2),
         end_a) = stack(
            at_w,
            ("kv_raw", [P, TT, 2 * HD], F32),
            ("kvw", [P, KC, 2 * HD], F32),
            ("kvw_hi", [P, KC, 2 * HD], F32R),
            ("kvw_lo", [P, KC, 2 * HD], F32R),
            ("wq", [P, KC, R * HD], F32),
            ("wo", [P, R, D], F32),
            ("kt_hi", [P, T], F32R),
            ("kt_lo", [P, T], F32R),
            ("v_hi", [P, TT, HD], F32R),
            ("v_lo", [P, TT, HD], F32R),
            ("qt_hi", [P, R, P], F32R),
            ("qt_lo", [P, R, P], F32R),
            ("q_sb", [P, R, HD], F32),
            ("scores", [P, R, T], F32),
            ("mask", [P, T], F32),
            ("pt_hi", [P, PR, R * P], F32R),
            ("pt_lo", [P, 2, R * P], F32R),
            ("a_xnT_hi", [P, KC, P], F32R),
            ("kj", [P, 2, HD], F32),
            ("kssq", [P, TT], F32),
            ("kms", [P, TT], F32),
            ("krstd", [P, TT], F32),
            ("qssq", [P, R], F32),
            ("qms", [P, R], F32),
            ("qrstd", [P, R], F32),
            ("mx", [P, R, TB], F32),
            ("nm", [P, R], F32),
            ("sums", [P, R], F32),
            ("rs", [P, R], F32),
            ("qkw", [P, 1], F32),
            ("qkv2", [P, 2], F32),
        )
        ctx_raw = scores[:, :, :].rearrange("p b (c n) -> p b c n", c=KC)
        dg = xn[:, :].rearrange("p (h q) -> p h q", h=R)
        ot = place("ot", [P, R, P], F32, starts["xn"])
        ot_lo = place("ot_lo", [P, R, P], F32R, starts["xn"])
        a_xnT_lo = place("a_xnT_lo", [P, KC, P], F32R, starts["xnT"])
        (a_wo_hi, a_ot_hi, a_wq_hi), _ = stack(
            starts["scores"],
            ("a_wo_hi", [P, R, D], F32R), ("a_ot_hi", [P, R, P], F32R), ("a_wq_hi", [P, KC, R * HD], F32R))
        a_wo_lo = place("a_wo_lo", [P, R, D], F32R, starts["wo"])
        a_wq_lo = place("a_wq_lo", [P, KC, R * HD], F32R, starts["wq"])
        r_sb = q_sb

        (wqkv, bo), at_b = stack(
            at_w,
            ("wqkv", [P, 2, KC, (R + 2) * HD], F32),
            ("bo", [P, 2, R, D], F32))
        (b_q, b_kv, b_qT, b_kT, b_p, b_pT, b_oT, band, b_mx, b_nm, b_sum, b_rs), _ = stack(
            at_b,
            ("b_q", [P, R, HD], F32),
            ("b_kv", [P, 2, 2 * HD], F32),
            ("b_qT", [P, R, P], F32),
            ("b_kT", [P, P], F32),
            ("b_p", [P, R, P], F32),
            ("b_pT", [P, R, P], F32),
            ("b_oT", [P, R, P], F32),
            ("band", [P, P], F32),
            ("b_mx", [P, R], F32),
            ("b_nm", [P, R], F32),
            ("b_sum", [P, R], F32),
            ("b_rs", [P, R], F32))

        (c_q, c_k), at_m = stack(
            at_w + 61 * 1024,
            ("c_q", [P, KC, D], F32),
            ("c_k", [P, KC, D], F32))
        at_small = at_m + 52 * 1024 + 256
        (rw, rb, eb, bq, bk), at_s2 = stack(
            at_small,
            ("rw", [P, KC, E], F32),
            ("rb", [P, E], F32),
            ("eb", [E, D], F32),
            ("bq", [P, D], F32),
            ("bk", [P, D], F32))
        (logits, r_nm, r_sum, r_rs, top8, above, same, rank, room, w_dense, w_sum, w_T, r_gt), _ = stack(
            at_w + 41 * 1024,
            ("logits", [P, E], F32),
            ("r_nm", [P, 1], F32),
            ("r_sum", [P, 1], F32),
            ("r_rs", [P, 1], F32),
            ("top8", [P, 8], F32),
            ("above", [P, E], F32),
            ("same", [P, E], F32),
            ("rank", [P, E], F32),
            ("room", [P, 1], F32),
            ("w_dense", [P, E], F32),
            ("w_sum", [P, 1], F32),
            ("w_T", [E, P], F32),
            ("r_gt", [P, 1], F32))
        (ctx_n,), at_d = stack(at_w, ("ctx_n", [P, TT, D], F32))
        (d_q, d_qT, d_qkT_hi, d_qkT_lo, d_p, d_pT, d_qb, d_mx, d_m, d_nm, d_sum, d_rs, d_bias), end_d = stack(
            at_d,
            ("d_q", [P, D], F32),
            ("d_qT", [P, KC, P], F32),
            ("d_qkT_hi", [P, KC, P], F32R),
            ("d_qkT_lo", [P, KC, P], F32R),
            ("d_p", [P, T], F32),
            ("d_pT", [P, TB, 4, P], F32),
            ("d_qb", [P, 1], F32),
            ("d_mx", [P, TB], F32),
            ("d_m", [P, 1], F32),
            ("d_nm", [P, 1], F32),
            ("d_sum", [P, 1], F32),
            ("d_rs", [P, 1], F32),
            ("d_bias", [P, 1], F32))
        (m_wdt, m_dtb, m_taps, m_cb, m_nw, gw), end_ms = stack(
            end_d,
            ("m_wdt", [P, KC, NG * MH], F32),
            ("m_dtb", [P, NG * MH], F32),
            ("m_taps", [P, NG * NCH * TAPS], F32),
            ("m_cb", [P, NG * NCH], F32),
            ("m_nw", [P, NG, MCC], F32),
            ("gw", [P, KC, NE], F32))
        assert end_ms <= at_w + 61 * 1024
        (m_wx, m_wg, m_wo), end_mw = stack(
            at_m,
            ("m_wx", [P, KC, NCH * P], F32),
            ("m_wg", [P, KC, MC], F32),
            ("m_wo", [P, MCC, D], F32))
        assert end_mw <= at_small
        (m_e, r_hi, r_lo, xc, x_tok, xdt, sg, y, yT, gm, dt, da, da_hi, da_lo, later, upto, z, ea, ue, wd, lnu,
         m_d, m_a, yssq, yms, yrstd), end_mm = stack(
            at_w,
            ("m_e", [P, MH, P], F32),
            ("r_hi", [P, MH, P], F32R),
            ("r_lo", [P, MH, P], F32R),
            ("xc", [P, NCH, P], F32),
            ("x_tok", [P, MH, MP], F32),
            ("xdt", [P, MH, MP], F32),
            ("sg", [P, MC], F32),
            ("y", [P, MC], F32),
            ("yT", [P, MCC, P], F32),
            ("gm", [P, P], F32),
            ("dt", [P, NG * MH], F32),
            ("da", [P, NG * MH], F32),
            ("da_hi", [P, NG * MH], F32R),
            ("da_lo", [P, NG * MH], F32R),
            ("later", [P, P], F32R),
            ("upto", [P, P], F32),
            ("z", [P, NG * MH], F32),
            ("ea", [P, NG * MH], F32),
            ("ue", [P, NG * MH], F32),
            ("wd", [P, NG * MH], F32),
            ("lnu", [P, NG * MH], F32),
            ("m_d", [P, NG * MH], F32),
            ("m_a", [P, NG * MH], F32),
            ("yssq", [P, 1], F32),
            ("yms", [P, 1], F32),
            ("yrstd", [P, 1], F32))
        assert end_mm <= end_d, (end_mm, end_d)
        (ew,), _ = stack(at_a, ("ew", [P, NE, KC, D], F32))
        (wg_hi,), end_wg = stack(at_w + 61 * 1024, ("wg_hi", [P, KC, MC], F32R))
        assert end_wg <= at_m
        (wg_lo,), _ = stack(at_m + 4 * KC * NCH * P, ("wg_lo", [P, KC, MC], F32R))
        (xnT_hi, xnT_lo), at_f = stack(
            at_small, ("xnT_hi", [P, KC, P], F32R), ("xnT_lo", [P, KC, P], F32R))
        (f_l, f_nm, f_top, f_above, f_same, f_rank, f_gt, f_room, f_w, f_sum, f_rs), _ = stack(
            at_f,
            ("f_l", [P, NE], F32),
            ("f_nm", [P, 1], F32),
            ("f_top", [P, 8], F32),
            ("f_above", [P, NE], F32),
            ("f_same", [P, NE], F32),
            ("f_rank", [P, NE], F32),
            ("f_gt", [P, 1], F32),
            ("f_room", [P, 1], F32),
            ("f_w", [P, NE], F32),
            ("f_sum", [P, 1], F32),
            ("f_rs", [P, 1], F32))

        x_in, ctx_in, mask_in, w_in = sem("x_in"), [sem(f"ctx_in{i}") for i in range(TB)], sem("mask_in"), sem("w_in")
        kvw_in, wq_in, wo_in = sem("kvw_in"), sem("wq_in"), sem("wo_in")
        const_ready = sem("const_ready")
        x_ready, ln_stats, ln_mean, ln_var, ln_rstd = (sem(n) for n in ("x_ready", "ln_stats", "ln_mean", "ln_var", "ln_rstd"))
        ln_x, ln_turned, ln_xT = (sem(n) for n in ("ln_x", "ln_turned", "ln_xT"))
        ctx_hi_done, ctx_lo_done, kvw_hi_done, kvw_lo_done = (sem(n) for n in (
            "ctx_hi_done", "ctx_lo_done", "kvw_hi_done", "kvw_lo_done"))
        kv_full, kv_kept, k_squared, k_meaned, k_rstd, k_normed = (sem(n) for n in (
            "kv_full", "kv_kept", "k_squared", "k_meaned", "k_rstd", "k_normed"))
        turned, hi_kept, lo_kept = (sem(n) for n in ("turned", "hi_kept", "lo_kept"))
        q_full, q_squared, q_meaned, q_rstd, q_normed, qt_full, qt_hi_done, qt_lo_done, qkw_done = (sem(n) for n in (
            "q_full", "q_squared", "q_meaned", "q_rstd", "q_normed", "qt_full", "qt_hi_done", "qt_lo_done", "qkw_done"))
        s_full, s_seen, s_masked, max_ready, p_ready = (sem(n) for n in ("s_full", "s_seen", "s_masked", "max_ready", "p_ready"))
        v_hi_done, v_lo_done, pv_done, rs_done, dg_done, inverse_full, r_kept, ot_kept, o_full, o_added = (sem(n) for n in (
            "v_hi_done", "v_lo_done", "pv_done", "rs_done", "dg_done", "inverse_full", "r_kept", "ot_kept", "o_full", "o_added"))
        a_xnT_hi_done, a_xnT_lo_done, a_wq_hi_done, a_wq_lo_done, a_wo_hi_done, a_wo_lo_done, ot_hi_done, ot_lo_done = (
            sem(n) for n in ("a_xnT_hi_done", "a_xnT_lo_done", "a_wq_hi_done", "a_wq_lo_done", "a_wo_hi_done",
                             "a_wo_lo_done", "ot_hi_done", "ot_lo_done"))
        out_done = sem("out_done")
        wqkv_in, bo_in = [sem(f"wqkv_in{i}") for i in range(2)], [sem(f"bo_in{i}") for i in range(2)]
        band_ready, acc_open = sem("band_ready"), sem("acc_open")
        b_qk_turned, b_kv_full, b_q_full, b_s_full, b_s_seen, b_p_turned, b_pv_done, b_o_done = (sem(n) for n in (
            "b_qk_turned", "b_kv_full", "b_q_full", "b_s_full", "b_s_seen", "b_p_turned", "b_pv_done", "b_o_done"))
        b_q_kept, b_kv_kept, b_qT_kept, b_kT_kept, b_masked, b_max, b_exp, b_inverse, b_normed, b_pT_kept, b_oT_kept = (
            sem(n) for n in ("b_q_kept", "b_kv_kept", "b_qT_kept", "b_kT_kept", "b_masked", "b_max", "b_exp",
                             "b_inverse", "b_normed", "b_pT_kept", "b_oT_kept"))
        small_in, r_full, r_step, r_exp, r_mixed, r_turned, r_T_kept = (sem(n) for n in (
            "small_in", "router_full", "r_step", "r_exp", "r_mixed", "r_turned", "r_T_kept"))
        c_in, ctx_n_in, d_full, d_kept, d_s_full, d_s_maxed, d_step, d_exp, d_turned, d_pT_kept, d_done = (
            sem(n) for n in ("c_in", "ctx_n_in", "d_full", "d_kept", "d_s_full", "d_s_maxed", "d_step", "d_exp",
                             "d_turned", "d_pT_kept", "d_done"))

        m_small_in, m_rows_in, m_wx_in, m_wg_in, m_wo_in = (sem(n) for n in (
            "m_small_in", "m_rows_in", "m_wx_in", "m_wg_in", "m_wo_in"))
        m_const, dt_full, dt_step, dt_exp, da_hi_done = (sem(n) for n in (
            "m_const", "dt_full", "dt_step", "dt_exp", "da_hi_done"))
        m_seg, m_in, m_gfull, m_xT, m_gate, m_y, m_yT, m_out = (sem(n) for n in (
            "m_seg_full", "m_in_full", "m_g_full", "m_x_turned", "m_gate_full", "m_y_full", "m_y_turned", "m_out_full"))
        m_exp, m_tap, m_silu, m_xtok, m_sg, m_sq = (sem(n) for n in (
            "m_exp", "m_tap", "m_silu", "m_xtok", "m_sg", "m_squared"))
        m_conv, m_gm, m_m, m_xdt, m_ysum, m_yg, m_yms, m_yn, m_yTk = (sem(n) for n in (
            "m_conv", "m_gm", "m_m", "m_xdt", "m_ysum", "m_yg", "m_yms", "m_yn", "m_yT_kept"))
        m_r, m_xd, m_rstd = (sem(n) for n in ("m_r", "m_xd", "m_rstd"))
        wg_hi_done, wg_lo_done, wg_lo2_done, xnT_hi_done, xnT_lo_done = (sem(n) for n in (
            "wg_hi_done", "wg_lo_done", "wg_lo2_done", "xnT_hi_done", "xnT_lo_done"))
        ew_in, f_full, f_step, f_exp, f_prod, f_used = (sem(n) for n in (
            "ew_in", "f_full", "f_step", "f_exp", "f_prod", "f_used"))

        KV = bank[0:2]
        TR = bank[4:6] + bank[2:4]
        S = TR
        OT = bank[6]
        M = bank[7]
        CREDIT = 2

        block = ctx.enter_context(nc.Block())

        @block.sync
        def _(sp):
            sp.dma_start(x[:, :], ins["x"]).then_inc(x_in, DMA)
            sp.dma_start(kvw[:, :, :], ins["a_kv"][0]).then_inc(kvw_in, DMA)
            for b in range(TB):
                sp.dma_start(ctx_raw[:, b], ins["ctxT"][b]).then_inc(ctx_in[b], DMA)
            sp.dma_start(wq[:, :, :], ins["a_q"][0]).then_inc(wq_in, DMA)
            sp.dma_start(mask[:, :], ins["mask"]).then_inc(mask_in, DMA)
            sp.dma_start(wo[:, :, :], ins["a_o"][0]).then_inc(wo_in, DMA)

            def next_kvw(g):
                sp.wait_ge(kvw_hi_done, g)
                sp.wait_ge(kvw_lo_done, g)
                sp.dma_start(kvw[:, :, :], ins["a_kv"][g]).then_inc(kvw_in, DMA)

            def next_q(g):
                sp.wait_ge(q_full, g)
                sp.dma_start(wq[:, :, :], ins["a_q"][g]).then_inc(wq_in, DMA)

            def next_o(g):
                sp.wait_ge(o_full, g)
                sp.dma_start(wo[:, :, :], ins["a_o"][g]).then_inc(wo_in, DMA)

            next_kvw(1)
            with sp.Fori(0, NG - 2) as g:
                next_q(g + 1)
                next_kvw(g + 2)
                next_o(g + 1)
            next_q(NG - 1)
            next_o(NG - 1)

            sp.wait_ge(turned, 20 * (NG - 1) + 4)
            sp.wait_ge(v_lo_done, 4 * NG)
            sp.wait_ge(q_full, NG)

            def load_qkv(g, slot):
                sp.dma_start(wqkv[:, slot], ins["b_qkv"][g]).then_inc(wqkv_in[slot], DMA)

            def load_o(g, slot):
                sp.dma_start(bo[:, slot], ins["b_o"][g]).then_inc(bo_in[slot], DMA)

            load_qkv(0, 0)
            load_qkv(1, 1)
            load_o(0, 0)
            sp.wait_ge(o_full, NG)
            load_o(1, 1)
            for name, to in (("rw", rw), ("rb", rb), ("eb", eb), ("bq", bq), ("bk", bk)):
                src = ins[name]
                if name in ("rb", "bq", "bk"):
                    src = src.partition_broadcast(P)
                sp.dma_start(to[:], src).then_inc(small_in, DMA)

            def next_qkv(g, slot):
                sp.wait_ge(b_q_full, g - 1)
                load_qkv(g, slot)

            def next_bo(g, slot):
                sp.wait_ge(b_o_done, g - 1)
                load_o(g, slot)

            next_qkv(2, 0)
            with sp.Fori(0, 2) as i:
                next_qkv(2 * i + 3, 1)
                next_bo(2 * i + 2, 0)
                next_qkv(2 * i + 4, 0)
                next_bo(2 * i + 3, 1)
            next_qkv(NG - 1, 1)
            next_bo(NG - 2, 0)
            sp.dma_start(c_q[:, :, :], ins["c_q"]).then_inc(c_in, DMA)
            sp.dma_start(c_k[:, :, :], ins["c_k"]).then_inc(c_in, DMA)
            next_bo(NG - 1, 1)
            sp.wait_ge(b_o_done, NG)
            sp.dma_start(ctx_n[:, :, :], ins["ctx_n"]).then_inc(ctx_n_in, DMA)
            for name, to in (("m_wdt", m_wdt), ("m_dtb", m_dtb), ("m_taps", m_taps), ("m_cb", m_cb), ("m_nw", m_nw),
                             ("gw", gw)):
                src = ins[name]
                if name == "m_dtb":
                    src = src.partition_broadcast(P)
                sp.dma_start(to[:], src).then_inc(m_small_in, DMA)
            sp.dma_start(m_wx[:, :, :], ins["m_wx"][0]).then_inc(m_wx_in, DMA)
            sp.dma_start(m_wg[:, :, :], ins["m_wg"][0]).then_inc(m_wg_in, DMA)
            sp.dma_start(m_wo[:, :, :], ins["m_wo"][0]).then_inc(m_wo_in, DMA)
            sp.wait_ge(x_ready, 5)
            sp.dma_start(m_a[:, :], ins["m_a"].partition_broadcast(P)).then_inc(m_rows_in, DMA)
            sp.dma_start(m_d[:, :], ins["m_d"].partition_broadcast(P)).then_inc(m_rows_in, DMA)

            def next_wx(g):
                sp.wait_ge(m_in, 3 * g)
                sp.dma_start(m_wx[:, :, :], ins["m_wx"][g]).then_inc(m_wx_in, DMA)

            def next_wg(g):
                sp.wait_ge(m_gate, 2 * g)
                sp.dma_start(m_wg[:, :, :], ins["m_wg"][g]).then_inc(m_wg_in, DMA)

            def next_wo(g):
                sp.wait_ge(m_out, g)
                sp.dma_start(m_wo[:, :, :], ins["m_wo"][g]).then_inc(m_wo_in, DMA)

            def expert(e):
                sp.dma_start(ew[:, bass.ds(e, 1), :, :], ins["ew"][e].unsqueeze(1)).then_inc(ew_in, DMA)

            next_wx(1)
            next_wg(1)
            expert(0)
            with sp.Fori(0, NG - 2) as i:
                next_wx(i + 2)
                next_wo(i + 1)
                next_wg(i + 2)
                expert(i + 1)
            expert(NE - 1)
            next_wo(NG - 1)
            sp.wait_ge(x_ready, 7)
            sp.dma_start(out, x[:, :]).then_inc(out_done, DMA)
            sp.wait_ge(out_done, DMA)

        @block.gpsimd
        def _(pool):
            pool.memset(ident[:, :], 0.0).then_inc(const_ready, 1)
            pool.memset(ones[:, :], 1.0).then_inc(const_ready, 1)
            pool.memset(powm[:, :], -0.5).then_inc(const_ready, 1)
            pool.wait_ge(const_ready, 3)
            pool.affine_select(out=ident[:, :], in_=ident[:, :], compare_op=ALU.not_equal, fill=1.0, base=0,
                               pattern=[[-1, P]], channel_multiplier=1).then_inc(const_ready, 1)
            pool.dma_start(qkv2[:, :], ins["a_norm"]).then_inc(w_in, DMA)

            def rsqrt_row(k):
                pool.wait_ge(ln_var, k + 1)
                pool.tensor_tensor(rstd[:, :], var_eps[:, :], powm[:, 0:1], ALU.pow).then_inc(ln_rstd, 1)

            def k_rsqrt(g, j):
                pool.wait_ge(k_meaned, 4 * g + j + 1)
                pool.tensor_tensor(krstd[:, 4 * j:4 * j + 4], kms[:, 4 * j:4 * j + 4], powm[:, :], ALU.pow)\
                    .then_inc(k_rstd, 1)

            def v_low(g, j):
                pool.wait_ge(v_hi_done, 4 * g + j + 1)
                pool.tensor_tensor(v_lo[:, 4 * j:4 * j + 4, :], kv_raw[:, 4 * j:4 * j + 4, HD:],
                                   v_hi[:, 4 * j:4 * j + 4, :].bitcast(F32), ALU.subtract).then_inc(v_lo_done, 1)

            def wq_low(g):
                for c in range(KC):
                    pool.wait_ge(a_wq_hi_done, KC * g + c + 1)
                    pool.tensor_tensor(a_wq_lo[:, c, :], wq[:, c, :], a_wq_hi[:, c, :].bitcast(F32), ALU.subtract)\
                        .then_inc(a_wq_lo_done, 1)

            rsqrt_row(0)
            wq_low(0)
            for j in range(TB):
                k_rsqrt(0, j)

            def group(g, more):
                v_low(g, 0)
                pool.wait_ge(q_meaned, g + 1)
                pool.tensor_tensor(qrstd[:, :], qms[:, :], powm[:, :], ALU.pow).then_inc(q_rstd, 1)
                for j in range(1, TB):
                    v_low(g, j)
                if more:
                    for j in range(TB - 1):
                        k_rsqrt(g + 1, j)
                    wq_low(g + 1)
                    k_rsqrt(g + 1, TB - 1)

            with pool.Fori(0, NG - 1) as g:
                group(g, True)
            group(NG - 1, False)

            pool.wait_ge(x_ready, 2)
            pool.memset(band[:, :], 0.0).then_inc(band_ready, 1)
            pool.wait_ge(band_ready, 1)
            pool.affine_select(out=band[:, :], in_=band[:, :], compare_op=ALU.is_ge, fill=-1.0e30, base=0,
                               pattern=[[-1, P]], channel_multiplier=1).then_inc(band_ready, 1)
            pool.wait_ge(band_ready, 2)
            pool.affine_select(out=band[:, :], in_=band[:, :], compare_op=ALU.is_ge, fill=-1.0e30, base=SLIDE - 1,
                               pattern=[[1, P]], channel_multiplier=-1).then_inc(band_ready, 1)
            for k in range(1, 4):
                rsqrt_row(k)

            def gate_low(g, cs):
                for c in cs:
                    pool.wait_ge(wg_hi_done, KC * g + c + 1)
                    pool.tensor_tensor(wg_lo[:, c, :], m_wg[:, c, :], wg_hi[:, c, :].bitcast(F32), ALU.subtract)\
                        .then_inc(wg_lo_done, 1)

            gate_low(0, range(KC))
            rsqrt_row(4)
            pool.memset(upto[:, :], 1.0).then_inc(m_const, 1)
            pool.memset(gm[:, :], 1.0).then_inc(m_const, 1)
            pool.wait_ge(m_const, 2)
            pool.affine_select(out=upto[:, :], in_=upto[:, :], compare_op=ALU.is_ge, fill=0.0, base=0,
                               pattern=[[1, P]], channel_multiplier=-1).then_inc(m_const, 1)
            pool.affine_select(out=gm[:, :], in_=gm[:, :], compare_op=ALU.is_gt, fill=0.0, base=0,
                               pattern=[[-1, P]], channel_multiplier=1).then_inc(m_const, 1)
            pool.wait_ge(m_const, 4)

            def decay_rows(g):
                for q in range(4):
                    for part, to in ((da_hi, r_hi), (da_lo, r_lo)):
                        pool.tensor_tensor(
                            to[:, 4 * q:4 * q + 4, :],
                            part[:, bass.ds(MH * g + 4 * q, 4)].bitcast(F32).unsqueeze(2).broadcast_to([P, 4, P]),
                            upto[:, :].unsqueeze(1).broadcast_to([P, 4, P]), ALU.mult).then_inc(m_r, 1)

            def y_rstd(g):
                pool.wait_ge(m_yms, g + 1)
                pool.tensor_tensor(yrstd[:, :], yms[:, :], powm[:, 0:1], ALU.pow).then_inc(m_rstd, 1)

            def skip(g, first):
                if not first:
                    pool.wait_ge(m_yT, 2 * g)
                pool.wait_ge(m_xtok, 2 * g + 2)
                pool.tensor_tensor(y[:, :].rearrange("p (h n) -> p h n", h=MH), x_tok[:, :, :],
                                   m_d[:, bass.ds(MH * g, MH)].unsqueeze(2).broadcast_to([P, MH, MP]), ALU.mult)\
                    .then_inc(m_xd, 1)

            pool.wait_ge(dt_step, DT_STEPS)
            decay_rows(0)
            pool.wait_ge(m_seg, 4)
            decay_rows(1)
            pool.wait_ge(m_rows_in, 2 * DMA)
            skip(0, True)
            with pool.Fori(0, NG - 2) as i:
                y_rstd(i)
                gate_low(i + 1, (0, 1))
                pool.wait_ge(m_seg, 4 * i + 8)
                decay_rows(i + 2)
                skip(i + 1, False)
            y_rstd(NG - 2)
            gate_low(NG - 1, (0, 1))
            skip(NG - 1, False)
            y_rstd(NG - 1)
            rsqrt_row(5)

        @block.scalar
        def _(act):
            def kvw_high(g):
                act.wait_ge(kvw_in, DMA * (g + 1))
                act.activation(kvw_hi[:, :, :], kvw[:, :, :], ACT.Copy).then_inc(kvw_hi_done, 1)

            def k_square(g, t):
                act.wait_ge(kv_kept, CREDIT + 8 * g + t // 2 + 1)
                act.wait_ge(k_squared, 16 * g + t + 1)
                act.activation(kj[:, t % 2, :], kv_raw[:, t, 0:HD], ACT.Square, accum_out=kssq[:, t:t + 1])\
                    .then_inc(k_squared, 1)

            def high(g, n, out, in_):
                act.wait_ge(turned, 20 * g + n + 1)
                act.activation(out, in_, ACT.Copy).then_inc(hi_kept, 1)

            def wq_high(g):
                act.wait_ge(wq_in, DMA * (g + 1))
                for c in range(KC):
                    act.activation(a_wq_hi[:, c, :], wq[:, c, :], ACT.Copy).then_inc(a_wq_hi_done, 1)

            act.sem_inc(k_squared, CREDIT)
            kvw_high(0)
            for b in range(TB):
                act.wait_ge(ctx_in[b], DMA)
                act.activation(ctx_hi[:, b], ctx_raw[:, b], ACT.Copy).then_inc(ctx_hi_done, 1)
            act.wait_ge(ln_xT, 1)
            act.activation(a_xnT_hi[:, :, :], xnT[:, :, :], ACT.Copy).then_inc(a_xnT_hi_done, 1)
            act.wait_ge(ctx_lo_done, TB)
            wq_high(0)
            for t in range(TT):
                k_square(0, t)

            def group(g, more):
                def v_high(j):
                    act.activation(v_hi[:, 4 * j:4 * j + 4, :], kv_raw[:, 4 * j:4 * j + 4, HD:], ACT.Copy)\
                        .then_inc(v_hi_done, 1)

                for b in range(2):
                    high(g, b, kt_hi[:, 512 * b:512 * b + 512], TR[b][:, :])
                act.wait_ge(pv_done, 1 + 16 * g)
                v_high(0)
                if more:
                    act.wait_ge(kv_full, 8 * g + 8)
                    kvw_high(g + 1)
                act.wait_ge(q_full, g + 1)
                for h in range(R):
                    act.activation(xn[:, h * HD:h * HD + HD], M[:, h * HD:h * HD + HD], ACT.Square,
                                   accum_out=qssq[:, h:h + 1]).then_inc(q_squared, 1)
                for b in range(2, 4):
                    high(g, b, kt_hi[:, 512 * b:512 * b + 512], TR[b][:, :])
                for j in range(1, TB):
                    v_high(j)
                act.wait_ge(qt_full, g + 1)
                act.activation(qt_hi[:, :, :], M[:, :].rearrange("p (h q) -> p h q", h=R), ACT.Copy,
                               scale=qkw[:, 0:1]).then_inc(qt_hi_done, 1)
                for h in range(R):
                    if more and h < 3:
                        k_square(g + 1, 2 * h)
                        k_square(g + 1, 2 * h + 1)
                    act.wait_ge(max_ready, 4 * g + h + 1)
                    act.activation(scores[:, h, :], scores[:, h, :], ACT.Exp, bias=nm[:, h:h + 1],
                                   accum_out=sums[:, h:h + 1]).then_inc(p_ready, 1)
                if more:
                    k_square(g + 1, 6)
                    k_square(g + 1, 7)
                for c in range(TT):
                    act.wait_ge(pv_done, 1 + 16 * g + max(c - PR + 1, 0))
                    high(g, 4 + c, pt_hi[:, c % PR, :], TR[c % 4][:, :])
                    if more and c in (6, 12):
                        t = 8 if c == 6 else 10
                        k_square(g + 1, t)
                        k_square(g + 1, t + 1)
                    if c == 8:
                        act.wait_ge(inverse_full, g + 1)
                        act.activation(r_sb[:, :, :], M[:, :].rearrange("p (h q) -> p h q", h=R), ACT.Copy)\
                            .then_inc(r_kept, 1)
                if more:
                    act.wait_ge(wo_in, DMA * (g + 1))
                    for h in range(R):
                        act.activation(a_wo_hi[:, h, :], wo[:, h, :], ACT.Copy).then_inc(a_wo_hi_done, 1)
                    act.wait_ge(ot_kept, g + 2)
                    act.activation(a_ot_hi[:, :, :], ot[:, :, :], ACT.Copy).then_inc(ot_hi_done, 1)
                    wq_high(g + 1)
                    for t in range(12, 16):
                        k_square(g + 1, t)

            with act.Fori(0, NG - 1) as g:
                group(g, True)
            group(NG - 1, False)

            def keep_projections(g, slot):
                act.wait_ge(b_kv_full, g + 1)
                act.activation(b_kv[:, slot, :], bank[1][:, 0:2 * HD], ACT.Copy).then_inc(b_kv_kept, 1)
                act.wait_ge(b_q_full, g + 1)
                act.activation(b_q[:, :, :], bank[0][:, :].rearrange("p (h q) -> p h q", h=R), ACT.Copy)\
                    .then_inc(b_q_kept, 1)

            def attend(g, slot, more):
                act.wait_ge(b_qk_turned, g + 1)
                act.activation(b_kT[:, :], bank[3][:, 0:P], ACT.Copy).then_inc(b_kT_kept, 1)
                for h in range(R):
                    if h == 0:
                        act.wait_ge(b_max, g + 1)
                    act.activation(b_p[:, h, :], b_p[:, h, :], ACT.Exp, bias=b_nm[:, h:h + 1],
                                   accum_out=b_sum[:, h:h + 1]).then_inc(b_exp, 1)
                if more:
                    keep_projections(g + 1, 1 - slot)
                act.wait_ge(b_p_turned, g + 1)
                act.activation(b_pT[:, :, :], bank[5][:, :].rearrange("p (h q) -> p h q", h=R), ACT.Copy)\
                    .then_inc(b_pT_kept, 1)

            keep_projections(0, 0)
            attend(0, 0, True)
            with act.Fori(0, NG // 2 - 1) as i:
                attend(2 * i + 1, 1, True)
                attend(2 * i + 2, 0, True)
            attend(NG - 1, 1, False)

            act.wait_ge(r_step, 2)
            act.activation(logits[:, :], logits[:, :], ACT.Exp, bias=r_nm[:, 0:1], accum_out=r_sum[:, 0:1])\
                .then_inc(r_exp, 1)
            act.wait_ge(r_turned, 1)
            act.activation(w_T[:, :], bank[5][0:E, 0:P], ACT.Copy).then_inc(r_T_kept, 1)

            act.wait_ge(d_full, 2)
            act.activation(d_qT[:, :, :], bank[5][:, :].rearrange("p (c t) -> p c t", c=KC), ACT.Copy)\
                .then_inc(d_kept, 1)
            act.wait_ge(d_full, 3)
            act.wait_ge(d_step, 2)
            act.activation(d_q[:, :], bank[0][:, :], ACT.Copy).then_inc(d_kept, 1)
            act.wait_ge(d_full, 4)
            act.activation(d_qkT_hi[:, :, :], bank[5][:, :].rearrange("p (c t) -> p c t", c=KC), ACT.Copy)\
                .then_inc(d_kept, 1)
            act.wait_ge(d_step, 7)
            for b in range(TB):
                act.activation(d_p[:, 512 * b:512 * b + 512], bank[b][:, :], ACT.Exp, bias=d_bias[:, 0:1],
                               scale=D ** -0.5, accum_out=d_mx[:, b:b + 1]).then_inc(d_exp, 1)
            for b in range(TB):
                act.wait_ge(d_turned, b + 1)
                act.activation(d_pT[:, b], bank[4 + b % 2][:, :].rearrange("p (i t) -> p i t", i=4), ACT.Copy)\
                    .then_inc(d_pT_kept, 1)

            def gate_high(g, cs):
                act.wait_ge(m_wg_in, DMA * (g + 1))
                for c in cs:
                    act.activation(wg_hi[:, c, :], m_wg[:, c, :], ACT.Copy).then_inc(wg_hi_done, 1)

            gate_high(0, range(KC))
            act.wait_ge(ln_xT, 5)
            act.activation(xnT_hi[:, :, :], xnT[:, :, :], ACT.Copy).then_inc(xnT_hi_done, 1)
            act.wait_ge(m_const, 4)
            act.activation(later[:, :], gm[:, :], ACT.Copy).then_inc(m_const, 1)
            act.wait_ge(dt_step, 2)
            act.activation(ea[:, :], ea[:, :], ACT.Exp, scale=-1.0).then_inc(dt_exp, 1)
            act.wait_ge(dt_step, 3)
            act.activation(lnu[:, :], ue[:, :], ACT.Ln).then_inc(dt_exp, 1)
            act.wait_ge(dt_step, DT_STEPS - 1)
            act.activation(da_hi[:, :], da[:, :], ACT.Copy).then_inc(da_hi_done, 1)

            def m_group(g, first):
                def decays(q):
                    act.wait_ge(m_seg, 4 * g + q + 1)
                    act.activation(m_e[:, 4 * q:4 * q + 4, :],
                                   bank[5 + q % 2][:, :].rearrange("p (h n) -> p h n", h=4), ACT.Exp)\
                        .then_inc(m_exp, 1)

                def taps(part, js):
                    act.wait_ge(m_in, 3 * g + part + 1)
                    for j in js:
                        b, r = (0, j) if j < 2 else (1 + (j - 2) // 4, (j - 2) % 4)
                        act.activation(xc[:, j, :], bank[b][:, P * r:P * r + P], ACT.Identity,
                                       bias=m_cb[:, bass.ds(NCH * g + j, 1)],
                                       scale=m_taps[:, bass.ds(TAPS * (NCH * g + j) + TAPS - 1, 1)])\
                            .then_inc(m_tap, 1)

                def silu(lo, hi, step):
                    act.wait_ge(m_conv, STEPS * g + step)
                    act.activation(xc[:, lo:hi, :], xc[:, lo:hi, :], ACT.Silu).then_inc(m_silu, 1)

                def keep_channels():
                    for i in range(2):
                        act.wait_ge(m_xT, 2 * g + i + 1)
                        if not first and i == 0:
                            act.wait_ge(m_xd, g)
                        act.activation(x_tok[:, 8 * i:8 * i + 8, :],
                                       bank[5 + i][:, :].rearrange("p (h n) -> p h n", n=MP), ACT.Copy)\
                            .then_inc(m_xtok, 1)

                def gates():
                    for i in range(2):
                        act.wait_ge(m_gate, 2 * g + i + 1)
                        if not first:
                            act.wait_ge(m_sq, g)
                        act.activation(sg[:, 512 * i:512 * i + 512], bank[3 + i][:, :], ACT.Silu).then_inc(m_sg, 1)

                if not first:
                    act.wait_ge(m_y, g)
                    decays(0)
                    decays(1)
                    square(g - 1)
                taps(0, range(2))
                if not first:
                    decays(2)
                    decays(3)
                    gate_high(g, (0, 1))
                taps(1, range(2, 6))
                silu(0, 2, 6)
                if not first:
                    gate_high(g, (2, 3))
                taps(2, range(6, 10))
                silu(2, 6, 18)
                silu(6, 10, 30)
                if first:
                    gates()
                    keep_channels()
                    for q in range(4):
                        decays(q)
                else:
                    keep_channels()
                    gates()

            def square(g):
                act.wait_ge(m_yg, 2 * g + 2)
                act.activation(sg[:, :], y[:, :], ACT.Square, accum_out=yssq[:, 0:1]).then_inc(m_sq, 1)

            m_group(0, True)
            with act.Fori(0, NG - 1) as i:
                m_group(i + 1, False)
            square(NG - 1)
            act.wait_ge(f_step, 5)
            act.activation(f_l[:, :], f_l[:, :], ACT.Exp, bias=f_nm[:, 0:1]).then_inc(f_exp, 1)

        @block.vector
        def _(dve):
            def layer_norm(k):
                dve.wait_ge(x_ready, k + 1)
                dve.bn_stats(stats[:, :], x[:, :]).then_inc(ln_stats, 1)
                dve.wait_ge(ln_stats, k + 1)
                dve.bn_aggr(mv[:, :], stats[:, :]).then_inc(ln_mean, 1)
                dve.wait_ge(ln_mean, k + 1)
                dve.tensor_scalar(var_eps[:, :], mv[:, 1:2], 1.0, EPS, ALU.mult, ALU.add).then_inc(ln_var, 1)
                dve.wait_ge(ln_rstd, k + 1)
                dve.tensor_scalar(xn[:, :], x[:, :], mv[:, 0:1], rstd[:, 0:1], ALU.subtract, ALU.mult)\
                    .then_inc(ln_x, 1)
                dve.wait_ge(ln_turned, k + 1)
                dve.tensor_copy(xnT[:, :, :], TR[0][:, :].rearrange("p (c t) -> p c t", c=KC)).then_inc(ln_xT, 1)

            def keep_kv(g, u):
                dve.wait_ge(kv_full, 8 * g + u + 1)
                dve.tensor_copy(kv_raw[:, 2 * u:2 * u + 2, :], KV[u % 2][:, :].rearrange("p (t n) -> p t n", t=2))\
                    .then_inc(kv_kept, 1)

            def replace_kv(g, u):
                j = u // 2
                dve.wait_ge(turned, 20 * (g - 1) + j + 1)
                dve.wait_ge(v_lo_done, 4 * (g - 1) + j + 1)
                keep_kv(g, u)

            def k_mean(g, j):
                dve.wait_ge(k_squared, CREDIT + 16 * g + 4 * j + 4)
                dve.tensor_scalar(kms[:, 4 * j:4 * j + 4], kssq[:, 4 * j:4 * j + 4], 1.0 / HD, EPS,
                                  ALU.mult, ALU.add).then_inc(k_meaned, 1)

            def k_norm(g, j):
                dve.wait_ge(k_rstd, 4 * g + j + 1)
                k = kv_raw[:, 4 * j:4 * j + 4, 0:HD]
                dve.tensor_tensor(k, k, krstd[:, 4 * j:4 * j + 4].unsqueeze(2).broadcast_to([P, 4, HD]),
                                  ALU.mult).then_inc(k_normed, 1)

            def kvw_low(g):
                dve.wait_ge(kvw_hi_done, g + 1)
                dve.tensor_tensor(kvw_lo[:, :, :], kvw[:, :, :], kvw_hi[:, :, :].bitcast(F32), ALU.subtract)\
                    .then_inc(kvw_lo_done, 1)

            def low(g, n, out, in_, hi):
                dve.wait_ge(hi_kept, 20 * g + n + 1)
                dve.tensor_tensor(out, in_, hi.bitcast(F32), ALU.subtract).then_inc(lo_kept, 1)

            dve.sem_inc(ot_kept, 1)
            dve.sem_inc(o_added, 1)
            dve.sem_inc(kv_kept, CREDIT)
            dve.sem_inc(lo_kept, len(TR))
            dve.sem_inc(s_masked, len(S))
            dve.wait_ge(x_in, DMA)
            dve.sem_inc(x_ready, 1)
            kvw_low(0)
            layer_norm(0)
            dve.wait_ge(w_in, DMA)
            dve.scalar_tensor_tensor(out=qkw[:, :], in0=qkv2[:, 0:1], scalar=SCALE, in1=qkv2[:, 1:2],
                                     op0=ALU.mult, op1=ALU.mult).then_inc(qkw_done, 1)
            for b in range(TB):
                dve.wait_ge(ctx_hi_done, b + 1)
                dve.tensor_tensor(ctx_lo[:, b], ctx_raw[:, b], ctx_hi[:, b].bitcast(F32), ALU.subtract)\
                    .then_inc(ctx_lo_done, 1)
            dve.wait_ge(a_xnT_hi_done, 1)
            dve.tensor_tensor(a_xnT_lo[:, :, :], xnT[:, :, :], a_xnT_hi[:, :, :].bitcast(F32), ALU.subtract)\
                .then_inc(a_xnT_lo_done, 1)
            for u in range(TT // 2):
                keep_kv(0, u)
                if u % 2 == 0 and u > 0:
                    k_mean(0, u // 2 - 1)
                if u % 2 == 1 and u > 1:
                    k_norm(0, u // 2 - 1)
            k_mean(0, 3)
            k_norm(0, 3)

            def group(g, more):
                def kt_low(b):
                    low(g, b, kt_lo[:, 512 * b:512 * b + 512], TR[b][:, :], kt_hi[:, 512 * b:512 * b + 512])

                kt_low(0)
                kt_low(1)
                if more:
                    kvw_low(g + 1)
                dve.wait_ge(q_squared, 4 * g + 4)
                dve.tensor_scalar(qms[:, :], qssq[:, :], 1.0 / HD, EPS, ALU.mult, ALU.add).then_inc(q_meaned, 1)
                kt_low(2)
                kt_low(3)
                dve.wait_ge(q_rstd, g + 1)
                dve.tensor_tensor(q_sb[:, :, :], M[:, :].rearrange("p (h q) -> p h q", h=R),
                                  qrstd[:, :].unsqueeze(2).broadcast_to([P, R, HD]), ALU.mult).then_inc(q_normed, 1)
                if more:
                    replace_kv(g + 1, 0)
                dve.wait_ge(qt_hi_done, g + 1)
                dve.scalar_tensor_tensor(out=qt_lo[:, :, :].rearrange("p h q -> p (h q)"), in0=M[:, :],
                                         scalar=qkw[:, 0:1],
                                         in1=qt_hi[:, :, :].bitcast(F32).rearrange("p h q -> p (h q)"),
                                         op0=ALU.mult, op1=ALU.subtract).then_inc(qt_lo_done, 1)
                for h in range(R):
                    for b in range(TB):
                        dve.wait_ge(s_full, 16 * g + 4 * h + b + 1)
                        dve.sem_inc(s_seen, 1)
                        dve.tensor_tensor_reduce(
                            out=scores[:, h, 512 * b:512 * b + 512], in0=S[b][:, :],
                            in1=mask[:, 512 * b:512 * b + 512], scale=1.0, scalar=NEG, op0=ALU.add, op1=ALU.max,
                            accum_out=mx[:, h, b:b + 1]).then_inc(s_masked, 1)
                    dve.wait_ge(s_masked, len(S) + 16 * g + 4 * h + 4)
                    dve.tensor_reduce(nm[:, h:h + 1], mx[:, h, :], AX.X, ALU.max, negate=True).then_inc(max_ready, 1)
                    if more:
                        if h == 0:
                            replace_kv(g + 1, 1)
                        if h == 1:
                            k_mean(g + 1, 0)
                            replace_kv(g + 1, 2)
                        if h == 2:
                            k_norm(g + 1, 0)
                        if h == 3:
                            replace_kv(g + 1, 3)
                for c in range(TT):
                    dve.wait_ge(pv_done, 1 + 16 * g + max(c - 1, 0))
                    low(g, 4 + c, pt_lo[:, c % 2, :], TR[c % 4][:, :], pt_hi[:, c % PR, :])
                    if more:
                        if c == 1:
                            k_mean(g + 1, 1)
                        if c == 3:
                            k_norm(g + 1, 1)
                        if c == 4:
                            replace_kv(g + 1, 4)
                        if c == 10:
                            replace_kv(g + 1, 5)
                        if c == 14:
                            k_mean(g + 1, 2)
                    if c == 2:
                        dve.wait_ge(p_ready, 4 * g + 4)
                        dve.reciprocal(rs[:, :], sums[:, :]).then_inc(rs_done, 1)
                        dve.wait_ge(rs_done, g + 1)
                        dve.tensor_tensor(dg[:, :, :], ident[:, :].unsqueeze(1).broadcast_to([P, R, P]),
                                          rs[:, :].unsqueeze(2).broadcast_to([P, R, P]), ALU.mult)\
                            .then_inc(dg_done, 1)
                dve.wait_ge(pv_done, 1 + 16 * g + 16)
                dve.wait_ge(r_kept, g + 1)
                dve.tensor_tensor(ot[:, :, :], OT[:, :].rearrange("p (h q) -> p h q", h=R), r_sb[:, :, :], ALU.mult)\
                    .then_inc(ot_kept, 1)
                if more:
                    for h in range(R):
                        dve.wait_ge(a_wo_hi_done, 4 * g + h + 1)
                        dve.tensor_tensor(a_wo_lo[:, h, :], wo[:, h, :], a_wo_hi[:, h, :].bitcast(F32), ALU.subtract)\
                            .then_inc(a_wo_lo_done, 1)
                    dve.wait_ge(ot_hi_done, g + 1)
                    dve.tensor_tensor(ot_lo[:, :, :], ot[:, :, :], a_ot_hi[:, :, :].bitcast(F32), ALU.subtract)\
                        .then_inc(ot_lo_done, 1)
                    replace_kv(g + 1, 6)
                    k_norm(g + 1, 2)
                    replace_kv(g + 1, 7)
                    k_mean(g + 1, 3)
                dve.wait_ge(o_full, g + 1)
                dve.tensor_tensor(x[:, :], x[:, :], M[:, :], ALU.add).then_inc(o_added, 1)
                if more:
                    k_norm(g + 1, 3)

            with dve.Fori(0, NG - 1) as g:
                group(g, True)
            group(NG - 1, False)
            dve.wait_ge(o_added, NG + 1)
            dve.sem_inc(x_ready, 1)

            layer_norm(1)

            def attend(g, slot, more):
                dve.wait_ge(b_qk_turned, g + 1)
                dve.tensor_scalar(b_qT[:, :, :], bank[2][:, :].rearrange("p (h q) -> p h q", h=R), SCALE, None,
                                  ALU.mult).then_inc(b_qT_kept, 1)
                dve.wait_ge(b_s_full, g + 1)
                dve.sem_inc(b_s_seen, 1)
                for h in range(R):
                    dve.tensor_tensor_reduce(
                        out=b_p[:, h, :], in0=bank[4][:, P * h:P * h + P], in1=band[:, :], scale=1.0, scalar=NEG,
                        op0=ALU.add, op1=ALU.max, accum_out=b_mx[:, h:h + 1]).then_inc(b_masked, 1)
                dve.wait_ge(b_masked, 4 * g + 4)
                dve.tensor_scalar(b_nm[:, :], b_mx[:, :], -1.0, None, ALU.mult).then_inc(b_max, 1)
                dve.wait_ge(b_exp, 4 * g + 4)
                dve.reciprocal(b_rs[:, :], b_sum[:, :]).then_inc(b_inverse, 1)
                dve.wait_ge(b_inverse, g + 1)
                dve.tensor_tensor(b_p[:, :, :], b_p[:, :, :], b_rs[:, :].unsqueeze(2).broadcast_to([P, R, P]),
                                  ALU.mult).then_inc(b_normed, 1)
                dve.wait_ge(b_pv_done, g + 1)
                dve.tensor_copy(b_oT[:, :, :], bank[6][:, :].rearrange("p (h q) -> p h q", h=R))\
                    .then_inc(b_oT_kept, 1)

            dve.wait_ge(band_ready, 3)
            attend(0, 0, True)
            with dve.Fori(0, NG // 2 - 1) as i:
                attend(2 * i + 1, 1, True)
                attend(2 * i + 2, 0, True)
            attend(NG - 1, 1, False)
            dve.wait_ge(b_o_done, NG)
            dve.tensor_copy(x[:, :], bank[7][:, :]).then_inc(x_ready, 1)

            layer_norm(2)
            dve.wait_ge(small_in, 5 * DMA)
            dve.wait_ge(r_full, 1)
            dve.tensor_tensor(logits[:, :], bank[0][:, 0:E], rb[:, :], ALU.add).then_inc(r_step, 1)
            dve.wait_ge(r_step, 1)
            dve.tensor_reduce(r_nm[:, :], logits[:, :], AX.X, ALU.max, negate=True).then_inc(r_step, 1)
            dve.wait_ge(r_exp, 1)
            dve.reciprocal(r_rs[:, :], r_sum[:, :]).then_inc(r_step, 1)
            dve.wait_ge(r_step, 3)
            dve.tensor_scalar(logits[:, :], logits[:, :], r_rs[:, 0:1], None, ALU.mult).then_inc(r_step, 1)
            dve.wait_ge(r_step, 4)
            dve.max(out=top8[:, :], in_=logits[:, :]).then_inc(r_step, 1)
            dve.wait_ge(r_step, 5)
            dve.tensor_scalar(above[:, :], logits[:, :], top8[:, TOP - 1:TOP], 0.0, ALU.is_gt, ALU.add,
                              accum_out=r_gt[:, 0:1]).then_inc(r_step, 1)
            dve.tensor_scalar(same[:, :], logits[:, :], top8[:, TOP - 1:TOP], None, ALU.is_equal).then_inc(r_step, 1)
            dve.wait_ge(r_step, 7)
            dve.tensor_tensor_scan(rank[:, :], ones[:, 0:E], same[:, :], 0.0, ALU.mult, ALU.add).then_inc(r_step, 1)
            dve.tensor_scalar(room[:, :], r_gt[:, :], -1.0, float(TOP), ALU.mult, ALU.add).then_inc(r_step, 1)
            dve.wait_ge(r_step, 9)
            dve.scalar_tensor_tensor(out=same[:, :], in0=rank[:, :], scalar=room[:, 0:1], in1=same[:, :],
                                     op0=ALU.is_le, op1=ALU.mult).then_inc(r_step, 1)
            dve.wait_ge(r_step, 10)
            dve.tensor_tensor(above[:, :], above[:, :], same[:, :], ALU.add).then_inc(r_step, 1)
            dve.wait_ge(r_step, 11)
            dve.tensor_tensor_reduce(out=w_dense[:, :], in0=logits[:, :], in1=above[:, :], scale=1.0, scalar=0.0,
                                     op0=ALU.mult, op1=ALU.add, accum_out=w_sum[:, 0:1]).then_inc(r_step, 1)
            dve.wait_ge(r_step, 12)
            dve.scalar_tensor_tensor(out=x[:, :], in0=xn[:, :], scalar=w_sum[:, 0:1], in1=x[:, :],
                                     op0=ALU.mult, op1=ALU.add).then_inc(r_step, 1)
            dve.wait_ge(r_step, 13)
            dve.wait_ge(r_mixed, 1)
            dve.tensor_tensor(x[:, :], x[:, :], bank[1][:, :], ALU.add).then_inc(x_ready, 1)

            layer_norm(3)
            dve.wait_ge(d_full, 1)
            dve.tensor_tensor(d_q[:, :], bank[0][:, :], bq[:, :], ALU.add).then_inc(d_step, 1)
            dve.wait_ge(d_step, 1)
            dve.tensor_tensor_reduce(out=xn[:, :], in0=d_q[:, :], in1=bk[:, :], scale=1.0, scalar=0.0, op0=ALU.mult,
                                     op1=ALU.add, accum_out=d_qb[:, 0:1]).then_inc(d_step, 1)
            dve.wait_ge(d_kept, 3)
            dve.tensor_tensor(d_qkT_lo[:, :, :], bank[5][:, :].rearrange("p (c t) -> p c t", c=KC),
                              d_qkT_hi[:, :, :].bitcast(F32), ALU.subtract).then_inc(d_step, 1)
            for b in range(TB):
                dve.wait_ge(d_s_full, b + 1)
                dve.tensor_reduce(d_mx[:, b:b + 1], bank[b][:, :], AX.X, ALU.max).then_inc(d_s_maxed, 1)
            dve.wait_ge(d_s_maxed, TB)
            dve.tensor_reduce(d_m[:, :], d_mx[:, :], AX.X, ALU.max).then_inc(d_step, 1)
            dve.wait_ge(d_step, 4)
            dve.tensor_scalar(d_nm[:, :], d_m[:, :], d_qb[:, 0:1], None, ALU.add).then_inc(d_step, 1)
            dve.wait_ge(d_step, 5)
            dve.tensor_scalar(d_bias[:, :], d_nm[:, :], -1.0, d_qb[:, 0:1], ALU.mult, ALU.add).then_inc(d_step, 1)
            dve.wait_ge(d_step, 6)
            dve.tensor_scalar(d_bias[:, :], d_bias[:, :], D ** -0.5, None, ALU.mult).then_inc(d_step, 1)
            dve.wait_ge(d_exp, TB)
            dve.tensor_reduce(d_sum[:, :], d_mx[:, :], AX.X, ALU.add).then_inc(d_step, 1)
            dve.wait_ge(d_step, 8)
            dve.reciprocal(d_rs[:, :], d_sum[:, :]).then_inc(d_step, 1)
            dve.wait_ge(d_step, 9)
            dve.wait_ge(d_done, 1)
            dve.scalar_tensor_tensor(out=x[:, :], in0=bank[6][:, :], scalar=d_rs[:, 0:1], in1=x[:, :],
                                     op0=ALU.mult, op1=ALU.add).then_inc(x_ready, 1)
            layer_norm(4)
            dve.wait_ge(xnT_hi_done, 1)
            dve.tensor_tensor(xnT_lo[:, :, :], xnT[:, :, :], xnT_hi[:, :, :].bitcast(F32), ALU.subtract)\
                .then_inc(xnT_lo_done, 1)
            dve.wait_ge(m_small_in, 6 * DMA)
            dve.wait_ge(dt_full, 1)
            dve.tensor_tensor(z[:, :], bank[6][:, 0:NG * MH], m_dtb[:, :], ALU.add).then_inc(dt_step, 1)
            dve.wait_ge(dt_step, 1)
            dve.scalar_tensor_tensor(out=ea[:, :], in0=z[:, :], scalar=-1.0, in1=z[:, :], op0=ALU.mult,
                                     op1=ALU.max).then_inc(dt_step, 1)
            dve.wait_ge(dt_exp, 1)
            dve.tensor_scalar(ue[:, :], ea[:, :], 1.0, None, ALU.add).then_inc(dt_step, 1)
            dve.wait_ge(dt_step, 3)
            dve.tensor_scalar(wd[:, :], ue[:, :], -1.0, 1e-30, ALU.add, ALU.max).then_inc(dt_step, 1)
            dve.wait_ge(dt_step, 4)
            dve.reciprocal(wd[:, :], wd[:, :]).then_inc(dt_step, 1)
            dve.wait_ge(dt_exp, 2)
            dve.tensor_tensor(ea[:, :], ea[:, :], lnu[:, :], ALU.mult).then_inc(dt_step, 1)
            dve.wait_ge(dt_step, 6)
            dve.tensor_tensor(ea[:, :], ea[:, :], wd[:, :], ALU.mult).then_inc(dt_step, 1)
            dve.wait_ge(dt_step, 7)
            dve.scalar_tensor_tensor(out=dt[:, :], in0=z[:, :], scalar=0.0, in1=ea[:, :], op0=ALU.max,
                                     op1=ALU.add).then_inc(dt_step, 1)
            dve.wait_ge(dt_step, 8)
            dve.tensor_scalar(dt[:, :], dt[:, :], DT_MIN, DT_MAX, ALU.max, ALU.min).then_inc(dt_step, 1)
            dve.wait_ge(dt_step, 9)
            dve.wait_ge(m_rows_in, 2 * DMA)
            dve.tensor_tensor(da[:, :], dt[:, :], m_a[:, :], ALU.mult).then_inc(dt_step, 1)
            dve.wait_ge(da_hi_done, 1)
            dve.tensor_tensor(da_lo[:, :], da[:, :], da_hi[:, :].bitcast(F32), ALU.subtract).then_inc(dt_step, 1)

            def m_group(g, first):
                def y_gate(g):
                    dve.wait_ge(m_y, g + 1)
                    dve.wait_ge(m_xd, g + 1)
                    for i in range(2):
                        h = slice(512 * i, 512 * i + 512)
                        dve.tensor_tensor(y[:, h], bank[1 + i][:, :], y[:, h], ALU.add).then_inc(m_ysum, 1)
                    for i in range(2):
                        h = slice(512 * i, 512 * i + 512)
                        dve.wait_ge(m_ysum, 2 * g + i + 1)
                        dve.wait_ge(m_sg, 2 * g + i + 1)
                        dve.tensor_tensor(y[:, h], y[:, h], sg[:, h], ALU.mult).then_inc(m_yg, 1)

                def y_mean(g):
                    dve.wait_ge(m_sq, g + 1)
                    dve.tensor_scalar(yms[:, :], yssq[:, :], 1.0 / MC, EPS, ALU.mult, ALU.add).then_inc(m_yms, 1)

                def y_norm(g):
                    dve.wait_ge(m_rstd, g + 1)
                    dve.tensor_scalar(y[:, :], y[:, :], yrstd[:, 0:1], None, ALU.mult).then_inc(m_yn, 1)

                def keep_yT(g):
                    for i in range(2):
                        dve.wait_ge(m_yT, 2 * g + i + 1)
                        dve.tensor_tensor(
                            yT[:, 4 * i:4 * i + 4, :], bank[3 + i][:, :].rearrange("p (c t) -> p c t", c=4),
                            m_nw[:, bass.ds(g, 1), 4 * i:4 * i + 4].rearrange("p a c -> p (a c)").unsqueeze(2)
                            .broadcast_to([P, 4, P]), ALU.mult).then_inc(m_yTk, 1)

                def conv(js, before):
                    for k in range(TAPS - 2, -1, -1):
                        back = TAPS - 1 - k
                        for i, j in enumerate(js):
                            b, r = (0, j) if j < 2 else (1 + (j - 2) // 4, (j - 2) % 4)
                            if back == 1:
                                dve.wait_ge(m_tap, NCH * g + js[-1] + 1)
                            else:
                                dve.wait_ge(m_conv, STEPS * g + before + (back - 2) * len(js) + i + 1)
                            dve.scalar_tensor_tensor(
                                out=xc[:, j, back:], in0=bank[b][:, P * r:P * r + P - back],
                                scalar=m_taps[:, bass.ds(TAPS * (NCH * g + j) + k, 1)], in1=xc[:, j, back:],
                                op0=ALU.mult, op1=ALU.add).then_inc(m_conv, 1)

                if first == "end":
                    y_gate(NG - 1)
                    y_mean(NG - 1)
                    y_norm(NG - 1)
                    keep_yT(NG - 1)
                    return
                if not first:
                    y_gate(g - 1)
                    y_mean(g - 1)
                    y_norm(g - 1)
                conv(range(2), 0)
                if not first:
                    keep_yT(g - 1)
                conv(range(2, 6), 6)
                dve.wait_ge(m_gfull, g + 1)
                dve.tensor_tensor(gm[:, :], bank[0][:, 256:256 + P], upto[:, :], ALU.mult).then_inc(m_gm, 1)
                if not first:
                    for c in (2, 3):
                        dve.wait_ge(wg_hi_done, KC * g + c + 1)
                        dve.tensor_tensor(wg_lo[:, c, :], m_wg[:, c, :], wg_hi[:, c, :].bitcast(F32), ALU.subtract)\
                            .then_inc(wg_lo2_done, 1)
                conv(range(6, 10), 18)
                dve.wait_ge(m_gm, g + 1)
                for q in range(4):
                    dve.wait_ge(m_exp, 4 * g + q + 1)
                    dve.tensor_tensor(m_e[:, 4 * q:4 * q + 4, :], m_e[:, 4 * q:4 * q + 4, :],
                                      gm[:, :].unsqueeze(1).broadcast_to([P, 4, P]), ALU.mult).then_inc(m_m, 1)
                dve.wait_ge(m_xtok, 2 * g + 2)
                dve.tensor_tensor(xdt[:, :, :], x_tok[:, :, :],
                                  dt[:, bass.ds(MH * g, MH)].unsqueeze(2).broadcast_to([P, MH, MP]), ALU.mult)\
                    .then_inc(m_xdt, 1)

            m_group(0, True)
            with dve.Fori(0, NG - 1) as i:
                m_group(i + 1, False)
            m_group(NG, "end")
            dve.wait_ge(m_out, NG)
            dve.tensor_copy(x[:, :], bank[7][:, :]).then_inc(x_ready, 1)
            layer_norm(5)
            dve.wait_ge(f_full, 1)
            dve.tensor_copy(f_l[:, :], bank[0][:, 0:NE]).then_inc(f_step, 1)
            dve.wait_ge(f_step, 1)
            dve.max(out=f_top[:, :], in_=f_l[:, :]).then_inc(f_step, 1)
            dve.wait_ge(f_step, 2)
            dve.tensor_scalar(f_nm[:, :], f_top[:, 0:1], -1.0, None, ALU.mult).then_inc(f_step, 1)
            dve.tensor_scalar(f_above[:, :], f_l[:, :], f_top[:, TOP2 - 1:TOP2], 0.0, ALU.is_gt, ALU.add,
                              accum_out=f_gt[:, 0:1]).then_inc(f_step, 1)
            dve.tensor_scalar(f_same[:, :], f_l[:, :], f_top[:, TOP2 - 1:TOP2], None, ALU.is_equal)\
                .then_inc(f_step, 1)
            dve.wait_ge(f_step, 5)
            dve.tensor_tensor_scan(f_rank[:, :], ones[:, 0:NE], f_same[:, :], 0.0, ALU.mult, ALU.add)\
                .then_inc(f_step, 1)
            dve.tensor_scalar(f_room[:, :], f_gt[:, :], -1.0, float(TOP2), ALU.mult, ALU.add).then_inc(f_step, 1)
            dve.wait_ge(f_step, 7)
            dve.scalar_tensor_tensor(out=f_same[:, :], in0=f_rank[:, :], scalar=f_room[:, 0:1], in1=f_same[:, :],
                                     op0=ALU.is_le, op1=ALU.mult).then_inc(f_step, 1)
            dve.wait_ge(f_step, 8)
            dve.tensor_tensor(f_above[:, :], f_above[:, :], f_same[:, :], ALU.add).then_inc(f_step, 1)
            dve.wait_ge(f_step, 9)
            dve.wait_ge(f_exp, 1)
            dve.tensor_tensor_reduce(out=f_w[:, :], in0=f_l[:, :], in1=f_above[:, :], scale=1.0, scalar=0.0,
                                     op0=ALU.mult, op1=ALU.add, accum_out=f_sum[:, 0:1]).then_inc(f_step, 1)
            dve.wait_ge(f_step, 10)
            dve.reciprocal(f_rs[:, :], f_sum[:, :]).then_inc(f_step, 1)
            dve.wait_ge(f_step, 11)
            dve.tensor_scalar(f_w[:, :], f_w[:, :], f_rs[:, 0:1], None, ALU.mult).then_inc(f_step, 1)
            dve.wait_ge(f_step, 12)
            dve.sem_inc(f_used, CREDIT)
            with dve.Fori(0, NE // 2) as i:
                for b in range(2):
                    dve.wait_ge(f_prod, 2 * i + b + 1)
                    dve.wait_ge(f_used, CREDIT + 2 * i + b)
                    dve.scalar_tensor_tensor(out=x[:, :], in0=bank[2 + b][:, :], scalar=f_w[:, bass.ds(2 * i + b, 1)],
                                             in1=x[:, :], op0=ALU.mult, op1=ALU.add).then_inc(f_used, 1)
            dve.wait_ge(f_used, CREDIT + NE)
            dve.sem_inc(x_ready, 1)

        @block.tensor
        def _(pe):
            def turn_x(k, src):
                for c in range(KC):
                    mm = pe.transpose(TR[0][:, c * P:c * P + P], src[:, c * P:c * P + P], ident[:, :])
                mm.then_inc(ln_turned, 1)

            def kv_tile(g, t):
                u = t // 2
                if t % 2 == 0:
                    pe.wait_ge(kv_kept, 8 * g + u + 1)
                if t == 0:
                    pe.wait_ge(kvw_lo_done, g + 1)
                b, r = t // 4, P * (t % 4)
                acc = KV[u % 2][:, (t % 2) * 2 * HD:(t % 2 + 1) * 2 * HD]
                for c in range(KC):
                    hi, lo = ctx_hi[:, b, c, r:r + P], ctx_lo[:, b, c, r:r + P]
                    pe.matmul(acc, hi, kvw_hi[:, c, :], start=(c == 0), stop=False)
                    pe.matmul(acc, hi, kvw_lo[:, c, :], start=False, stop=False)
                    mm = pe.matmul(acc, lo, kvw_hi[:, c, :], start=False, stop=(c == KC - 1))
                if t % 2 == 1:
                    mm.then_inc(kv_full, 1)

            pe.wait_ge(const_ready, 4)
            pe.sem_inc(pv_done, 1)
            pe.wait_ge(ln_x, 1)
            turn_x(0, xn)
            for t in range(TT):
                if t % 4 == 0:
                    pe.wait_ge(ctx_lo_done, t // 4 + 1)
                kv_tile(0, t)

            def group(g, more):
                def turn_k(b):
                    pe.wait_ge(k_normed, 4 * g + b + 1)
                    pe.wait_ge(lo_kept, 20 * g + b + 1)
                    for i in range(4):
                        mm = pe.transpose(TR[b][:, P * i:P * i + P], kv_raw[:, 4 * b + i, 0:HD], ident[:, :])
                    mm.then_inc(turned, 1)

                def turn_p(c):
                    pe.wait_ge(lo_kept, 20 * g + 4 + c + 1)
                    if c == 0:
                        pe.wait_ge(s_masked, len(S) + 16 * g + 13)
                    for h in range(R):
                        if c == 0:
                            pe.wait_ge(p_ready, 4 * g + h + 1)
                        mm = pe.transpose(TR[c % 4][:, P * h:P * h + P], scores[:, h, P * c:P * c + P], ident[:, :])
                    mm.then_inc(turned, 1)

                def pv(c):
                    if c == 0:
                        pe.wait_ge(ot_kept, g + 1)
                        pe.wait_ge(v_lo_done, 4 * g + 4)
                    pe.wait_ge(lo_kept, len(TR) + 20 * g + 4 + c + 1)
                    pe.matmul(OT[:, :], v_hi[:, c, :], pt_hi[:, c % PR, :], start=(c == 0), stop=False)
                    pe.matmul(OT[:, :], v_lo[:, c, :], pt_hi[:, c % PR, :], start=False, stop=False)
                    pe.matmul(OT[:, :], v_hi[:, c, :], pt_lo[:, c % 2, :], start=False, stop=(c == TT - 1))\
                        .then_inc(pv_done, 1)

                def ahead(*tiles):
                    if more:
                        for t in tiles:
                            kv_tile(g + 1, t)

                turn_k(0)
                turn_k(1)
                pe.wait_ge(o_added, g + 1)
                pe.wait_ge(a_xnT_lo_done, 1)
                for c in range(KC):
                    pe.wait_ge(a_wq_lo_done, KC * g + c + 1)
                    pe.matmul(M[:, :], a_xnT_hi[:, c, :], a_wq_hi[:, c, :], start=(c == 0), stop=False)
                    pe.matmul(M[:, :], a_xnT_hi[:, c, :], a_wq_lo[:, c, :], start=False, stop=False)
                    mm = pe.matmul(M[:, :], a_xnT_lo[:, c, :], a_wq_hi[:, c, :], start=False, stop=(c == KC - 1))
                mm.then_inc(q_full, 1)
                turn_k(2)
                turn_k(3)
                ahead(0, 1)
                pe.wait_ge(q_normed, g + 1)
                for h in range(R):
                    mm = pe.transpose(M[:, P * h:P * h + P], q_sb[:, h, :], ident[:, :])
                mm.then_inc(qt_full, 1)
                ahead(2, 3)
                pe.wait_ge(qt_lo_done, g + 1)
                for h in range(R):
                    for b in range(TB):
                        if h == 0:
                            pe.wait_ge(lo_kept, len(TR) + 20 * g + b + 1)
                        pe.wait_ge(s_masked, 16 * g + 4 * h + b + 1)
                        k_hi, k_lo = kt_hi[:, 512 * b:512 * b + 512], kt_lo[:, 512 * b:512 * b + 512]
                        pe.matmul(S[b][:, :], qt_hi[:, h, :], k_hi, start=True, stop=False)
                        pe.matmul(S[b][:, :], qt_hi[:, h, :], k_lo, start=False, stop=False)
                        pe.matmul(S[b][:, :], qt_lo[:, h, :], k_hi, start=False, stop=True).then_inc(s_full, 1)
                    ahead(*((4,), (5,), (), (6, 7, 8))[h])
                turn_p(0)
                turn_p(1)
                for c in range(TT):
                    if c + 2 < TT:
                        turn_p(c + 2)
                    pv(c)
                    if c in (2, 5, 8, 11):
                        ahead(9 + (c - 2) // 3)
                    if c == 6:
                        pe.wait_ge(dg_done, g + 1)
                        pe.matmul(M[:, :], ones[:, :], dg[:, :, :].rearrange("p h q -> p (h q)"),
                                  start=True, stop=True).then_inc(inverse_full, 1)
                ahead(13, 14, 15)
                if more:
                    pe.wait_ge(a_wo_lo_done, 4 * g + 4)
                    pe.wait_ge(ot_lo_done, g + 1)
                    for h in range(R):
                        pe.matmul(M[:, :], a_ot_hi[:, h, :], a_wo_hi[:, h, :], start=(h == 0), stop=False)
                        pe.matmul(M[:, :], a_ot_hi[:, h, :], a_wo_lo[:, h, :], start=False, stop=False)
                        mm = pe.matmul(M[:, :], ot_lo[:, h, :], a_wo_hi[:, h, :], start=False, stop=(h == R - 1))
                else:
                    pe.wait_ge(wo_in, DMA * (g + 1))
                    pe.wait_ge(ot_kept, g + 2)
                    for h in range(R):
                        mm = pe.matmul(M[:, :], ot[:, h, :], wo[:, h, :], start=(h == 0), stop=(h == R - 1))
                mm.then_inc(o_full, 1)

            with pe.Fori(0, NG - 1) as g:
                group(g, True)
            group(NG - 1, False)

            pe.wait_ge(x_ready, 2)
            pe.matmul(bank[7][:, :], ident[:, :], x[:, :], start=True, stop=False)
            pe.wait_ge(ln_x, 2)
            turn_x(1, xn)
            pe.wait_ge(ln_xT, 2)

            def project_kv(slot, use):
                pe.wait_ge(wqkv_in[slot], DMA * use)
                for c in range(KC):
                    mm = pe.matmul(bank[1][:, 0:2 * HD], xnT[:, c, :], wqkv[:, slot, c, R * HD:],
                                   start=(c == 0), stop=(c == KC - 1))
                mm.then_inc(b_kv_full, 1)

            def project_q(slot):
                for c in range(KC):
                    mm = pe.matmul(bank[0][:, :], xnT[:, c, :], wqkv[:, slot, c, 0:R * HD],
                                   start=(c == 0), stop=(c == KC - 1))
                mm.then_inc(b_q_full, 1)

            def project_out(g, slot, use, last):
                pe.wait_ge(bo_in[slot], DMA * use)
                pe.wait_ge(b_oT_kept, g + 1)
                for h in range(R):
                    mm = pe.matmul(bank[7][:, :], b_oT[:, h, :], bo[:, slot, h, :], start=False,
                                   stop=(last and h == R - 1))
                mm.then_inc(b_o_done, 1)

            def attend(g, slot, use, more, first=False):
                pe.wait_ge(b_q_kept, g + 1)
                pe.wait_ge(b_kv_kept, g + 1)
                for h in range(R):
                    pe.transpose(bank[2][:, P * h:P * h + P], b_q[:, h, :], ident[:, :])
                pe.transpose(bank[3][:, 0:P], b_kv[:, slot, 0:HD], ident[:, :]).then_inc(b_qk_turned, 1)
                if more:
                    project_kv(1 - slot, use + slot)
                pe.wait_ge(b_qT_kept, g + 1)
                pe.wait_ge(b_kT_kept, g + 1)
                for h in range(R):
                    mm = pe.matmul(bank[4][:, P * h:P * h + P], b_qT[:, h, :], b_kT[:, :], start=True, stop=True)
                mm.then_inc(b_s_full, 1)
                if more:
                    project_q(1 - slot)
                pe.wait_ge(b_normed, g + 1)
                for h in range(R):
                    mm = pe.transpose(bank[5][:, P * h:P * h + P], b_p[:, h, :], ident[:, :])
                mm.then_inc(b_p_turned, 1)
                if not first:
                    project_out(g - 1, 1 - slot, use - 1 + slot, False)
                pe.wait_ge(b_pT_kept, g + 1)
                pe.matmul(bank[6][:, :], b_kv[:, slot, HD:], b_pT[:, :, :].rearrange("p h q -> p (h q)"),
                          start=True, stop=True).then_inc(b_pv_done, 1)

            project_kv(0, 1)
            project_q(0)
            attend(0, 0, 1, True, True)
            with pe.Fori(0, NG // 2 - 1) as i:
                attend(2 * i + 1, 1, i + 1, True)
                attend(2 * i + 2, 0, i + 2, True)
            attend(NG - 1, 1, NG // 2, False)
            project_out(NG - 1, 1, NG // 2, True)

            pe.wait_ge(ln_x, 3)
            turn_x(2, xn)
            pe.wait_ge(ln_xT, 3)
            pe.wait_ge(small_in, 5 * DMA)
            for c in range(KC):
                mm = pe.matmul(bank[0][:, 0:E], xnT[:, c, :], rw[:, c, :], start=(c == 0), stop=(c == KC - 1))
            mm.then_inc(r_full, 1)
            pe.wait_ge(r_step, 12)
            pe.transpose(bank[5][0:E, 0:P], w_dense[:, :], ident[:, :]).then_inc(r_turned, 1)
            pe.wait_ge(r_T_kept, 1)
            pe.matmul(bank[1][:, :], w_T[:, :], eb[:, :], start=True, stop=True).then_inc(r_mixed, 1)

            pe.wait_ge(ln_x, 4)
            turn_x(3, xn)
            pe.wait_ge(ln_xT, 4)
            pe.wait_ge(c_in, 2 * DMA)
            for c in range(KC):
                mm = pe.matmul(bank[0][:, :], xnT[:, c, :], c_q[:, c, :], start=(c == 0), stop=(c == KC - 1))
            mm.then_inc(d_full, 1)
            pe.wait_ge(d_step, 1)
            for c in range(KC):
                mm = pe.transpose(bank[5][:, P * c:P * c + P], d_q[:, P * c:P * c + P], ident[:, :])
            mm.then_inc(d_full, 1)
            pe.wait_ge(d_kept, 1)
            for c in range(KC):
                mm = pe.matmul(bank[0][:, :], d_qT[:, c, :], c_k[:, c, :], start=(c == 0), stop=(c == KC - 1))
            mm.then_inc(d_full, 1)
            pe.wait_ge(d_kept, 2)
            for c in range(KC):
                mm = pe.transpose(bank[5][:, P * c:P * c + P], d_q[:, P * c:P * c + P], ident[:, :])
            mm.then_inc(d_full, 1)
            pe.wait_ge(d_step, 3)
            for b in range(TB):
                for c in range(KC):
                    hi, lo = ctx_hi[:, b, c, :], ctx_lo[:, b, c, :]
                    pe.matmul(bank[b][:, :], d_qkT_hi[:, c, :], hi, start=(c == 0), stop=False)
                    pe.matmul(bank[b][:, :], d_qkT_hi[:, c, :], lo, start=False, stop=False)
                    mm = pe.matmul(bank[b][:, :], d_qkT_lo[:, c, :], hi, start=False, stop=(c == KC - 1))
                mm.then_inc(d_s_full, 1)
            for b in range(TB):
                pe.wait_ge(d_exp, b + 1)
                if b >= 2:
                    pe.wait_ge(d_pT_kept, b - 1)
                for i in range(4):
                    t = 4 * b + i
                    mm = pe.transpose(bank[4 + b % 2][:, P * i:P * i + P], d_p[:, P * t:P * t + P], ident[:, :])
                mm.then_inc(d_turned, 1)
            pe.wait_ge(ctx_n_in, DMA)
            for b in range(TB):
                pe.wait_ge(d_pT_kept, b + 1)
                for i in range(4):
                    t = 4 * b + i
                    mm = pe.matmul(bank[6][:, :], d_pT[:, b, i, :], ctx_n[:, t, :], start=(t == 0),
                                   stop=(t == TT - 1))
            mm.then_inc(d_done, 1)
            pe.wait_ge(x_ready, 5)
            pe.matmul(bank[7][:, :], ident[:, :], x[:, :], start=True, stop=False)
            pe.wait_ge(ln_x, 5)
            turn_x(4, xn)
            pe.wait_ge(ln_xT, 5)
            pe.wait_ge(m_small_in, 6 * DMA)
            for c in range(KC):
                mm = pe.matmul(bank[6][:, 0:NG * MH], xnT[:, c, :], m_wdt[:, c, :], start=(c == 0),
                               stop=(c == KC - 1))
            mm.then_inc(dt_full, 1)

            def m_outputs_turned(g):
                pe.wait_ge(m_yn, g + 1)
                for i in range(2):
                    for j in range(4):
                        n = P * (4 * i + j)
                        mm = pe.transpose(bank[3 + i][:, P * j:P * j + P], y[:, n:n + P], ident[:, :])
                    mm.then_inc(m_yT, 1)

            def m_project_out(g, last):
                pe.wait_ge(m_wo_in, DMA * (g + 1))
                for c in range(MCC):
                    if c % 4 == 0:
                        pe.wait_ge(m_yTk, 2 * g + c // 4 + 1)
                    mm = pe.matmul(bank[7][:, :], yT[:, c, :], m_wo[:, c, :], start=False,
                                   stop=(last and c == MCC - 1))
                mm.then_inc(m_out, 1)

            def m_group(g, first):
                def seg(q):
                    pe.wait_ge(m_r, 8 * g + 2 * q + 2)
                    if q >= 2:
                        pe.wait_ge(m_exp, 4 * g + q - 1)
                    elif first:
                        pe.wait_ge(m_xtok, q + 1)
                    for part, stop in ((r_hi, False), (r_lo, True)):
                        mm = pe.matmul(bank[5 + q % 2][:, :], later[:, :],
                                       part[:, 4 * q:4 * q + 4, :].rearrange("p h n -> p (h n)"),
                                       start=not stop, stop=stop)
                    mm.then_inc(m_seg, 1)

                def channels(js):
                    for j in js:
                        b, r = (0, j) if j < 2 else (1 + (j - 2) // 4, (j - 2) % 4)
                        for c in range(KC):
                            mm = pe.matmul(bank[b][:, P * r:P * r + P], m_wx[:, c, P * j:P * j + P], xnT[:, c, :],
                                           start=(c == 0), stop=(c == KC - 1))
                    mm.then_inc(m_in, 1)

                def sources_targets():
                    pe.wait_ge(m_silu, 3 * g + 1)
                    pe.matmul(bank[0][:, 256:256 + P], xc[:, 0, :], xc[:, 1, :], start=True, stop=True)\
                        .then_inc(m_gfull, 1)

                def turn_channels():
                    for i in range(2):
                        if not first:
                            pe.wait_ge(m_exp, 4 * g + 3 + i)
                        pe.wait_ge(m_silu, 3 * g + 2 + i)
                        for j in range(4):
                            mm = pe.transpose(bank[5 + i][:, P * j:P * j + P], xc[:, 2 + 4 * i + j, :], ident[:, :])
                        mm.then_inc(m_xT, 1)

                def gates():
                    if first:
                        pe.wait_ge(xnT_lo_done, 1)
                        pe.wait_ge(wg_lo_done, KC)
                    for i in range(2):
                        for c in range(KC):
                            if not first and i == 0:
                                if c < 2:
                                    pe.wait_ge(wg_lo_done, 2 * g + c + 3)
                                else:
                                    pe.wait_ge(wg_lo2_done, 2 * g + c - 3)
                            hi, lo = wg_hi[:, c, 512 * i:512 * i + 512], wg_lo[:, c, 512 * i:512 * i + 512]
                            pe.matmul(bank[3 + i][:, :], xnT_hi[:, c, :], hi, start=(c == 0), stop=False)
                            pe.matmul(bank[3 + i][:, :], xnT_hi[:, c, :], lo, start=False, stop=False)
                            mm = pe.matmul(bank[3 + i][:, :], xnT_lo[:, c, :], hi, start=False, stop=(c == KC - 1))
                        mm.then_inc(m_gate, 1)

                if not first:
                    seg(0)
                    seg(1)
                pe.wait_ge(m_wx_in, DMA * (g + 1))
                channels(range(2))
                if first:
                    channels(range(2, 6))
                    channels(range(6, 10))
                    sources_targets()
                    gates()
                    turn_channels()
                    pe.wait_ge(m_const, 5)
                    for q in range(4):
                        seg(q)
                else:
                    seg(2)
                    seg(3)
                    pe.wait_ge(m_ysum, 2 * g - 1)
                    channels(range(2, 6))
                    m_outputs_turned(g - 1)
                    pe.wait_ge(m_ysum, 2 * g)
                    channels(range(6, 10))
                    sources_targets()
                    m_project_out(g - 1, False)
                    turn_channels()
                    gates()
                pe.wait_ge(m_xdt, g + 1)
                for h in range(MH):
                    if h % 4 == 0:
                        pe.wait_ge(m_m, 4 * g + h // 4 + 1)
                    mm = pe.matmul(bank[1 + h // 8][:, MP * (h % 8):MP * (h % 8) + MP], m_e[:, h, :], xdt[:, h, :],
                                   start=True, stop=True)
                mm.then_inc(m_y, 1)

            m_group(0, True)
            with pe.Fori(0, NG - 1) as i:
                m_group(i + 1, False)
            m_outputs_turned(NG - 1)
            m_project_out(NG - 1, True)
            pe.wait_ge(ln_x, 6)
            turn_x(5, xn)
            pe.wait_ge(ln_xT, 6)
            for c in range(KC):
                mm = pe.matmul(bank[0][:, 0:NE], xnT[:, c, :], gw[:, c, :], start=(c == 0), stop=(c == KC - 1))
            mm.then_inc(f_full, 1)
            pe.wait_ge(ew_in, NE * DMA)

            def expert(e, b):
                for c in range(KC):
                    mm = pe.matmul(bank[2 + b][:, :], xnT[:, c, :],
                                   ew[:, bass.ds(e, 1), c, :].rearrange("p a n -> p (a n)"),
                                   start=(c == 0), stop=(c == KC - 1))
                mm.then_inc(f_prod, 1)

            expert(0, 0)
            expert(1, 1)
            with pe.Fori(0, NE // 2 - 1) as i:
                for b in range(2):
                    pe.wait_ge(f_used, CREDIT + 2 * i + b + 1)
                    expert(2 * i + b + 2, b)


def kernel(**inputs):
    import numpy as _np
    import concourse.bacc as _bacc
    from concourse import mybir as _mybir
    from concourse.bass_utils import run_bass_kernel_spmd as _run

    w = {k: _np.asarray(v) for k, v in inputs.items()}
    arrays = layout(w)
    nc = _bacc.Bacc("TRN2", target_bir_lowering=False, num_devices=1)
    ins = {}
    sent = {}
    for name, a in arrays.items():
        sent[name] = _np.ascontiguousarray(a)
        ins[name] = nc.dram_tensor(name, sent[name].shape, _mybir.dt.from_np(sent[name].dtype),
                                   kind="ExternalInput").ap()
    out = nc.dram_tensor("out", (P, D), F32, kind="ExternalOutput").ap()
    perceiver(nc, ins, out)
    r = _run(nc, [sent], core_ids=[0])
    return _np.asarray(r.results[0]["out"]).reshape(1, P, D)


def layout(w):
    import numpy as np

    def in_rows(m):
        return m.T.reshape(m.shape[1] // P, P, m.shape[0]).transpose(1, 0, 2)

    def by_group(m, n):
        return m.reshape(n, m.shape[0] // n, KC, P).transpose(0, 3, 2, 1)

    def out_group(m):
        return m.T.reshape(NG, R, HD, D).transpose(0, 2, 1, 3)

    ctx = w["ctx_4096"][0]
    a = {
        "x": w["x"][0],
        "ctxT": ctx.reshape(TB, 512, KC, P).transpose(0, 3, 2, 1),
        "mask": w["mask_1x1xSxS2_ff0"][0, 0],
        "a_norm": np.stack([w["L0_xattn_q_norm_w"], w["L0_xattn_k_norm_w"]], 1),
        "a_q": by_group(w["L0_xattn_q_proj_w"], NG),
        "a_kv": np.concatenate([by_group(w["L0_xattn_k_proj_w"], NG), by_group(w["L0_xattn_v_proj_w"], NG)], 3),
        "a_o": out_group(w["L0_xattn_o_proj_w"]),
    }
    a |= {
        "b_qkv": np.concatenate([by_group(w["L0_attn_" + n], NG) for n in ("wq", "wk", "wv")], 3),
        "b_o": out_group(w["L0_attn_wo"]),
        "rw": in_rows(w["L0_ffn_router_weight"]),
        "rb": w["L0_ffn_router_bias"],
        "eb": w["L0_ffn_expert_bias"],
        "c_q": in_rows(w["L1_xattn_Wq"]),
        "c_k": w["L1_xattn_Wk"].reshape(KC, P, D).transpose(1, 0, 2),
        "bq": w["L1_xattn_bq"],
        "bk": w["L1_xattn_bk"],
        "ctx_n": ctx.reshape(TT, P, D).transpose(1, 0, 2),
    }
    inter, ng = NG * MC, NG * P
    gate, ch, bm, cm, wdt = np.split(w["L1_attn_in_proj_w"], np.cumsum([inter, inter, ng, ng]))
    n = KC, P

    def conv_rows(m):
        ch, bm, cm = np.split(m, np.cumsum([inter, ng]))
        return np.concatenate([v.reshape(NG, -1, *v.shape[1:]) for v in (bm, cm, ch)], 1)

    wx = np.concatenate([v.reshape(NG, -1, D) for v in (bm, cm, ch)], 1)
    a |= {
        "m_wx": wx.reshape(NG, NCH * P, *n).transpose(0, 3, 2, 1),
        "m_wg": by_group(gate, NG),
        "m_wo": w["L1_attn_out_proj_w"].T.reshape(NG, MCC, P, D).transpose(0, 2, 1, 3),
        "m_wdt": in_rows(wdt),
        "m_dtb": w["L1_attn_dt_bias"],
        "m_d": w["L1_attn_D"],
        "m_a": -np.arange(1, NG * MH + 1, dtype=np.float32),
        "m_taps": conv_rows(w["L1_attn_conv_w"][:, 0, :]).reshape(NG, NCH, P, TAPS).transpose(2, 0, 1, 3)
        .reshape(P, -1),
        "m_cb": conv_rows(w["L1_attn_conv_b"]).reshape(NG, NCH, P).transpose(2, 0, 1).reshape(P, -1),
        "m_nw": w["L1_attn_norm_w"].reshape(NG, MCC, P).transpose(2, 0, 1),
        "gw": w["L1_ffn_gate_w"].reshape(KC, P, NE).transpose(1, 0, 2),
        "ew": w["L1_ffn_expert_w"].reshape(NE, KC, P, D).transpose(0, 2, 1, 3),
    }
    return a
```

```python
from contextlib import ExitStack

import concourse.bass as bass
from concourse import mybir

F32 = mybir.dt.float32
F32R = mybir.dt.float32r
ALU = mybir.AluOpType
ACT = mybir.ActivationFunctionType
AX = mybir.AxisListType

P = 128
D = 512
KC = D // P
EPS = 1e-5
NEG = -3.0e38
DMA = 16

T = 2048
TT = T // P
TB = T // 512
HD = 128
NG = 8
R = 4
SCALE = HD ** -0.5
SLIDE = 64
E = 64
TOP = 8
MH = 16
MP = 64
MC = MH * MP
MCC = MC // P
NCH = MCC + 2
TAPS = 4
STEPS = NCH * (TAPS - 1)
DT_STEPS = 11
DT_MIN, DT_MAX = 1e-3, 100.0
NE = 8
TOP2 = 2
EARLY = 6
PARTS = R - 1 + TB
PR = 3

SBUF0 = 16512
SBUF_BYTES = 212832


def perceiver(nc, ins, out):
    ctx = ExitStack()
    with ctx:
        starts = {}

        def place(name, shape, dt, at):
            size = 4
            for n in shape[1:]:
                size *= n
            assert at + size <= SBUF_BYTES, (name, at + size)
            starts[name] = at
            return nc.alloc_sbuf_tensor_at(name, shape, dt, offset=SBUF0 + at)

        def stack(at, *arrays):
            made = []
            for name, shape, dt in arrays:
                made.append(place(name, shape, dt, at))
                size = 4
                for n in shape[1:]:
                    size *= n
                at += -(-size // 32) * 32
            return made, at

        def sem(name):
            return ctx.enter_context(nc.semaphore(name))

        bank = [ctx.enter_context(nc.psum_tensor(f"bank{i}", [P, 512], F32)) for i in range(8)]

        (x, xn, xnT, ident, ones, stats, mv, var_eps, rstd, powm), at_a = stack(
            0,
            ("x", [P, D], F32),
            ("xn", [P, D], F32),
            ("xnT", [P, KC, P], F32),
            ("ident", [P, P], F32),
            ("ones", [P, P], F32),
            ("stats", [P, 6], F32),
            ("mv", [P, 2], F32),
            ("var_eps", [P, 1], F32),
            ("rstd", [P, 1], F32),
            ("powm", [P, 4], F32),
        )
        (ctx_hi, ctx_lo), at_w = stack(
            at_a, ("ctx_hi", [P, TB, KC, 512], F32R), ("ctx_lo", [P, TB, KC, 512], F32R))

        ((kv_raw, kvw, kvw_hi, kvw_lo, wq, wo, kt_hi, kt_lo, v_hi, v_lo, qt_hi, qt_lo, q_sb, scores,
          mask, pt_hi, pt_lo, a_xnT_hi, kj, kssq, kms, krstd, qssq, qms, qrstd, mx, nm, sums, last_sums, rs, qkw, qkv2),
         end_a) = stack(
            at_w,
            ("kv_raw", [P, TT, 2 * HD], F32),
            ("kvw", [P, KC, 2 * HD], F32),
            ("kvw_hi", [P, KC, 2 * HD], F32R),
            ("kvw_lo", [P, KC, 2 * HD], F32R),
            ("wq", [P, KC, R * HD], F32),
            ("wo", [P, R, D], F32),
            ("kt_hi", [P, T], F32R),
            ("kt_lo", [P, T], F32R),
            ("v_hi", [P, TT, HD], F32R),
            ("v_lo", [P, TT, HD], F32R),
            ("qt_hi", [P, R, P], F32R),
            ("qt_lo", [P, R, P], F32R),
            ("q_sb", [P, R, HD], F32),
            ("scores", [P, R, T], F32),
            ("mask", [P, T], F32),
            ("pt_hi", [P, PR, R * P], F32R),
            ("pt_lo", [P, 2, R * P], F32R),
            ("a_xnT_hi", [P, KC, P], F32R),
            ("kj", [P, 2, HD], F32),
            ("kssq", [P, TT], F32),
            ("kms", [P, TT], F32),
            ("krstd", [P, TT], F32),
            ("qssq", [P, R], F32),
            ("qms", [P, R], F32),
            ("qrstd", [P, R], F32),
            ("mx", [P, R, TB], F32),
            ("nm", [P, R], F32),
            ("sums", [P, R], F32),
            ("last_sums", [P, TB], F32),
            ("rs", [P, R], F32),
            ("qkw", [P, 1], F32),
            ("qkv2", [P, 2], F32),
        )
        ctx_raw = scores[:, :, :].rearrange("p b (c n) -> p b c n", c=KC)
        dg = xn[:, :].rearrange("p (h q) -> p h q", h=R)
        ot = place("ot", [P, R, P], F32, starts["xn"])
        ot_lo = place("ot_lo", [P, R, P], F32R, starts["xn"])
        a_xnT_lo = place("a_xnT_lo", [P, KC, P], F32R, starts["xnT"])
        (a_wo_hi, a_ot_hi, a_wq_hi), _ = stack(
            starts["scores"],
            ("a_wo_hi", [P, R, D], F32R), ("a_ot_hi", [P, R, P], F32R), ("a_wq_hi", [P, KC, R * HD], F32R))
        a_wo_lo = place("a_wo_lo", [P, R, D], F32R, starts["wo"])
        a_wq_lo = place("a_wq_lo", [P, KC, R * HD], F32R, starts["wq"])
        r_sb = q_sb

        (wqkv, bo), at_b = stack(
            at_w,
            ("wqkv", [P, 2, KC, (R + 2) * HD], F32),
            ("bo", [P, 2, R, D], F32))
        (b_q, b_kv, b_qT, b_kT, b_p, b_pT, b_oT, band, b_mx, b_nm, b_sum, b_rs), _ = stack(
            at_b,
            ("b_q", [P, R, HD], F32),
            ("b_kv", [P, 2, 2 * HD], F32),
            ("b_qT", [P, R, P], F32),
            ("b_kT", [P, P], F32),
            ("b_p", [P, R, P], F32),
            ("b_pT", [P, R, P], F32),
            ("b_oT", [P, R, P], F32),
            ("band", [P, P], F32),
            ("b_mx", [P, R], F32),
            ("b_nm", [P, R], F32),
            ("b_sum", [P, R], F32),
            ("b_rs", [P, R], F32))

        at_split = at_w + 77 * 1024
        (bq_hi, bo_hi, b_xnT_hi, b_xnT_lo, b_oT_hi), end_split = stack(
            at_split,
            ("bq_hi", [P, 2, KC, (R + 2) * HD], F32R),
            ("bo_hi", [P, 2, R, D], F32R),
            ("b_xnT_hi", [P, KC, P], F32R),
            ("b_xnT_lo", [P, KC, P], F32R),
            ("b_oT_hi", [P, R, P], F32R))
        bq_lo = place("bq_lo", [P, 2, KC, (R + 2) * HD], F32R, starts["wqkv"])
        bo_lo = place("bo_lo", [P, 2, R, D], F32R, starts["bo"])
        b_oT_lo = place("b_oT_lo", [P, R, P], F32R, starts["b_oT"])

        (c_q, c_k), at_m = stack(
            at_w + 61 * 1024,
            ("c_q", [P, KC, D], F32),
            ("c_k", [P, KC, D], F32))
        assert at_m == at_split
        at_small = at_m + 52 * 1024 + 256
        assert end_split <= at_small
        (rw, rb, eb), at_s2 = stack(
            at_small,
            ("rw", [P, KC, E], F32),
            ("rb", [P, E], F32),
            ("eb", [E, D], F32))
        (bqc, bkc, wqk, b_row, v_col, b_one), end_fold = stack(
            at_split + 4 * (R + 2) * HD * KC - 10 * 1024 - 512,
            ("bqc", [P, KC], F32),
            ("bkc", [P, KC], F32),
            ("wqk", [P, KC, D], F32),
            ("b_row", [1, D], F32),
            ("v_col", [P, KC], F32),
            ("b_one", [1, 1], F32))
        assert end_fold <= at_split + 4 * (R + 2) * HD * KC
        (logits, r_nm, r_sum, r_rs, top8, above, same, rank, room, w_dense, w_sum, w_T, r_gt), _ = stack(
            at_w + 41 * 1024,
            ("logits", [P, E], F32),
            ("r_nm", [P, 1], F32),
            ("r_sum", [P, 1], F32),
            ("r_rs", [P, 1], F32),
            ("top8", [P, 8], F32),
            ("above", [P, E], F32),
            ("same", [P, E], F32),
            ("rank", [P, E], F32),
            ("room", [P, 1], F32),
            ("w_dense", [P, E], F32),
            ("w_sum", [P, 1], F32),
            ("w_T", [E, P], F32),
            ("r_gt", [P, 1], F32))
        (ctx_n,), at_d = stack(at_w, ("ctx_n", [P, TT, D], F32))
        (d_q, d_qkT_hi, d_qkT_lo, d_p, d_pT, d_qb, d_mx, d_m, d_nm, d_sum, d_rs, d_bias), end_d = stack(
            at_d,
            ("d_q", [P, D], F32),
            ("d_qkT_hi", [P, KC, P], F32R),
            ("d_qkT_lo", [P, KC, P], F32R),
            ("d_p", [P, T], F32),
            ("d_pT", [P, TB, 4, P], F32),
            ("d_qb", [P, 1], F32),
            ("d_mx", [P, TB], F32),
            ("d_m", [P, 1], F32),
            ("d_nm", [P, 1], F32),
            ("d_sum", [P, 1], F32),
            ("d_rs", [P, 1], F32),
            ("d_bias", [P, 1], F32))
        (m_wdt, m_dtb, m_taps, m_cb, m_nw, gw), end_ms = stack(
            end_d + 2048,
            ("m_wdt", [P, KC, NG * MH], F32),
            ("m_dtb", [P, NG * MH], F32),
            ("m_taps", [P, NG * NCH * TAPS], F32),
            ("m_cb", [P, NG * NCH], F32),
            ("m_nw", [P, NG, MCC], F32),
            ("gw", [P, KC, NE], F32))
        assert end_ms <= at_w + 61 * 1024
        (m_wx, m_wg, m_wo), end_mw = stack(
            at_m,
            ("m_wx", [P, KC, NCH * P], F32),
            ("m_wg", [P, KC, MC], F32),
            ("m_wo", [P, MCC, D], F32))
        assert end_mw <= at_small
        (m_e, r_hi, r_lo, xc, x_tok, xdt, sg, y, yT, gm, dt, da, da_hi, da_lo, later, upto, z, ea, ue, wd, lnu,
         m_d, m_a, yssq, yms, yrstd), end_mm = stack(
            at_w,
            ("m_e", [P, MH, P], F32),
            ("r_hi", [P, MH, P], F32R),
            ("r_lo", [P, MH, P], F32R),
            ("xc", [P, NCH, P], F32),
            ("x_tok", [P, MH, MP], F32),
            ("xdt", [P, MH, MP], F32),
            ("sg", [P, MC], F32),
            ("y", [P, MC], F32),
            ("yT", [P, MCC, P], F32),
            ("gm", [P, P], F32),
            ("dt", [P, NG * MH], F32),
            ("da", [P, NG * MH], F32),
            ("da_hi", [P, NG * MH], F32R),
            ("da_lo", [P, NG * MH], F32R),
            ("later", [P, P], F32R),
            ("upto", [P, P], F32),
            ("z", [P, NG * MH], F32),
            ("ea", [P, NG * MH], F32),
            ("ue", [P, NG * MH], F32),
            ("wd", [P, NG * MH], F32),
            ("lnu", [P, NG * MH], F32),
            ("m_d", [P, NG * MH], F32),
            ("m_a", [P, NG * MH], F32),
            ("yssq", [P, 1], F32),
            ("yms", [P, 1], F32),
            ("yrstd", [P, 1], F32))
        assert end_mm <= end_d + 2048
        (ew,), _ = stack(at_a, ("ew", [P, NE, KC, D], F32))
        ew_lo = place("ew_lo", [P, NE, KC, D], F32R, at_a)
        (ew_hi,), end_ew = stack(at_w + 61 * 1024, ("ew_hi", [P, NE, KC, D], F32R))
        assert end_ew <= at_small and at_w + 61 * 1024 + 4 * EARLY * KC * D <= at_m + 4 * KC * (NCH * P + MC)
        (wg_hi,), end_wg = stack(at_w + 61 * 1024, ("wg_hi", [P, KC, MC], F32R))
        assert end_wg <= at_m
        (wg_lo,), _ = stack(at_m + 4 * KC * NCH * P, ("wg_lo", [P, KC, MC], F32R))
        (xnT_hi, xnT_lo), at_f = stack(
            at_small, ("xnT_hi", [P, KC, P], F32R), ("xnT_lo", [P, KC, P], F32R))
        (f_l, f_nm, f_top, f_above, f_same, f_rank, f_gt, f_room, f_w, f_sum, f_rs), _ = stack(
            at_f,
            ("f_l", [P, NE], F32),
            ("f_nm", [P, 1], F32),
            ("f_top", [P, 8], F32),
            ("f_above", [P, NE], F32),
            ("f_same", [P, NE], F32),
            ("f_rank", [P, NE], F32),
            ("f_gt", [P, 1], F32),
            ("f_room", [P, 1], F32),
            ("f_w", [P, NE], F32),
            ("f_sum", [P, 1], F32),
            ("f_rs", [P, 1], F32))

        x_in, ctx_in, mask_in, w_in = sem("x_in"), [sem(f"ctx_in{i}") for i in range(TB)], sem("mask_in"), sem("w_in")
        kvw_in, wq_in, wo_in = sem("kvw_in"), sem("wq_in"), sem("wo_in")
        const_ready = sem("const_ready")
        x_ready, ln_step, ln_rstd = (sem(n) for n in ("x_ready", "ln_step", "ln_rstd"))
        ln_x, ln_turned, ln_xT = (sem(n) for n in ("ln_x", "ln_turned", "ln_xT"))
        ctx_hi_done, ctx_lo_done, kvw_hi_done, kvw_lo_done = (sem(n) for n in (
            "ctx_hi_done", "ctx_lo_done", "kvw_hi_done", "kvw_lo_done"))
        kv_full, kv_kept, k_squared, k_meaned, k_rstd, k_normed = (sem(n) for n in (
            "kv_full", "kv_kept", "k_squared", "k_meaned", "k_rstd", "k_normed"))
        turned, hi_kept, lo_kept = (sem(n) for n in ("turned", "hi_kept", "lo_kept"))
        q_full, q_squared, q_meaned, q_rstd, q_normed, qt_full, qt_hi_done, qt_lo_done, qkw_done = (sem(n) for n in (
            "q_full", "q_squared", "q_meaned", "q_rstd", "q_normed", "qt_full", "qt_hi_done", "qt_lo_done", "qkw_done"))
        s_full, s_seen, s_masked, max_ready, p_ready = (
            sem(n) for n in ("s_full", "s_seen", "s_masked", "max_ready", "p_ready"))
        v_hi_done, v_lo_done, pv_done, rs_done, dg_done, inverse_full, r_kept, ot_kept, o_full, o_added = (
            sem(n) for n in (
            "v_hi_done", "v_lo_done", "pv_done", "rs_done", "dg_done", "inverse_full", "r_kept",
            "ot_kept", "o_full", "o_added"))
        xnT_hi_done, xnT_lo_done, a_wq_hi_done, a_wq_lo_done, a_wo_hi_done, a_wo_lo_done, ot_hi_done, ot_lo_done = (
            sem(n) for n in ("xnT_hi_done", "xnT_lo_done", "a_wq_hi_done", "a_wq_lo_done", "a_wo_hi_done",
                             "a_wo_lo_done", "ot_hi_done", "ot_lo_done"))
        out_done = sem("out_done")
        wqkv_in, bo_in = [sem(f"wqkv_in{i}") for i in range(2)], [sem(f"bo_in{i}") for i in range(2)]
        band_ready = sem("band_ready")
        b_qk_turned, b_kv_full, b_q_full, b_s_full, b_p_turned, b_pv_done, b_o_done = (sem(n) for n in (
            "b_qk_turned", "b_kv_full", "b_q_full", "b_s_full", "b_p_turned", "b_pv_done", "b_o_done"))
        b_q_kept, b_kv_kept, b_qT_kept, b_kT_kept, b_masked, b_max, b_exp, b_inverse, b_normed, b_pT_kept, b_oT_kept = (
            sem(n) for n in ("b_q_kept", "b_kv_kept", "b_qT_kept", "b_kT_kept", "b_masked", "b_max", "b_exp",
                             "b_inverse", "b_normed", "b_pT_kept", "b_oT_kept"))
        bq_hi_done, bq_lo_done, bq_lo1_done, bo_hi_done, bo_lo_done, b_oT_hi_done, b_oT_lo_done = (
            sem(n) for n in ("bq_hi_done", "bq_lo_done", "bq_lo1_done", "bo_hi_done", "bo_lo_done", "b_oT_hi_done",
                             "b_oT_lo_done"))
        fold_full, fold_kept = sem("fold_full"), sem("fold_kept")
        small_in, router_full, router_step, router_act = (sem(n) for n in (
            "small_in", "router_full", "router_step", "router_act"))
        c_in, ctx_n_in, d_full, d_kept, d_s_full, d_s_maxed, d_step, d_exp, d_turned, d_pT_kept, d_done = (
            sem(n) for n in ("c_in", "ctx_n_in", "d_full", "d_kept", "d_s_full", "d_s_maxed", "d_step", "d_exp",
                             "d_turned", "d_pT_kept", "d_done"))

        m_small_in, m_wx_in, m_wg_in, m_wo_in = (sem(n) for n in (
            "m_small_in", "m_wx_in", "m_wg_in", "m_wo_in"))
        m_const, dt_full, dt_step, dt_act = (sem(n) for n in (
            "m_const", "dt_full", "dt_step", "dt_act"))
        m_seg, m_in, m_gfull, m_xT, m_gate, m_y, m_yT, m_out = (sem(n) for n in (
            "m_seg_full", "m_in_full", "m_g_full", "m_x_turned", "m_gate_full", "m_y_full", "m_y_turned", "m_out_full"))
        m_exp, m_tap, m_silu, m_xtok, m_sg, m_sq = (sem(n) for n in (
            "m_exp", "m_tap", "m_silu", "m_xtok", "m_sg", "m_squared"))
        m_conv, m_gm, m_m, m_xdt, m_ysum, m_yg, m_yms, m_yn, m_yTk = (sem(n) for n in (
            "m_conv", "m_gm", "m_m", "m_xdt", "m_ysum", "m_yg", "m_yms", "m_yn", "m_yT_kept"))
        m_r, m_xd, m_rstd = (sem(n) for n in ("m_r", "m_xd", "m_rstd"))
        wg_hi_done, wg_lo_done, wg_lo2_done = (sem(n) for n in ("wg_hi_done", "wg_lo_done", "wg_lo2_done"))
        ew_hi_done, ew_lo_done, ew_lo2_done = (sem(n) for n in ("ew_hi_done", "ew_lo_done", "ew_lo2_done"))
        ew_in, f_step, f_exp, f_prod, f_used = (sem(n) for n in (
            "ew_in", "f_step", "f_exp", "f_prod", "f_used"))

        KV = bank[0:2]
        TR = bank[4:6] + bank[2:4]
        S = TR
        OT = bank[6]
        M = bank[7]
        CREDIT = 2

        def last(g, n):
            return isinstance(g, int) and g + n >= NG

        block = ctx.enter_context(nc.Block())

        @block.sync
        def _(sp):
            sp.dma_start(x[:, :], ins["x"]).then_inc(x_in, DMA)
            sp.dma_start(kvw[:, :, :], ins["a_kv"][0]).then_inc(kvw_in, DMA)
            for b in range(TB):
                sp.dma_start(ctx_raw[:, b], ins["ctxT"][b]).then_inc(ctx_in[b], DMA)
            sp.dma_start(wq[:, :, :], ins["a_q"][0]).then_inc(wq_in, DMA)
            sp.dma_start(mask[:, :], ins["mask"]).then_inc(mask_in, DMA)
            sp.dma_start(wo[:, :, :], ins["a_o"][0]).then_inc(wo_in, DMA)

            def next_kvw(g):
                sp.wait_ge(kvw_hi_done, g)
                sp.wait_ge(kvw_lo_done, g)
                sp.dma_start(kvw[:, :, :], ins["a_kv"][g]).then_inc(kvw_in, DMA)

            def next_q(g):
                sp.wait_ge(q_full, g)
                sp.dma_start(wq[:, :, :], ins["a_q"][g]).then_inc(wq_in, DMA)

            def next_o(g):
                sp.wait_ge(o_full, g)
                sp.dma_start(wo[:, :, :], ins["a_o"][g]).then_inc(wo_in, DMA)

            next_kvw(1)
            with sp.Fori(0, NG - 2) as g:
                next_q(g + 1)
                next_kvw(g + 2)
                next_o(g + 1)
            next_q(NG - 1)
            next_o(NG - 1)

            sp.wait_ge(turned, 20 * (NG - 1) + 4)
            sp.wait_ge(v_lo_done, 4 * NG)
            sp.wait_ge(q_full, NG)

            def load_qkv(g, slot):
                sp.dma_start(wqkv[:, slot], ins["b_qkv"][g]).then_inc(wqkv_in[slot], DMA)

            def load_o(g, slot):
                sp.dma_start(bo[:, slot], ins["b_o"][g]).then_inc(bo_in[slot], DMA)

            load_qkv(0, 0)
            load_qkv(1, 1)
            load_o(0, 0)
            sp.wait_ge(o_full, NG)
            load_o(1, 1)
            for name, to in (("rw", rw), ("rb", rb), ("eb", eb)):
                src = ins[name]
                if name == "rb":
                    src = src.partition_broadcast(P)
                sp.dma_start(to[:], src).then_inc(small_in, DMA)

            def next_qkv(g, slot):
                sp.wait_ge(b_q_full, g - 1)
                load_qkv(g, slot)

            def next_bo(g, slot):
                sp.wait_ge(b_o_done, g - 1)
                load_o(g, slot)

            next_qkv(2, 0)
            next_qkv(3, 1)
            with sp.Fori(0, NG // 2 - 2) as i:
                next_qkv(2 * i + 4, 0)
                next_bo(2 * i + 2, 0)
                next_qkv(2 * i + 5, 1)
                next_bo(2 * i + 3, 1)
            next_bo(NG - 2, 0)
            sp.wait_ge(b_q_full, NG - 1)
            sp.dma_start(bqc[:, :], ins["bqc"]).then_inc(c_in, DMA)
            sp.dma_start(bkc[:, :], ins["bkc"]).then_inc(c_in, DMA)
            sp.dma_start(c_q[:, :, :], ins["c_q"]).then_inc(c_in, DMA)
            sp.dma_start(c_k[:, :, :], ins["c_k"]).then_inc(c_in, DMA)
            next_bo(NG - 1, 1)
            sp.wait_ge(b_o_done, NG)
            sp.dma_start(ctx_n[:, :, :], ins["ctx_n"]).then_inc(ctx_n_in, DMA)
            for name, to in (("m_wdt", m_wdt), ("m_dtb", m_dtb), ("m_taps", m_taps), ("m_cb", m_cb), ("m_nw", m_nw),
                             ("gw", gw)):
                src = ins[name]
                if name == "m_dtb":
                    src = src.partition_broadcast(P)
                sp.dma_start(to[:], src).then_inc(m_small_in, DMA)
            sp.dma_start(m_wg[:, :, :], ins["m_wg"][0]).then_inc(m_wg_in, DMA)
            sp.dma_start(m_wo[:, :, :], ins["m_wo"][0]).then_inc(m_wo_in, DMA)
            sp.wait_ge(fold_full, 7)
            sp.dma_start(m_wx[:, :, :], ins["m_wx"][0]).then_inc(m_wx_in, DMA)
            sp.wait_ge(x_ready, 5)
            sp.wait_ge(m_small_in, 6 * DMA)
            sp.dma_start(m_a[:, :], ins["m_a"].partition_broadcast(P)).then_inc(m_small_in, DMA)
            sp.dma_start(m_d[:, :], ins["m_d"].partition_broadcast(P)).then_inc(m_small_in, DMA)

            def next_wx(g):
                sp.wait_ge(m_in, 3 * g)
                sp.dma_start(m_wx[:, :, :], ins["m_wx"][g]).then_inc(m_wx_in, DMA)

            def next_wg(g):
                sp.wait_ge(m_gate, 2 * g)
                sp.dma_start(m_wg[:, :, :], ins["m_wg"][g]).then_inc(m_wg_in, DMA)

            def next_wo(g):
                sp.wait_ge(m_out, g)
                sp.dma_start(m_wo[:, :, :], ins["m_wo"][g]).then_inc(m_wo_in, DMA)

            def expert(e):
                sp.dma_start(ew[:, bass.ds(e, 1), :, :], ins["ew"][e].unsqueeze(1)).then_inc(ew_in, DMA)

            next_wx(1)
            next_wg(1)
            expert(0)
            with sp.Fori(0, NG - 2) as i:
                next_wx(i + 2)
                next_wo(i + 1)
                next_wg(i + 2)
                expert(i + 1)
            expert(NE - 1)
            next_wo(NG - 1)
            sp.wait_ge(x_ready, 7)
            sp.dma_start(out, x[:, :]).then_inc(out_done, DMA)
            sp.wait_ge(out_done, DMA)

        @block.gpsimd
        def _(pool):
            pool.memset(ident[:, :], 0.0).then_inc(const_ready, 1)
            pool.memset(ones[:, :], 1.0).then_inc(const_ready, 1)
            pool.memset(powm[:, :], -0.5).then_inc(const_ready, 1)
            pool.wait_ge(const_ready, 3)
            pool.affine_select(out=ident[:, :], in_=ident[:, :], compare_op=ALU.not_equal, fill=1.0, base=0,
                               pattern=[[-1, P]], channel_multiplier=1).then_inc(const_ready, 1)
            pool.dma_start(qkv2[:, :], ins["a_norm"]).then_inc(w_in, DMA)

            def rsqrt_row(k):
                pool.wait_ge(ln_step, 3 * k + 3)
                pool.tensor_tensor(rstd[:, :], var_eps[:, :], powm[:, 0:1], ALU.pow).then_inc(ln_rstd, 1)

            def k_rsqrt(g, j):
                pool.wait_ge(k_meaned, 4 * g + j + 1)
                pool.tensor_tensor(krstd[:, 4 * j:4 * j + 4], kms[:, 4 * j:4 * j + 4], powm[:, :], ALU.pow)\
                    .then_inc(k_rstd, 1)

            def v_low(g, j):
                pool.wait_ge(v_hi_done, 4 * g + j + 1)
                pool.tensor_tensor(v_lo[:, 4 * j:4 * j + 4, :], kv_raw[:, 4 * j:4 * j + 4, HD:],
                                   v_hi[:, 4 * j:4 * j + 4, :].bitcast(F32), ALU.subtract).then_inc(v_lo_done, 1)

            def wq_low(g):
                for c in range(KC):
                    pool.wait_ge(a_wq_hi_done, KC * g + c + 1)
                    pool.tensor_tensor(a_wq_lo[:, c, :], wq[:, c, :], a_wq_hi[:, c, :].bitcast(F32), ALU.subtract)\
                        .then_inc(a_wq_lo_done, 1)

            rsqrt_row(0)
            for j in range(TB):
                if j == TB // 2:
                    wq_low(0)
                k_rsqrt(0, j)

            def group(g, more):
                v_low(g, 0)
                pool.wait_ge(q_meaned, g + 1)
                pool.tensor_tensor(qrstd[:, :], qms[:, :], powm[:, :], ALU.pow).then_inc(q_rstd, 1)
                for j in range(1, TB):
                    v_low(g, j)
                if more:
                    for j in range(TB - 1):
                        k_rsqrt(g + 1, j)
                    wq_low(g + 1)
                    k_rsqrt(g + 1, TB - 1)

            with pool.Fori(0, NG - 1) as g:
                group(g, True)
            group(NG - 1, False)

            pool.wait_ge(x_ready, 2)
            pool.memset(band[:, :], 0.0).then_inc(band_ready, 1)
            pool.wait_ge(band_ready, 1)
            pool.affine_select(out=band[:, :], in_=band[:, :], compare_op=ALU.is_ge, fill=-1.0e30, base=0,
                               pattern=[[-1, P]], channel_multiplier=1).then_inc(band_ready, 1)
            pool.wait_ge(band_ready, 2)
            pool.affine_select(out=band[:, :], in_=band[:, :], compare_op=ALU.is_ge, fill=-1.0e30, base=SLIDE - 1,
                               pattern=[[1, P]], channel_multiplier=-1).then_inc(band_ready, 1)
            rsqrt_row(1)

            def out_weights_low(g, slot):
                for h in range(R):
                    pool.wait_ge(bo_hi_done, R * g + h + 1)
                    pool.tensor_tensor(bo_lo[:, slot, h, :], bo[:, slot, h, :], bo_hi[:, slot, h, :].bitcast(F32),
                                       ALU.subtract).then_inc(bo_lo_done, 1)

            for c in range(KC):
                pool.wait_ge(bq_hi_done, c + 1)
                pool.tensor_tensor(bq_lo[:, 1, c, :], wqkv[:, 1, c, :], bq_hi[:, 1, c, :].bitcast(F32), ALU.subtract)\
                    .then_inc(bq_lo1_done, 1)
            with pool.Fori(0, NG // 2) as i:
                out_weights_low(2 * i, 0)
                out_weights_low(2 * i + 1, 1)
            for k in range(2, 4):
                rsqrt_row(k)

            def gate_low(g, cs):
                for c in cs:
                    pool.wait_ge(wg_hi_done, KC * g + c + 1)
                    pool.tensor_tensor(wg_lo[:, c, :], m_wg[:, c, :], wg_hi[:, c, :].bitcast(F32), ALU.subtract)\
                        .then_inc(wg_lo_done, 1)

            gate_low(0, range(KC))
            rsqrt_row(4)
            pool.memset(upto[:, :], 1.0).then_inc(m_const, 1)
            pool.memset(gm[:, :], 1.0).then_inc(m_const, 1)
            pool.wait_ge(m_const, 2)
            pool.affine_select(out=upto[:, :], in_=upto[:, :], compare_op=ALU.is_ge, fill=0.0, base=0,
                               pattern=[[1, P]], channel_multiplier=-1).then_inc(m_const, 1)
            pool.affine_select(out=gm[:, :], in_=gm[:, :], compare_op=ALU.is_gt, fill=0.0, base=0,
                               pattern=[[-1, P]], channel_multiplier=1).then_inc(m_const, 1)
            pool.wait_ge(m_const, 4)

            def decay_rows(g):
                for q in range(4):
                    for part, to in ((da_hi, r_hi), (da_lo, r_lo)):
                        pool.tensor_tensor(
                            to[:, 4 * q:4 * q + 4, :],
                            part[:, bass.ds(MH * g + 4 * q, 4)].bitcast(F32).unsqueeze(2).broadcast_to([P, 4, P]),
                            upto[:, :].unsqueeze(1).broadcast_to([P, 4, P]), ALU.mult).then_inc(m_r, 1)

            def y_rstd(g):
                pool.wait_ge(m_yms, g + 1)
                pool.tensor_tensor(yrstd[:, :], yms[:, :], powm[:, 0:1], ALU.pow).then_inc(m_rstd, 1)

            def skip(g, first):
                if not first:
                    pool.wait_ge(m_yT, 2 * g)
                pool.wait_ge(m_xtok, 2 * g + 2)
                pool.tensor_tensor(y[:, :].rearrange("p (h n) -> p h n", h=MH), x_tok[:, :, :],
                                   m_d[:, bass.ds(MH * g, MH)].unsqueeze(2).broadcast_to([P, MH, MP]), ALU.mult)\
                    .then_inc(m_xd, 1)

            pool.wait_ge(dt_step, DT_STEPS)
            decay_rows(0)
            pool.wait_ge(m_seg, 4)
            decay_rows(1)
            pool.wait_ge(m_small_in, 8 * DMA)
            skip(0, True)
            with pool.Fori(0, NG - 2) as i:
                y_rstd(i)
                gate_low(i + 1, (0, 1))
                pool.wait_ge(m_seg, 4 * i + 8)
                decay_rows(i + 2)
                skip(i + 1, False)
            y_rstd(NG - 2)
            gate_low(NG - 1, (0, 1))
            skip(NG - 1, False)

            def experts_low(es):
                for e in es:
                    pool.wait_ge(ew_hi_done, e + 1)
                    pool.tensor_tensor(ew_lo[:, e], ew[:, e], ew_hi[:, e].bitcast(F32), ALU.subtract)\
                        .then_inc(ew_lo_done, 1)

            experts_low(range(1))
            y_rstd(NG - 1)
            experts_low(range(1, EARLY // 2))
            rsqrt_row(5)
            experts_low(range(EARLY, NE))

        @block.scalar
        def _(act):
            def kvw_high(g):
                act.wait_ge(kvw_in, DMA * (g + 1))
                act.activation(kvw_hi[:, :, :], kvw[:, :, :], ACT.Copy).then_inc(kvw_hi_done, 1)

            def k_square(g, t):
                act.wait_ge(kv_kept, CREDIT + 8 * g + t // 2 + 1)
                act.wait_ge(k_squared, 16 * g + t + 1)
                act.activation(kj[:, t % 2, :], kv_raw[:, t, 0:HD], ACT.Square, accum_out=kssq[:, t:t + 1])\
                    .then_inc(k_squared, 1)

            def high(g, n, out, in_):
                act.wait_ge(turned, 20 * g + n + 1)
                act.activation(out, in_, ACT.Copy).then_inc(hi_kept, 1)

            def wq_high(g):
                act.wait_ge(wq_in, DMA * (g + 1))
                for c in range(KC):
                    act.activation(a_wq_hi[:, c, :], wq[:, c, :], ACT.Copy).then_inc(a_wq_hi_done, 1)

            act.sem_inc(k_squared, CREDIT)
            kvw_high(0)
            for b in range(TB):
                act.wait_ge(ctx_in[b], DMA)
                for c in range(0, KC, 2):
                    act.activation(ctx_hi[:, b, c:c + 2], ctx_raw[:, b, c:c + 2], ACT.Copy).then_inc(ctx_hi_done, 1)
            act.wait_ge(ln_xT, 1)
            act.activation(a_xnT_hi[:, :, :], xnT[:, :, :], ACT.Copy).then_inc(xnT_hi_done, 1)
            for t in range(TT // 2):
                k_square(0, t)
            act.wait_ge(ctx_lo_done, 2 * TB)
            wq_high(0)
            for t in range(TT // 2, TT):
                k_square(0, t)

            def group(g, more):
                def v_high(j):
                    act.activation(v_hi[:, 4 * j:4 * j + 4, :], kv_raw[:, 4 * j:4 * j + 4, HD:], ACT.Copy)\
                        .then_inc(v_hi_done, 1)

                for b in range(2):
                    high(g, b, kt_hi[:, 512 * b:512 * b + 512], TR[b][:, :])
                act.wait_ge(pv_done, 1 + 16 * g)
                v_high(0)
                if more:
                    act.wait_ge(kv_full, 8 * g + 8)
                    kvw_high(g + 1)
                act.wait_ge(q_full, g + 1)
                for h in range(R):
                    act.activation(xn[:, h * HD:h * HD + HD], M[:, h * HD:h * HD + HD], ACT.Square,
                                   accum_out=qssq[:, h:h + 1]).then_inc(q_squared, 1)
                for b in range(2, 4):
                    high(g, b, kt_hi[:, 512 * b:512 * b + 512], TR[b][:, :])
                for j in range(1, TB):
                    v_high(j)
                act.wait_ge(qt_full, g + 1)
                act.activation(qt_hi[:, :, :], M[:, :].rearrange("p (h q) -> p h q", h=R), ACT.Copy,
                               scale=qkw[:, 0:1]).then_inc(qt_hi_done, 1)
                def last_head(b):
                    p = scores[:, R - 1, 512 * b:512 * b + 512]
                    act.activation(p, p, ACT.Exp, bias=nm[:, R - 1:R], accum_out=last_sums[:, b:b + 1])\
                        .then_inc(p_ready, 1)

                for h in range(R):
                    if more and h < 3:
                        k_square(g + 1, 2 * h)
                        k_square(g + 1, 2 * h + 1)
                    act.wait_ge(max_ready, 4 * g + h + 1)
                    if h < R - 1:
                        act.activation(scores[:, h, :], scores[:, h, :], ACT.Exp, bias=nm[:, h:h + 1],
                                       accum_out=sums[:, h:h + 1]).then_inc(p_ready, 1)
                    else:
                        last_head(0)
                        last_head(1)
                for c in range(TT):
                    act.wait_ge(pv_done, 1 + 16 * g + max(c - PR + 1, 0))
                    high(g, 4 + c, pt_hi[:, c % PR, :], TR[c % 4][:, :])
                    if c < 2:
                        last_head(c + 2)
                    if more and c == 2:
                        k_square(g + 1, 6)
                        k_square(g + 1, 7)
                    if more and c in (6, 12):
                        t = 8 if c == 6 else 10
                        k_square(g + 1, t)
                        k_square(g + 1, t + 1)
                    if c == 8:
                        act.wait_ge(inverse_full, g + 1)
                        act.activation(r_sb[:, :, :], M[:, :].rearrange("p (h q) -> p h q", h=R), ACT.Copy)\
                            .then_inc(r_kept, 1)
                if more:
                    act.wait_ge(wo_in, DMA * (g + 1))
                    for h in range(R):
                        act.activation(a_wo_hi[:, h, :], wo[:, h, :], ACT.Copy).then_inc(a_wo_hi_done, 1)
                    act.wait_ge(ot_kept, g + 2)
                    act.activation(a_ot_hi[:, :, :], ot[:, :, :], ACT.Copy).then_inc(ot_hi_done, 1)
                    wq_high(g + 1)
                    for t in range(12, 16):
                        k_square(g + 1, t)

            with act.Fori(0, NG - 1) as g:
                group(g, True)
            group(NG - 1, False)

            def keep_projections(g, slot):
                act.wait_ge(b_kv_full, g + 1)
                act.activation(b_kv[:, slot, :], bank[1][:, 0:2 * HD], ACT.Copy).then_inc(b_kv_kept, 1)
                act.wait_ge(b_q_full, g + 1)
                act.activation(b_q[:, :, :], bank[0][:, :].rearrange("p (h q) -> p h q", h=R), ACT.Copy)\
                    .then_inc(b_q_kept, 1)

            def keep_fold(n, to, at):
                act.wait_ge(fold_full, n)
                act.activation(to, at, ACT.Copy).then_inc(fold_kept, 1)

            def qkv_high(n, slot, use, cs):
                act.wait_ge(wqkv_in[slot], DMA * use)
                for c in cs:
                    act.activation(bq_hi[:, slot, c, :], wqkv[:, slot, c, :], ACT.Copy).then_inc(bq_hi_done, 1)

            def outputs_high(g):
                act.wait_ge(b_oT_kept, g + 1)
                act.activation(b_oT_hi[:, :, :], b_oT[:, :, :], ACT.Copy).then_inc(b_oT_hi_done, 1)

            def attend(g, slot, use, first=False):
                more, split = not last(g, 1), not last(g, 2)
                act.wait_ge(b_qk_turned, g + 1)
                act.activation(b_kT[:, :], bank[3][:, 0:P], ACT.Copy).then_inc(b_kT_kept, 1)
                if not first:
                    outputs_high(g - 1)
                if split and not first:
                    qkv_high(g + 2, slot, use + 1, (0, 1))
                for h in range(R):
                    if h == 0:
                        act.wait_ge(b_max, g + 1)
                    act.activation(b_p[:, h, :], b_p[:, h, :], ACT.Exp, bias=b_nm[:, h:h + 1],
                                   accum_out=b_sum[:, h:h + 1]).then_inc(b_exp, 1)
                if more:
                    keep_projections(g + 1, 1 - slot)
                else:
                    keep_fold(1, wqk[:, 0, :], bank[0][:, :])
                act.wait_ge(b_p_turned, g + 1)
                act.activation(b_pT[:, :, :], bank[5][:, :].rearrange("p (h q) -> p h q", h=R), ACT.Copy)\
                    .then_inc(b_pT_kept, 1)
                if split:
                    qkv_high(g + 2, slot, use + 1, range(KC) if first else (2, 3))
                act.wait_ge(bo_in[slot], DMA * use)
                for h in range(R):
                    act.activation(bo_hi[:, slot, h, :], bo[:, slot, h, :], ACT.Copy).then_inc(bo_hi_done, 1)

            act.wait_ge(x_ready, 2)
            qkv_high(1, 1, 1, range(KC))
            act.wait_ge(ln_xT, 2)
            act.activation(b_xnT_hi[:, :, :], xnT[:, :, :], ACT.Copy).then_inc(xnT_hi_done, 1)
            keep_projections(0, 0)
            attend(0, 0, 1, True)
            with act.Fori(0, NG // 2 - 2) as i:
                attend(2 * i + 1, 1, i + 1)
                attend(2 * i + 2, 0, i + 2)
            for g in range(NG - 3, NG):
                attend(g, g % 2, g // 2 + 1)
            outputs_high(NG - 1)
            keep_fold(2, b_row[:, :], bank[1][0:1, :])
            keep_fold(3, wqk[:, 1, :], bank[2][:, :])

            act.wait_ge(router_step, 2)
            act.activation(logits[:, :], logits[:, :], ACT.Exp, bias=r_nm[:, 0:1], accum_out=r_sum[:, 0:1])\
                .then_inc(router_act, 1)
            keep_fold(4, wqk[:, 2, :], bank[6][:, :])
            act.wait_ge(router_full, 2)
            act.activation(w_T[:, :], bank[5][0:E, 0:P], ACT.Copy).then_inc(router_act, 1)

            keep_fold(5, wqk[:, 3, :], bank[7][:, :])
            act.wait_ge(d_full, 1)
            act.activation(d_q[:, :], bank[0][:, :], ACT.Copy).then_inc(d_kept, 1)
            keep_fold(6, v_col[:, :], bank[7][:, 0:KC])
            act.activation(b_one[:, :], bank[7][0:1, KC:KC + 1], ACT.Copy).then_inc(fold_kept, 1)
            act.wait_ge(d_full, 2)
            act.activation(d_qkT_hi[:, :, :], bank[5][:, :].rearrange("p (c t) -> p c t", c=KC), ACT.Copy)\
                .then_inc(d_kept, 1)
            act.wait_ge(d_step, 6)
            for b in range(TB):
                act.activation(d_p[:, 512 * b:512 * b + 512], bank[b][:, :], ACT.Exp, bias=d_bias[:, 0:1],
                               scale=D ** -0.5, accum_out=d_mx[:, b:b + 1]).then_inc(d_exp, 1)
            for b in range(TB):
                act.wait_ge(d_turned, b + 1)
                act.activation(d_pT[:, b], bank[4 + b % 2][:, :].rearrange("p (i t) -> p i t", i=4), ACT.Copy)\
                    .then_inc(d_pT_kept, 1)

            def gate_high(g, cs):
                act.wait_ge(m_wg_in, DMA * (g + 1))
                for c in cs:
                    act.activation(wg_hi[:, c, :], m_wg[:, c, :], ACT.Copy).then_inc(wg_hi_done, 1)

            gate_high(0, range(KC))
            act.wait_ge(ln_xT, 5)
            act.activation(xnT_hi[:, :, :], xnT[:, :, :], ACT.Copy).then_inc(xnT_hi_done, 1)
            act.wait_ge(m_const, 4)
            act.activation(later[:, :], gm[:, :], ACT.Copy).then_inc(m_const, 1)
            act.wait_ge(dt_step, 2)
            act.activation(ea[:, :], ea[:, :], ACT.Exp, scale=-1.0).then_inc(dt_act, 1)
            act.wait_ge(dt_step, 3)
            act.activation(lnu[:, :], ue[:, :], ACT.Ln).then_inc(dt_act, 1)
            act.wait_ge(dt_step, DT_STEPS - 1)
            act.activation(da_hi[:, :], da[:, :], ACT.Copy).then_inc(dt_act, 1)

            def m_group(g, first):
                def decays(q):
                    act.wait_ge(m_seg, 4 * g + q + 1)
                    act.activation(m_e[:, 4 * q:4 * q + 4, :],
                                   bank[(1 if first else 5) + q % 2][:, :].rearrange("p (h n) -> p h n", h=4), ACT.Exp)\
                        .then_inc(m_exp, 1)

                def taps(part, js):
                    act.wait_ge(m_in, 3 * g + part + 1)
                    for j in js:
                        b, r = (0, j) if j < 2 else (1 + (j - 2) // 4, (j - 2) % 4)
                        act.activation(xc[:, j, :], bank[b][:, P * r:P * r + P], ACT.Identity,
                                       bias=m_cb[:, bass.ds(NCH * g + j, 1)],
                                       scale=m_taps[:, bass.ds(TAPS * (NCH * g + j) + TAPS - 1, 1)])\
                            .then_inc(m_tap, 1)

                def silu(lo, hi, step):
                    act.wait_ge(m_conv, STEPS * g + step)
                    act.activation(xc[:, lo:hi, :], xc[:, lo:hi, :], ACT.Silu).then_inc(m_silu, 1)

                def keep_channels():
                    for i in range(2):
                        act.wait_ge(m_xT, 2 * g + i + 1)
                        if not first and i == 0:
                            act.wait_ge(m_xd, g)
                        act.activation(x_tok[:, 8 * i:8 * i + 8, :],
                                       bank[5 + i][:, :].rearrange("p (h n) -> p h n", n=MP), ACT.Copy)\
                            .then_inc(m_xtok, 1)

                def gates():
                    for i in range(2):
                        act.wait_ge(m_gate, 2 * g + i + 1)
                        if not first:
                            act.wait_ge(m_sq, g)
                        act.activation(sg[:, 512 * i:512 * i + 512], bank[3 + i][:, :], ACT.Silu).then_inc(m_sg, 1)

                if not first:
                    act.wait_ge(m_y, g)
                    decays(0)
                    decays(1)
                    square(g - 1)
                taps(0, range(2))
                if not first:
                    decays(2)
                    decays(3)
                    gate_high(g, (0, 1))
                taps(1, range(2, 6))
                silu(0, 2, 6)
                if not first:
                    gate_high(g, (2, 3))
                taps(2, range(6, 10))
                silu(2, 6, 18)
                silu(6, 10, 30)
                if first:
                    gates()
                    decays(0)
                    decays(1)
                    keep_channels()
                    decays(2)
                    decays(3)
                else:
                    keep_channels()
                    gates()

            def square(g):
                act.wait_ge(m_yg, 2 * g + 2)
                act.activation(sg[:, :], y[:, :], ACT.Square, accum_out=yssq[:, 0:1]).then_inc(m_sq, 1)

            m_group(0, True)
            with act.Fori(0, NG - 1) as i:
                m_group(i + 1, False)

            def experts_high(es):
                for e in es:
                    act.activation(ew_hi[:, e], ew[:, e], ACT.Copy).then_inc(ew_hi_done, 1)

            act.wait_ge(ew_in, NE * DMA)
            act.wait_ge(m_gate, 2 * NG)
            experts_high(range(2))
            square(NG - 1)
            experts_high(range(2, EARLY))
            act.wait_ge(m_out, NG)
            experts_high(range(EARLY, NE - 1))
            act.wait_ge(ln_xT, 6)
            act.activation(xnT_hi[:, :, :], xnT[:, :, :], ACT.Copy).then_inc(xnT_hi_done, 1)
            act.wait_ge(f_step, 5)
            act.activation(f_l[:, :], f_l[:, :], ACT.Exp, bias=f_nm[:, 0:1]).then_inc(f_exp, 1)
            experts_high(range(NE - 1, NE))

        @block.vector
        def _(dve):
            def norm(k):
                dve.wait_ge(x_ready, k + 1)
                dve.bn_stats(stats[:, :], x[:, :]).then_inc(ln_step, 1)
                dve.wait_ge(ln_step, 3 * k + 1)
                dve.bn_aggr(mv[:, :], stats[:, :]).then_inc(ln_step, 1)
                dve.wait_ge(ln_step, 3 * k + 2)
                dve.tensor_scalar(var_eps[:, :], mv[:, 1:2], 1.0, EPS, ALU.mult, ALU.add).then_inc(ln_step, 1)
                dve.wait_ge(ln_rstd, k + 1)
                dve.tensor_scalar(xn[:, :], x[:, :], mv[:, 0:1], rstd[:, 0:1], ALU.subtract, ALU.mult)\
                    .then_inc(ln_x, 1)

            def keep_turned(k):
                dve.wait_ge(ln_turned, k + 1)
                dve.tensor_copy(xnT[:, :, :], TR[0][:, :].rearrange("p (c t) -> p c t", c=KC)).then_inc(ln_xT, 1)

            def layer_norm(k):
                norm(k)
                keep_turned(k)

            def keep_kv(g, u):
                dve.wait_ge(kv_full, 8 * g + u + 1)
                dve.tensor_copy(kv_raw[:, 2 * u:2 * u + 2, :], KV[u % 2][:, :].rearrange("p (t n) -> p t n", t=2))\
                    .then_inc(kv_kept, 1)

            def replace_kv(g, u):
                j = u // 2
                dve.wait_ge(turned, 20 * (g - 1) + j + 1)
                dve.wait_ge(v_lo_done, 4 * (g - 1) + j + 1)
                keep_kv(g, u)

            def k_mean(g, j):
                dve.wait_ge(k_squared, CREDIT + 16 * g + 4 * j + 4)
                dve.tensor_scalar(kms[:, 4 * j:4 * j + 4], kssq[:, 4 * j:4 * j + 4], 1.0 / HD, EPS,
                                  ALU.mult, ALU.add).then_inc(k_meaned, 1)

            def k_norm(g, j):
                dve.wait_ge(k_rstd, 4 * g + j + 1)
                k = kv_raw[:, 4 * j:4 * j + 4, 0:HD]
                dve.tensor_tensor(k, k, krstd[:, 4 * j:4 * j + 4].unsqueeze(2).broadcast_to([P, 4, HD]),
                                  ALU.mult).then_inc(k_normed, 1)

            def kvw_low(g):
                dve.wait_ge(kvw_hi_done, g + 1)
                dve.tensor_tensor(kvw_lo[:, :, :], kvw[:, :, :], kvw_hi[:, :, :].bitcast(F32), ALU.subtract)\
                    .then_inc(kvw_lo_done, 1)

            def low(g, n, out, in_, hi):
                dve.wait_ge(hi_kept, 20 * g + n + 1)
                dve.tensor_tensor(out, in_, hi.bitcast(F32), ALU.subtract).then_inc(lo_kept, 1)

            dve.sem_inc(ot_kept, 1)
            dve.sem_inc(o_added, 1)
            dve.sem_inc(kv_kept, CREDIT)
            dve.sem_inc(lo_kept, len(TR))
            dve.sem_inc(s_masked, len(S))
            dve.wait_ge(x_in, DMA)
            dve.sem_inc(x_ready, 1)
            norm(0)
            kvw_low(0)

            def ctx_low(b):
                for c in range(0, KC, 2):
                    dve.wait_ge(ctx_hi_done, 2 * b + c // 2 + 1)
                    dve.tensor_tensor(ctx_lo[:, b, c:c + 2], ctx_raw[:, b, c:c + 2],
                                      ctx_hi[:, b, c:c + 2].bitcast(F32), ALU.subtract).then_inc(ctx_lo_done, 1)

            ctx_low(0)
            ctx_low(1)
            dve.wait_ge(w_in, DMA)
            dve.scalar_tensor_tensor(out=qkw[:, :], in0=qkv2[:, 0:1], scalar=SCALE, in1=qkv2[:, 1:2],
                                     op0=ALU.mult, op1=ALU.mult).then_inc(qkw_done, 1)
            for u in range(TT // 2):
                keep_kv(0, u)
                if u == 0:
                    ctx_low(2)
                if u == 1:
                    keep_turned(0)
                if u == 2:
                    ctx_low(3)
                if u == 3:
                    dve.wait_ge(xnT_hi_done, 1)
                    dve.tensor_tensor(a_xnT_lo[:, :, :], xnT[:, :, :], a_xnT_hi[:, :, :].bitcast(F32),
                                      ALU.subtract).then_inc(xnT_lo_done, 1)
                if u % 2 == 0 and u > 0:
                    k_mean(0, u // 2 - 1)
                if u % 2 == 1 and u > 1:
                    k_norm(0, u // 2 - 1)
            k_mean(0, 3)
            k_norm(0, 3)
            dve.wait_ge(mask_in, DMA)

            def group(g, more):
                def kt_low(b):
                    low(g, b, kt_lo[:, 512 * b:512 * b + 512], TR[b][:, :], kt_hi[:, 512 * b:512 * b + 512])

                kt_low(0)
                kt_low(1)
                if more:
                    kvw_low(g + 1)
                dve.wait_ge(q_squared, 4 * g + 4)
                dve.tensor_scalar(qms[:, :], qssq[:, :], 1.0 / HD, EPS, ALU.mult, ALU.add).then_inc(q_meaned, 1)
                kt_low(2)
                kt_low(3)
                dve.wait_ge(q_rstd, g + 1)
                dve.tensor_tensor(q_sb[:, :, :], M[:, :].rearrange("p (h q) -> p h q", h=R),
                                  qrstd[:, :].unsqueeze(2).broadcast_to([P, R, HD]), ALU.mult).then_inc(q_normed, 1)
                if more:
                    replace_kv(g + 1, 0)
                dve.wait_ge(qt_hi_done, g + 1)
                dve.scalar_tensor_tensor(out=qt_lo[:, :, :].rearrange("p h q -> p (h q)"), in0=M[:, :],
                                         scalar=qkw[:, 0:1],
                                         in1=qt_hi[:, :, :].bitcast(F32).rearrange("p h q -> p (h q)"),
                                         op0=ALU.mult, op1=ALU.subtract).then_inc(qt_lo_done, 1)
                for h in range(R):
                    for b in range(TB):
                        dve.wait_ge(s_full, 16 * g + 4 * h + b + 1)
                        dve.sem_inc(s_seen, 1)
                        dve.tensor_tensor_reduce(
                            out=scores[:, h, 512 * b:512 * b + 512], in0=S[b][:, :],
                            in1=mask[:, 512 * b:512 * b + 512], scale=1.0, scalar=NEG, op0=ALU.add, op1=ALU.max,
                            accum_out=mx[:, h, b:b + 1]).then_inc(s_masked, 1)
                    dve.wait_ge(s_masked, len(S) + 16 * g + 4 * h + 4)
                    dve.tensor_reduce(nm[:, h:h + 1], mx[:, h, :], AX.X, ALU.max, negate=True).then_inc(max_ready, 1)
                    if more:
                        if h == 0:
                            replace_kv(g + 1, 1)
                        if h == 1:
                            k_mean(g + 1, 0)
                            replace_kv(g + 1, 2)
                        if h == 2:
                            k_norm(g + 1, 0)
                        if h == 3:
                            replace_kv(g + 1, 3)
                for c in range(TT):
                    dve.wait_ge(pv_done, 1 + 16 * g + max(c - 1, 0))
                    low(g, 4 + c, pt_lo[:, c % 2, :], TR[c % 4][:, :], pt_hi[:, c % PR, :])
                    if more:
                        if c == 3:
                            k_mean(g + 1, 1)
                        if c == 5:
                            k_norm(g + 1, 1)
                        if c == 4:
                            replace_kv(g + 1, 4)
                        if c == 10:
                            replace_kv(g + 1, 5)
                        if c == 14:
                            k_mean(g + 1, 2)
                    if c == 2:
                        dve.wait_ge(p_ready, PARTS * g + PARTS)
                        dve.tensor_reduce(sums[:, R - 1:R], last_sums[:, :], AX.X, ALU.add).then_inc(rs_done, 1)
                        dve.wait_ge(rs_done, 2 * g + 1)
                        dve.reciprocal(rs[:, :], sums[:, :]).then_inc(rs_done, 1)
                        dve.wait_ge(rs_done, 2 * g + 2)
                        dve.tensor_tensor(dg[:, :, :], ident[:, :].unsqueeze(1).broadcast_to([P, R, P]),
                                          rs[:, :].unsqueeze(2).broadcast_to([P, R, P]), ALU.mult)\
                            .then_inc(dg_done, 1)
                dve.wait_ge(pv_done, 1 + 16 * g + 16)
                dve.wait_ge(r_kept, g + 1)
                dve.tensor_tensor(ot[:, :, :], OT[:, :].rearrange("p (h q) -> p h q", h=R), r_sb[:, :, :], ALU.mult)\
                    .then_inc(ot_kept, 1)
                if more:
                    for h in range(R):
                        dve.wait_ge(a_wo_hi_done, 4 * g + h + 1)
                        dve.tensor_tensor(a_wo_lo[:, h, :], wo[:, h, :], a_wo_hi[:, h, :].bitcast(F32), ALU.subtract)\
                            .then_inc(a_wo_lo_done, 1)
                    dve.wait_ge(ot_hi_done, g + 1)
                    dve.tensor_tensor(ot_lo[:, :, :], ot[:, :, :], a_ot_hi[:, :, :].bitcast(F32), ALU.subtract)\
                        .then_inc(ot_lo_done, 1)
                    replace_kv(g + 1, 6)
                    k_norm(g + 1, 2)
                    replace_kv(g + 1, 7)
                    k_mean(g + 1, 3)
                dve.wait_ge(o_full, g + 1)
                dve.tensor_tensor(x[:, :], x[:, :], M[:, :], ALU.add).then_inc(o_added, 1)
                if more:
                    k_norm(g + 1, 3)

            with dve.Fori(0, NG - 1) as g:
                group(g, True)
            group(NG - 1, False)
            dve.wait_ge(o_added, NG + 1)
            dve.sem_inc(x_ready, 1)

            layer_norm(1)

            def qkv_low(n, slot):
                for c in range(KC):
                    dve.wait_ge(bq_hi_done, KC * (n - 1) + c + 1)
                    dve.tensor_tensor(bq_lo[:, slot, c, :], wqkv[:, slot, c, :], bq_hi[:, slot, c, :].bitcast(F32),
                                      ALU.subtract).then_inc(bq_lo_done, 1)

            def outputs_low(g):
                dve.wait_ge(b_oT_hi_done, g + 1)
                dve.tensor_tensor(b_oT_lo[:, :, :], b_oT[:, :, :], b_oT_hi[:, :, :].bitcast(F32), ALU.subtract)\
                    .then_inc(b_oT_lo_done, 1)

            def attend(g, slot, first=False):
                dve.wait_ge(b_qk_turned, g + 1)
                dve.tensor_scalar(b_qT[:, :, :], bank[2][:, :].rearrange("p (h q) -> p h q", h=R), SCALE, None,
                                  ALU.mult).then_inc(b_qT_kept, 1)
                if not first:
                    outputs_low(g - 1)
                dve.wait_ge(b_s_full, g + 1)
                dve.sem_inc(s_seen, 1)
                for h in range(R):
                    dve.tensor_tensor_reduce(
                        out=b_p[:, h, :], in0=bank[4][:, P * h:P * h + P], in1=band[:, :], scale=1.0, scalar=NEG,
                        op0=ALU.add, op1=ALU.max, accum_out=b_mx[:, h:h + 1]).then_inc(b_masked, 1)
                dve.wait_ge(b_masked, 4 * g + 4)
                dve.tensor_scalar(b_nm[:, :], b_mx[:, :], -1.0, None, ALU.mult).then_inc(b_max, 1)
                dve.wait_ge(b_exp, 4 * g + 4)
                dve.reciprocal(b_rs[:, :], b_sum[:, :]).then_inc(b_inverse, 1)
                dve.wait_ge(b_inverse, g + 1)
                dve.tensor_tensor(b_p[:, :, :], b_p[:, :, :], b_rs[:, :].unsqueeze(2).broadcast_to([P, R, P]),
                                  ALU.mult).then_inc(b_normed, 1)
                if not last(g, 2):
                    qkv_low(g + 2, slot)
                dve.wait_ge(b_pv_done, g + 1)
                dve.tensor_copy(b_oT[:, :, :], bank[6][:, :].rearrange("p (h q) -> p h q", h=R))\
                    .then_inc(b_oT_kept, 1)

            dve.wait_ge(xnT_hi_done, 2)
            dve.tensor_tensor(b_xnT_lo[:, :, :], xnT[:, :, :], b_xnT_hi[:, :, :].bitcast(F32), ALU.subtract)\
                .then_inc(xnT_lo_done, 1)
            dve.wait_ge(band_ready, 3)
            attend(0, 0, True)
            with dve.Fori(0, NG // 2 - 2) as i:
                attend(2 * i + 1, 1)
                attend(2 * i + 2, 0)
            for g in range(NG - 3, NG):
                attend(g, g % 2)
            outputs_low(NG - 1)
            dve.wait_ge(b_o_done, NG)
            dve.tensor_copy(x[:, :], bank[7][:, :]).then_inc(x_ready, 1)

            layer_norm(2)
            dve.wait_ge(small_in, 3 * DMA)
            dve.wait_ge(router_full, 1)
            dve.tensor_tensor(logits[:, :], bank[0][:, 0:E], rb[:, :], ALU.add).then_inc(router_step, 1)
            dve.wait_ge(router_step, 1)
            dve.tensor_reduce(r_nm[:, :], logits[:, :], AX.X, ALU.max, negate=True).then_inc(router_step, 1)
            dve.wait_ge(router_act, 1)
            dve.reciprocal(r_rs[:, :], r_sum[:, :]).then_inc(router_step, 1)
            dve.wait_ge(router_step, 3)
            dve.tensor_scalar(logits[:, :], logits[:, :], r_rs[:, 0:1], None, ALU.mult).then_inc(router_step, 1)
            dve.wait_ge(router_step, 4)
            dve.max(out=top8[:, :], in_=logits[:, :]).then_inc(router_step, 1)
            dve.wait_ge(router_step, 5)
            dve.tensor_scalar(above[:, :], logits[:, :], top8[:, TOP - 1:TOP], 0.0, ALU.is_gt, ALU.add,
                              accum_out=r_gt[:, 0:1]).then_inc(router_step, 1)
            dve.tensor_scalar(same[:, :], logits[:, :], top8[:, TOP - 1:TOP], None, ALU.is_equal)\
                .then_inc(router_step, 1)
            dve.wait_ge(router_step, 7)
            dve.tensor_tensor_scan(rank[:, :], ones[:, 0:E], same[:, :], 0.0, ALU.mult, ALU.add)\
                .then_inc(router_step, 1)
            dve.tensor_scalar(room[:, :], r_gt[:, :], -1.0, float(TOP), ALU.mult, ALU.add).then_inc(router_step, 1)
            dve.wait_ge(router_step, 9)
            dve.scalar_tensor_tensor(out=same[:, :], in0=rank[:, :], scalar=room[:, 0:1], in1=same[:, :],
                                     op0=ALU.is_le, op1=ALU.mult).then_inc(router_step, 1)
            dve.wait_ge(router_step, 10)
            dve.tensor_tensor(above[:, :], above[:, :], same[:, :], ALU.add).then_inc(router_step, 1)
            dve.wait_ge(router_step, 11)
            dve.tensor_tensor_reduce(out=w_dense[:, :], in0=logits[:, :], in1=above[:, :], scale=1.0, scalar=0.0,
                                     op0=ALU.mult, op1=ALU.add, accum_out=w_sum[:, 0:1]).then_inc(router_step, 1)
            dve.wait_ge(router_step, 12)
            dve.scalar_tensor_tensor(out=x[:, :], in0=xn[:, :], scalar=w_sum[:, 0:1], in1=x[:, :],
                                     op0=ALU.mult, op1=ALU.add).then_inc(router_step, 1)
            dve.wait_ge(router_step, 13)
            dve.wait_ge(router_full, 3)
            dve.tensor_tensor(x[:, :], x[:, :], bank[1][:, :], ALU.add).then_inc(x_ready, 1)

            layer_norm(3)
            dve.wait_ge(d_kept, 2)
            dve.tensor_tensor(d_qkT_lo[:, :, :], bank[5][:, :].rearrange("p (c t) -> p c t", c=KC),
                              d_qkT_hi[:, :, :].bitcast(F32), ALU.subtract).then_inc(d_step, 1)
            dve.wait_ge(fold_full, 7)
            dve.tensor_copy(d_qb[:, :], bank[7][:, 8:9]).then_inc(d_step, 1)
            for b in range(TB):
                dve.wait_ge(d_s_full, b + 1)
                dve.tensor_reduce(d_mx[:, b:b + 1], bank[b][:, :], AX.X, ALU.max).then_inc(d_s_maxed, 1)
            dve.wait_ge(d_s_maxed, TB)
            dve.tensor_reduce(d_m[:, :], d_mx[:, :], AX.X, ALU.max).then_inc(d_step, 1)
            dve.wait_ge(d_step, 3)
            dve.tensor_scalar(d_nm[:, :], d_m[:, :], d_qb[:, 0:1], None, ALU.add).then_inc(d_step, 1)
            dve.wait_ge(d_step, 4)
            dve.tensor_scalar(d_bias[:, :], d_nm[:, :], -1.0, d_qb[:, 0:1], ALU.mult, ALU.add).then_inc(d_step, 1)
            dve.wait_ge(d_step, 5)
            dve.tensor_scalar(d_bias[:, :], d_bias[:, :], D ** -0.5, None, ALU.mult).then_inc(d_step, 1)
            dve.wait_ge(d_exp, TB)
            dve.tensor_reduce(d_sum[:, :], d_mx[:, :], AX.X, ALU.add).then_inc(d_step, 1)
            dve.wait_ge(d_step, 7)
            dve.reciprocal(d_rs[:, :], d_sum[:, :]).then_inc(d_step, 1)
            dve.wait_ge(d_step, 8)
            dve.wait_ge(d_done, 1)
            dve.scalar_tensor_tensor(out=x[:, :], in0=bank[6][:, :], scalar=d_rs[:, 0:1], in1=x[:, :],
                                     op0=ALU.mult, op1=ALU.add).then_inc(x_ready, 1)
            layer_norm(4)
            dve.wait_ge(xnT_hi_done, 3)
            dve.tensor_tensor(xnT_lo[:, :, :], xnT[:, :, :], xnT_hi[:, :, :].bitcast(F32), ALU.subtract)\
                .then_inc(xnT_lo_done, 1)
            dve.wait_ge(m_small_in, 6 * DMA)
            dve.wait_ge(dt_full, 1)
            dve.tensor_tensor(z[:, :], bank[6][:, 0:NG * MH], m_dtb[:, :], ALU.add).then_inc(dt_step, 1)
            dve.wait_ge(dt_step, 1)
            dve.scalar_tensor_tensor(out=ea[:, :], in0=z[:, :], scalar=-1.0, in1=z[:, :], op0=ALU.mult,
                                     op1=ALU.max).then_inc(dt_step, 1)
            dve.wait_ge(dt_act, 1)
            dve.tensor_scalar(ue[:, :], ea[:, :], 1.0, None, ALU.add).then_inc(dt_step, 1)
            dve.wait_ge(dt_step, 3)
            dve.tensor_scalar(wd[:, :], ue[:, :], -1.0, 1e-30, ALU.add, ALU.max).then_inc(dt_step, 1)
            dve.wait_ge(dt_step, 4)
            dve.reciprocal(wd[:, :], wd[:, :]).then_inc(dt_step, 1)
            dve.wait_ge(dt_act, 2)
            dve.tensor_tensor(ea[:, :], ea[:, :], lnu[:, :], ALU.mult).then_inc(dt_step, 1)
            dve.wait_ge(dt_step, 6)
            dve.tensor_tensor(ea[:, :], ea[:, :], wd[:, :], ALU.mult).then_inc(dt_step, 1)
            dve.wait_ge(dt_step, 7)
            dve.scalar_tensor_tensor(out=dt[:, :], in0=z[:, :], scalar=0.0, in1=ea[:, :], op0=ALU.max,
                                     op1=ALU.add).then_inc(dt_step, 1)
            dve.wait_ge(dt_step, 8)
            dve.tensor_scalar(dt[:, :], dt[:, :], DT_MIN, DT_MAX, ALU.max, ALU.min).then_inc(dt_step, 1)
            dve.wait_ge(dt_step, 9)
            dve.wait_ge(m_small_in, 8 * DMA)
            dve.tensor_tensor(da[:, :], dt[:, :], m_a[:, :], ALU.mult).then_inc(dt_step, 1)
            dve.wait_ge(dt_act, 3)
            dve.tensor_tensor(da_lo[:, :], da[:, :], da_hi[:, :].bitcast(F32), ALU.subtract).then_inc(dt_step, 1)

            def m_group(g, first):
                def y_gate(g):
                    dve.wait_ge(m_y, g + 1)
                    dve.wait_ge(m_xd, g + 1)
                    for i in range(2):
                        h = slice(512 * i, 512 * i + 512)
                        dve.tensor_tensor(y[:, h], bank[1 + i][:, :], y[:, h], ALU.add).then_inc(m_ysum, 1)
                    for i in range(2):
                        h = slice(512 * i, 512 * i + 512)
                        dve.wait_ge(m_ysum, 2 * g + i + 1)
                        dve.wait_ge(m_sg, 2 * g + i + 1)
                        dve.tensor_tensor(y[:, h], y[:, h], sg[:, h], ALU.mult).then_inc(m_yg, 1)

                def y_mean(g):
                    dve.wait_ge(m_sq, g + 1)
                    dve.tensor_scalar(yms[:, :], yssq[:, :], 1.0 / MC, EPS, ALU.mult, ALU.add).then_inc(m_yms, 1)

                def y_norm(g):
                    dve.wait_ge(m_rstd, g + 1)
                    dve.tensor_scalar(y[:, :], y[:, :], yrstd[:, 0:1], None, ALU.mult).then_inc(m_yn, 1)

                def keep_yT(g):
                    for i in range(2):
                        dve.wait_ge(m_yT, 2 * g + i + 1)
                        dve.tensor_tensor(
                            yT[:, 4 * i:4 * i + 4, :], bank[3 + i][:, :].rearrange("p (c t) -> p c t", c=4),
                            m_nw[:, bass.ds(g, 1), 4 * i:4 * i + 4].rearrange("p a c -> p (a c)").unsqueeze(2)
                            .broadcast_to([P, 4, P]), ALU.mult).then_inc(m_yTk, 1)

                def conv(js, before):
                    for k in range(TAPS - 2, -1, -1):
                        back = TAPS - 1 - k
                        for i, j in enumerate(js):
                            b, r = (0, j) if j < 2 else (1 + (j - 2) // 4, (j - 2) % 4)
                            if back == 1:
                                dve.wait_ge(m_tap, NCH * g + js[-1] + 1)
                            else:
                                dve.wait_ge(m_conv, STEPS * g + before + (back - 2) * len(js) + i + 1)
                            dve.scalar_tensor_tensor(
                                out=xc[:, j, back:], in0=bank[b][:, P * r:P * r + P - back],
                                scalar=m_taps[:, bass.ds(TAPS * (NCH * g + j) + k, 1)], in1=xc[:, j, back:],
                                op0=ALU.mult, op1=ALU.add).then_inc(m_conv, 1)

                if first == "end":
                    y_gate(NG - 1)
                    y_mean(NG - 1)
                    y_norm(NG - 1)
                    keep_yT(NG - 1)
                    return
                if not first:
                    y_gate(g - 1)
                    y_mean(g - 1)
                    y_norm(g - 1)
                conv(range(2), 0)
                if not first:
                    keep_yT(g - 1)
                conv(range(2, 6), 6)
                dve.wait_ge(m_gfull, g + 1)
                dve.tensor_tensor(gm[:, :], bank[0][:, 256:256 + P], upto[:, :], ALU.mult).then_inc(m_gm, 1)
                if not first:
                    for c in (2, 3):
                        dve.wait_ge(wg_hi_done, KC * g + c + 1)
                        dve.tensor_tensor(wg_lo[:, c, :], m_wg[:, c, :], wg_hi[:, c, :].bitcast(F32), ALU.subtract)\
                            .then_inc(wg_lo2_done, 1)
                conv(range(6, 10), 18)
                dve.wait_ge(m_gm, g + 1)
                for q in range(4):
                    dve.wait_ge(m_exp, 4 * g + q + 1)
                    dve.tensor_tensor(m_e[:, 4 * q:4 * q + 4, :], m_e[:, 4 * q:4 * q + 4, :],
                                      gm[:, :].unsqueeze(1).broadcast_to([P, 4, P]), ALU.mult).then_inc(m_m, 1)
                dve.wait_ge(m_xtok, 2 * g + 2)
                dve.tensor_tensor(xdt[:, :, :], x_tok[:, :, :],
                                  dt[:, bass.ds(MH * g, MH)].unsqueeze(2).broadcast_to([P, MH, MP]), ALU.mult)\
                    .then_inc(m_xdt, 1)

            m_group(0, True)
            with dve.Fori(0, NG - 1) as i:
                m_group(i + 1, False)
            m_group(NG, "end")
            for e in range(EARLY // 2, EARLY):
                dve.wait_ge(ew_hi_done, e + 1)
                dve.tensor_tensor(ew_lo[:, e], ew[:, e], ew_hi[:, e].bitcast(F32), ALU.subtract)\
                    .then_inc(ew_lo2_done, 1)
            dve.wait_ge(m_out, NG)
            dve.tensor_copy(x[:, :], bank[7][:, :]).then_inc(x_ready, 1)
            layer_norm(5)
            dve.wait_ge(xnT_hi_done, 4)
            dve.tensor_tensor(xnT_lo[:, :, :], xnT[:, :, :], xnT_hi[:, :, :].bitcast(F32), ALU.subtract)\
                .then_inc(xnT_lo_done, 1)
            dve.wait_ge(router_full, 4)
            dve.tensor_copy(f_l[:, :], bank[0][:, 0:NE]).then_inc(f_step, 1)
            dve.wait_ge(f_step, 1)
            dve.max(out=f_top[:, :], in_=f_l[:, :]).then_inc(f_step, 1)
            dve.wait_ge(f_step, 2)
            dve.tensor_scalar(f_nm[:, :], f_top[:, 0:1], -1.0, None, ALU.mult).then_inc(f_step, 1)
            dve.tensor_scalar(f_above[:, :], f_l[:, :], f_top[:, TOP2 - 1:TOP2], 0.0, ALU.is_gt, ALU.add,
                              accum_out=f_gt[:, 0:1]).then_inc(f_step, 1)
            dve.tensor_scalar(f_same[:, :], f_l[:, :], f_top[:, TOP2 - 1:TOP2], None, ALU.is_equal)\
                .then_inc(f_step, 1)
            dve.wait_ge(f_step, 5)
            dve.tensor_tensor_scan(f_rank[:, :], ones[:, 0:NE], f_same[:, :], 0.0, ALU.mult, ALU.add)\
                .then_inc(f_step, 1)
            dve.tensor_scalar(f_room[:, :], f_gt[:, :], -1.0, float(TOP2), ALU.mult, ALU.add).then_inc(f_step, 1)
            dve.wait_ge(f_step, 7)
            dve.scalar_tensor_tensor(out=f_same[:, :], in0=f_rank[:, :], scalar=f_room[:, 0:1], in1=f_same[:, :],
                                     op0=ALU.is_le, op1=ALU.mult).then_inc(f_step, 1)
            dve.wait_ge(f_step, 8)
            dve.tensor_tensor(f_above[:, :], f_above[:, :], f_same[:, :], ALU.add).then_inc(f_step, 1)
            dve.wait_ge(f_step, 9)
            dve.wait_ge(f_exp, 1)
            dve.tensor_tensor_reduce(out=f_w[:, :], in0=f_l[:, :], in1=f_above[:, :], scale=1.0, scalar=0.0,
                                     op0=ALU.mult, op1=ALU.add, accum_out=f_sum[:, 0:1]).then_inc(f_step, 1)
            dve.wait_ge(f_step, 10)
            dve.reciprocal(f_rs[:, :], f_sum[:, :]).then_inc(f_step, 1)
            dve.wait_ge(f_step, 11)
            dve.tensor_scalar(f_w[:, :], f_w[:, :], f_rs[:, 0:1], None, ALU.mult).then_inc(f_step, 1)
            dve.wait_ge(f_step, 12)
            dve.sem_inc(f_used, CREDIT)
            with dve.Fori(0, NE // 2) as i:
                for b in range(2):
                    dve.wait_ge(f_prod, 2 * i + b + 1)
                    dve.wait_ge(f_used, CREDIT + 2 * i + b)
                    dve.scalar_tensor_tensor(out=x[:, :], in0=bank[2 + b][:, :], scalar=f_w[:, bass.ds(2 * i + b, 1)],
                                             in1=x[:, :], op0=ALU.mult, op1=ALU.add).then_inc(f_used, 1)
            dve.wait_ge(f_used, CREDIT + NE)
            dve.sem_inc(x_ready, 1)

        @block.tensor
        def _(pe):
            def turn_x(k, src):
                for c in range(KC):
                    mm = pe.transpose(TR[0][:, c * P:c * P + P], src[:, c * P:c * P + P], ident[:, :])
                mm.then_inc(ln_turned, 1)

            def kv_tile(g, t):
                u = t // 2
                if t % 2 == 0:
                    pe.wait_ge(kv_kept, 8 * g + u + 1)
                if t == 0:
                    pe.wait_ge(kvw_lo_done, g + 1)
                b, r = t // 4, P * (t % 4)
                acc = KV[u % 2][:, (t % 2) * 2 * HD:(t % 2 + 1) * 2 * HD]
                for c in range(KC):
                    hi, lo = ctx_hi[:, b, c, r:r + P], ctx_lo[:, b, c, r:r + P]
                    pe.matmul(acc, hi, kvw_hi[:, c, :], start=(c == 0), stop=False)
                    pe.matmul(acc, hi, kvw_lo[:, c, :], start=False, stop=False)
                    mm = pe.matmul(acc, lo, kvw_hi[:, c, :], start=False, stop=(c == KC - 1))
                if t % 2 == 1:
                    mm.then_inc(kv_full, 1)

            pe.wait_ge(const_ready, 4)
            pe.sem_inc(pv_done, 1)
            for t in range(TT):
                if t == 4:
                    pe.wait_ge(ln_x, 1)
                    turn_x(0, xn)
                if t % 4 == 0:
                    pe.wait_ge(ctx_lo_done, 2 * (t // 4) + 2)
                kv_tile(0, t)

            def group(g, more):
                def turn_k(b):
                    pe.wait_ge(k_normed, 4 * g + b + 1)
                    pe.wait_ge(lo_kept, 20 * g + b + 1)
                    for i in range(4):
                        mm = pe.transpose(TR[b][:, P * i:P * i + P], kv_raw[:, 4 * b + i, 0:HD], ident[:, :])
                    mm.then_inc(turned, 1)

                def turn_p(c):
                    pe.wait_ge(lo_kept, 20 * g + 4 + c + 1)
                    if c == 0:
                        pe.wait_ge(s_masked, len(S) + 16 * g + 13)
                    for h in range(R):
                        if h < R - 1 and c == 0:
                            pe.wait_ge(p_ready, PARTS * g + h + 1)
                        if h == R - 1 and c % 4 == 0:
                            pe.wait_ge(p_ready, PARTS * g + R + c // 4)
                        mm = pe.transpose(TR[c % 4][:, P * h:P * h + P], scores[:, h, P * c:P * c + P], ident[:, :])
                    mm.then_inc(turned, 1)

                def pv(c):
                    if c == 0:
                        pe.wait_ge(ot_kept, g + 1)
                        pe.wait_ge(v_lo_done, 4 * g + 4)
                    pe.wait_ge(lo_kept, len(TR) + 20 * g + 4 + c + 1)
                    pe.matmul(OT[:, :], v_hi[:, c, :], pt_hi[:, c % PR, :], start=(c == 0), stop=False)
                    pe.matmul(OT[:, :], v_lo[:, c, :], pt_hi[:, c % PR, :], start=False, stop=False)
                    pe.matmul(OT[:, :], v_hi[:, c, :], pt_lo[:, c % 2, :], start=False, stop=(c == TT - 1))\
                        .then_inc(pv_done, 1)

                def ahead(*tiles):
                    if more:
                        for t in tiles:
                            kv_tile(g + 1, t)

                turn_k(0)
                turn_k(1)
                pe.wait_ge(o_added, g + 1)
                pe.wait_ge(xnT_lo_done, 1)
                for c in range(KC):
                    pe.wait_ge(a_wq_lo_done, KC * g + c + 1)
                    pe.matmul(M[:, :], a_xnT_hi[:, c, :], a_wq_hi[:, c, :], start=(c == 0), stop=False)
                    pe.matmul(M[:, :], a_xnT_hi[:, c, :], a_wq_lo[:, c, :], start=False, stop=False)
                    mm = pe.matmul(M[:, :], a_xnT_lo[:, c, :], a_wq_hi[:, c, :], start=False, stop=(c == KC - 1))
                mm.then_inc(q_full, 1)
                turn_k(2)
                turn_k(3)
                ahead(0, 1)
                pe.wait_ge(q_normed, g + 1)
                for h in range(R):
                    mm = pe.transpose(M[:, P * h:P * h + P], q_sb[:, h, :], ident[:, :])
                mm.then_inc(qt_full, 1)
                ahead(2, 3)
                pe.wait_ge(qt_lo_done, g + 1)
                for h in range(R):
                    for b in range(TB):
                        if h == 0:
                            pe.wait_ge(lo_kept, len(TR) + 20 * g + b + 1)
                        pe.wait_ge(s_masked, 16 * g + 4 * h + b + 1)
                        k_hi, k_lo = kt_hi[:, 512 * b:512 * b + 512], kt_lo[:, 512 * b:512 * b + 512]
                        pe.matmul(S[b][:, :], qt_hi[:, h, :], k_hi, start=True, stop=False)
                        pe.matmul(S[b][:, :], qt_hi[:, h, :], k_lo, start=False, stop=False)
                        pe.matmul(S[b][:, :], qt_lo[:, h, :], k_hi, start=False, stop=True).then_inc(s_full, 1)
                    ahead(*((4,), (5,), (), (6, 7))[h])
                turn_p(0)
                ahead(8)
                turn_p(1)
                for c in range(TT):
                    if c + 2 < TT:
                        turn_p(c + 2)
                    pv(c)
                    if c in (2, 5, 8, 11):
                        ahead(9 + (c - 2) // 3)
                    if c == 6:
                        pe.wait_ge(dg_done, g + 1)
                        pe.matmul(M[:, :], ones[:, :], dg[:, :, :].rearrange("p h q -> p (h q)"),
                                  start=True, stop=True).then_inc(inverse_full, 1)
                ahead(13, 14, 15)
                if more:
                    pe.wait_ge(a_wo_lo_done, 4 * g + 4)
                    pe.wait_ge(ot_lo_done, g + 1)
                    for h in range(R):
                        pe.matmul(M[:, :], a_ot_hi[:, h, :], a_wo_hi[:, h, :], start=(h == 0), stop=False)
                        pe.matmul(M[:, :], a_ot_hi[:, h, :], a_wo_lo[:, h, :], start=False, stop=False)
                        mm = pe.matmul(M[:, :], ot_lo[:, h, :], a_wo_hi[:, h, :], start=False, stop=(h == R - 1))
                else:
                    pe.wait_ge(wo_in, DMA * (g + 1))
                    pe.wait_ge(ot_kept, g + 2)
                    for h in range(R):
                        mm = pe.matmul(M[:, :], ot[:, h, :], wo[:, h, :], start=(h == 0), stop=(h == R - 1))
                mm.then_inc(o_full, 1)

            with pe.Fori(0, NG - 1) as g:
                group(g, True)
            group(NG - 1, False)

            pe.wait_ge(x_ready, 2)
            pe.matmul(bank[7][:, :], ident[:, :], x[:, :], start=True, stop=False)
            pe.wait_ge(ln_x, 2)
            turn_x(1, xn)
            pe.wait_ge(ln_xT, 2)

            def project(to, n, slot, first, last_col, done):
                cols = slice(first, last_col)
                for c in range(KC):
                    start, stop = c == 0, c == KC - 1
                    if isinstance(n, int) and n <= 1:
                        if n == 1:
                            pe.wait_ge(bq_lo1_done, c + 1)
                    else:
                        pe.wait_ge(bq_lo_done, KC * (n - 2) + c + 1)
                    if isinstance(n, int) and n == 0:
                        mm = pe.matmul(to, xnT[:, c, :], wqkv[:, slot, c, cols], start=start, stop=stop)
                    else:
                        pe.matmul(to, b_xnT_hi[:, c, :], bq_hi[:, slot, c, cols], start=start, stop=False)
                        pe.matmul(to, b_xnT_hi[:, c, :], bq_lo[:, slot, c, cols], start=False, stop=False)
                        mm = pe.matmul(to, b_xnT_lo[:, c, :], bq_hi[:, slot, c, cols], start=False, stop=stop)
                mm.then_inc(done, 1)

            def project_kv(n, slot):
                project(bank[1][:, 0:2 * HD], n, slot, R * HD, (R + 2) * HD, b_kv_full)

            def project_q(n, slot):
                project(bank[0][:, :], n, slot, 0, R * HD, b_q_full)

            def project_out(g, slot, hs):
                pe.wait_ge(b_oT_lo_done, g + 1)
                for h in hs:
                    pe.wait_ge(bo_lo_done, R * g + h + 1)
                    pe.matmul(bank[7][:, :], b_oT_hi[:, h, :], bo_hi[:, slot, h, :], start=False, stop=False)
                    pe.matmul(bank[7][:, :], b_oT_hi[:, h, :], bo_lo[:, slot, h, :], start=False, stop=False)
                    mm = pe.matmul(bank[7][:, :], b_oT_lo[:, h, :], bo_hi[:, slot, h, :], start=False,
                                   stop=(last(g, 1) and h == R - 1))
                if hs[-1] == R - 1:
                    mm.then_inc(b_o_done, 1)

            def fold(j, to):
                for c in range(KC):
                    mm = pe.matmul(to, c_q[:, c, P * j:P * j + P], c_k[:, c, :], start=(c == 0), stop=(c == KC - 1))
                mm.then_inc(fold_full, 1)

            def attend(g, slot, first=False):
                pe.wait_ge(b_q_kept, g + 1)
                pe.wait_ge(b_kv_kept, g + 1)
                for h in range(R):
                    pe.transpose(bank[2][:, P * h:P * h + P], b_q[:, h, :], ident[:, :])
                pe.transpose(bank[3][:, 0:P], b_kv[:, slot, 0:HD], ident[:, :]).then_inc(b_qk_turned, 1)
                if not last(g, 1):
                    if first:
                        pe.wait_ge(xnT_lo_done, 2)
                    project_kv(g + 1, 1 - slot)
                pe.wait_ge(b_qT_kept, g + 1)
                pe.wait_ge(b_kT_kept, g + 1)
                for h in range(R):
                    mm = pe.matmul(bank[4][:, P * h:P * h + P], b_qT[:, h, :], b_kT[:, :], start=True, stop=True)
                mm.then_inc(b_s_full, 1)
                if not last(g, 1):
                    project_q(g + 1, 1 - slot)
                else:
                    pe.wait_ge(c_in, 4 * DMA)
                    fold(0, bank[0][:, :])
                if not first:
                    project_out(g - 1, 1 - slot, range(0, 2))
                pe.wait_ge(b_normed, g + 1)
                for h in range(R):
                    mm = pe.transpose(bank[5][:, P * h:P * h + P], b_p[:, h, :], ident[:, :])
                mm.then_inc(b_p_turned, 1)
                if not first:
                    project_out(g - 1, 1 - slot, range(2, R))
                pe.wait_ge(b_pT_kept, g + 1)
                pe.matmul(bank[6][:, :], b_kv[:, slot, HD:], b_pT[:, :, :].rearrange("p h q -> p (h q)"),
                          start=True, stop=True).then_inc(b_pv_done, 1)

            pe.wait_ge(wqkv_in[0], DMA)
            project_kv(0, 0)
            project_q(0, 0)
            attend(0, 0, True)
            with pe.Fori(0, NG // 2 - 2) as i:
                attend(2 * i + 1, 1)
                attend(2 * i + 2, 0)
            for g in range(NG - 3, NG):
                attend(g, g % 2)
            for c in range(KC):
                mm = pe.matmul(bank[1][0:1, :], bqc[:, c:c + 1], c_k[:, c, :], start=(c == 0), stop=(c == KC - 1))
            mm.then_inc(fold_full, 1)
            project_out(NG - 1, 1, range(R))

            fold(1, bank[2][:, :])
            pe.wait_ge(ln_x, 3)
            turn_x(2, xn)
            pe.wait_ge(ln_xT, 3)
            pe.wait_ge(small_in, 3 * DMA)
            pe.wait_ge(fold_kept, 1)
            for c in range(KC):
                mm = pe.matmul(bank[0][:, 0:E], xnT[:, c, :], rw[:, c, :], start=(c == 0), stop=(c == KC - 1))
            mm.then_inc(router_full, 1)
            fold(2, bank[6][:, :])
            pe.wait_ge(router_step, 12)
            pe.transpose(bank[5][0:E, 0:P], w_dense[:, :], ident[:, :]).then_inc(router_full, 1)
            pe.wait_ge(router_act, 2)
            pe.wait_ge(fold_kept, 2)
            pe.matmul(bank[1][:, :], w_T[:, :], eb[:, :], start=True, stop=True).then_inc(router_full, 1)
            fold(3, bank[7][:, :])

            pe.wait_ge(ln_x, 4)
            turn_x(3, xn)
            pe.wait_ge(ln_xT, 4)
            pe.wait_ge(fold_kept, 5)
            for c in range(KC):
                pe.matmul(bank[0][:, :], xnT[:, c, :], wqk[:, c, :], start=(c == 0), stop=False)
            pe.matmul(bank[0][:, :], ones[0:1, :], b_row[:, :], start=False, stop=True).then_inc(d_full, 1)
            for j in range(KC):
                for c in range(KC):
                    pe.matmul(bank[7][:, j:j + 1], c_q[:, c, P * j:P * j + P], bkc[:, c:c + 1], start=(c == 0),
                              stop=(c == KC - 1))
            for c in range(KC):
                mm = pe.matmul(bank[7][0:1, KC:KC + 1], bqc[:, c:c + 1], bkc[:, c:c + 1], start=(c == 0),
                               stop=(c == KC - 1))
            mm.then_inc(fold_full, 1)
            pe.wait_ge(d_kept, 1)
            for c in range(KC):
                mm = pe.transpose(bank[5][:, P * c:P * c + P], d_q[:, P * c:P * c + P], ident[:, :])
            mm.then_inc(d_full, 1)
            pe.wait_ge(fold_kept, 7)
            for c in range(KC):
                pe.matmul(bank[7][:, 8:9], xnT[:, c, :], v_col[:, c:c + 1], start=(c == 0), stop=False)
            pe.matmul(bank[7][:, 8:9], ones[0:1, :], b_one[:, :], start=False, stop=True).then_inc(fold_full, 1)
            pe.wait_ge(d_step, 1)
            for b in range(TB):
                for c in range(KC):
                    hi, lo = ctx_hi[:, b, c, :], ctx_lo[:, b, c, :]
                    pe.matmul(bank[b][:, :], d_qkT_hi[:, c, :], hi, start=(c == 0), stop=False)
                    pe.matmul(bank[b][:, :], d_qkT_hi[:, c, :], lo, start=False, stop=False)
                    mm = pe.matmul(bank[b][:, :], d_qkT_lo[:, c, :], hi, start=False, stop=(c == KC - 1))
                mm.then_inc(d_s_full, 1)
            for b in range(TB):
                pe.wait_ge(d_exp, b + 1)
                if b >= 2:
                    pe.wait_ge(d_pT_kept, b - 1)
                for i in range(4):
                    t = 4 * b + i
                    mm = pe.transpose(bank[4 + b % 2][:, P * i:P * i + P], d_p[:, P * t:P * t + P], ident[:, :])
                mm.then_inc(d_turned, 1)
            pe.wait_ge(ctx_n_in, DMA)
            for b in range(TB):
                pe.wait_ge(d_pT_kept, b + 1)
                for i in range(4):
                    t = 4 * b + i
                    mm = pe.matmul(bank[6][:, :], d_pT[:, b, i, :], ctx_n[:, t, :], start=(t == 0),
                                   stop=(t == TT - 1))
            mm.then_inc(d_done, 1)
            pe.wait_ge(x_ready, 5)
            pe.matmul(bank[7][:, :], ident[:, :], x[:, :], start=True, stop=False)
            pe.wait_ge(ln_x, 5)
            turn_x(4, xn)
            pe.wait_ge(ln_xT, 5)
            pe.wait_ge(m_small_in, 6 * DMA)
            for c in range(KC):
                mm = pe.matmul(bank[6][:, 0:NG * MH], xnT[:, c, :], m_wdt[:, c, :], start=(c == 0),
                               stop=(c == KC - 1))
            mm.then_inc(dt_full, 1)

            def m_outputs_turned(g):
                pe.wait_ge(m_yn, g + 1)
                for i in range(2):
                    for j in range(4):
                        n = P * (4 * i + j)
                        mm = pe.transpose(bank[3 + i][:, P * j:P * j + P], y[:, n:n + P], ident[:, :])
                    mm.then_inc(m_yT, 1)

            def m_project_out(g, last):
                pe.wait_ge(m_wo_in, DMA * (g + 1))
                for c in range(MCC):
                    if c % 4 == 0:
                        pe.wait_ge(m_yTk, 2 * g + c // 4 + 1)
                    mm = pe.matmul(bank[7][:, :], yT[:, c, :], m_wo[:, c, :], start=False,
                                   stop=(last and c == MCC - 1))
                mm.then_inc(m_out, 1)

            def m_group(g, first):
                def seg(q):
                    pe.wait_ge(m_r, 8 * g + 2 * q + 2)
                    if q >= 2:
                        pe.wait_ge(m_exp, 4 * g + q - 1)
                    elif first:
                        pe.wait_ge(m_silu, 3)
                    for part, stop in ((r_hi, False), (r_lo, True)):
                        mm = pe.matmul(bank[(1 if first else 5) + q % 2][:, :], later[:, :],
                                       part[:, 4 * q:4 * q + 4, :].rearrange("p h n -> p (h n)"),
                                       start=not stop, stop=stop)
                    mm.then_inc(m_seg, 1)

                def channels(js):
                    for j in js:
                        b, r = (0, j) if j < 2 else (1 + (j - 2) // 4, (j - 2) % 4)
                        for c in range(KC):
                            mm = pe.matmul(bank[b][:, P * r:P * r + P], m_wx[:, c, P * j:P * j + P], xnT[:, c, :],
                                           start=(c == 0), stop=(c == KC - 1))
                    mm.then_inc(m_in, 1)

                def sources_targets():
                    pe.wait_ge(m_silu, 3 * g + 1)
                    pe.matmul(bank[0][:, 256:256 + P], xc[:, 0, :], xc[:, 1, :], start=True, stop=True)\
                        .then_inc(m_gfull, 1)

                def turn_channels():
                    for i in range(2):
                        if not first:
                            pe.wait_ge(m_exp, 4 * g + 3 + i)
                        pe.wait_ge(m_silu, 3 * g + 2 + i)
                        for j in range(4):
                            mm = pe.transpose(bank[5 + i][:, P * j:P * j + P], xc[:, 2 + 4 * i + j, :], ident[:, :])
                        mm.then_inc(m_xT, 1)

                def gates():
                    if first:
                        pe.wait_ge(xnT_lo_done, 3)
                        pe.wait_ge(wg_lo_done, KC)
                    for i in range(2):
                        for c in range(KC):
                            if not first and i == 0:
                                if c < 2:
                                    pe.wait_ge(wg_lo_done, 2 * g + c + 3)
                                else:
                                    pe.wait_ge(wg_lo2_done, 2 * g + c - 3)
                            hi, lo = wg_hi[:, c, 512 * i:512 * i + 512], wg_lo[:, c, 512 * i:512 * i + 512]
                            pe.matmul(bank[3 + i][:, :], xnT_hi[:, c, :], hi, start=(c == 0), stop=False)
                            pe.matmul(bank[3 + i][:, :], xnT_hi[:, c, :], lo, start=False, stop=False)
                            mm = pe.matmul(bank[3 + i][:, :], xnT_lo[:, c, :], hi, start=False, stop=(c == KC - 1))
                        mm.then_inc(m_gate, 1)

                if not first:
                    seg(0)
                    seg(1)
                pe.wait_ge(m_wx_in, DMA * (g + 1))
                channels(range(2))
                if first:
                    channels(range(2, 6))
                    channels(range(6, 10))
                    sources_targets()
                    gates()
                    pe.wait_ge(m_const, 5)
                    seg(0)
                    seg(1)
                    turn_channels()
                    seg(2)
                    seg(3)
                    pe.wait_ge(m_exp, 4)
                else:
                    seg(2)
                    seg(3)
                    pe.wait_ge(m_ysum, 2 * g - 1)
                    channels(range(2, 6))
                    m_outputs_turned(g - 1)
                    pe.wait_ge(m_ysum, 2 * g)
                    channels(range(6, 10))
                    sources_targets()
                    m_project_out(g - 1, False)
                    turn_channels()
                    gates()
                pe.wait_ge(m_xdt, g + 1)
                for h in range(MH):
                    if h % 4 == 0:
                        pe.wait_ge(m_m, 4 * g + h // 4 + 1)
                    mm = pe.matmul(bank[1 + h // 8][:, MP * (h % 8):MP * (h % 8) + MP], m_e[:, h, :], xdt[:, h, :],
                                   start=True, stop=True)
                mm.then_inc(m_y, 1)

            m_group(0, True)
            with pe.Fori(0, NG - 1) as i:
                m_group(i + 1, False)
            m_outputs_turned(NG - 1)
            m_project_out(NG - 1, True)
            pe.wait_ge(ln_x, 6)
            turn_x(5, xn)
            pe.wait_ge(ln_xT, 6)
            for c in range(KC):
                mm = pe.matmul(bank[0][:, 0:NE], xnT[:, c, :], gw[:, c, :], start=(c == 0), stop=(c == KC - 1))
            mm.then_inc(router_full, 1)
            pe.wait_ge(xnT_lo_done, 4)
            pe.wait_ge(ew_lo_done, EARLY // 2)
            pe.wait_ge(ew_lo2_done, EARLY // 2)

            def expert(e, b):
                for c in range(KC):
                    hi = ew_hi[:, bass.ds(e, 1), c, :].rearrange("p a n -> p (a n)")
                    lo = ew_lo[:, bass.ds(e, 1), c, :].rearrange("p a n -> p (a n)")
                    pe.matmul(bank[2 + b][:, :], xnT_hi[:, c, :], hi, start=(c == 0), stop=False)
                    pe.matmul(bank[2 + b][:, :], xnT_hi[:, c, :], lo, start=False, stop=False)
                    mm = pe.matmul(bank[2 + b][:, :], xnT_lo[:, c, :], hi, start=False, stop=(c == KC - 1))
                mm.then_inc(f_prod, 1)

            expert(0, 0)
            expert(1, 1)
            with pe.Fori(0, EARLY // 2 - 1) as i:
                for b in range(2):
                    pe.wait_ge(f_used, CREDIT + 2 * i + b + 1)
                    expert(2 * i + b + 2, b)
            for e in range(EARLY, NE):
                pe.wait_ge(ew_lo_done, EARLY // 2 + e - EARLY + 1)
                pe.wait_ge(f_used, CREDIT + e - 1)
                expert(e, e % 2)


def kernel(**inputs):
    import numpy as _np
    import concourse.bacc as _bacc
    from concourse import mybir as _mybir
    from concourse.bass_utils import run_bass_kernel_spmd as _run

    w = {k: _np.asarray(v) for k, v in inputs.items()}
    arrays = layout(w)
    nc = _bacc.Bacc("TRN2", target_bir_lowering=False, num_devices=1)
    ins = {}
    sent = {}
    for name, a in arrays.items():
        sent[name] = _np.ascontiguousarray(a)
        ins[name] = nc.dram_tensor(name, sent[name].shape, _mybir.dt.from_np(sent[name].dtype),
                                   kind="ExternalInput").ap()
    out = nc.dram_tensor("out", (P, D), F32, kind="ExternalOutput").ap()
    perceiver(nc, ins, out)
    r = _run(nc, [sent], core_ids=[0])
    return _np.asarray(r.results[0]["out"]).reshape(1, P, D)


def layout(w):
    import numpy as np

    def in_rows(m):
        return m.T.reshape(m.shape[1] // P, P, m.shape[0]).transpose(1, 0, 2)

    def by_group(m, n):
        return m.reshape(n, m.shape[0] // n, KC, P).transpose(0, 3, 2, 1)

    def out_group(m):
        return m.T.reshape(NG, R, HD, D).transpose(0, 2, 1, 3)

    ctx = w["ctx_4096"][0]
    a = {
        "x": w["x"][0],
        "ctxT": ctx.reshape(TB, 512, KC, P).transpose(0, 3, 2, 1),
        "mask": w["mask_1x1xSxS2_ff0"][0, 0],
        "a_norm": np.stack([w["L0_xattn_q_norm_w"], w["L0_xattn_k_norm_w"]], 1),
        "a_q": by_group(w["L0_xattn_q_proj_w"], NG),
        "a_kv": np.concatenate([by_group(w["L0_xattn_k_proj_w"], NG), by_group(w["L0_xattn_v_proj_w"], NG)], 3),
        "a_o": out_group(w["L0_xattn_o_proj_w"]),
    }
    a |= {
        "b_qkv": np.concatenate([by_group(w["L0_attn_" + n], NG) for n in ("wq", "wk", "wv")], 3),
        "b_o": out_group(w["L0_attn_wo"]),
        "rw": in_rows(w["L0_ffn_router_weight"]),
        "rb": w["L0_ffn_router_bias"],
        "eb": w["L0_ffn_expert_bias"],
        "c_q": w["L1_xattn_Wq"].reshape(KC, P, D).transpose(1, 0, 2),
        "c_k": w["L1_xattn_Wk"].reshape(KC, P, D).transpose(1, 0, 2),
        "bqc": w["L1_xattn_bq"].reshape(KC, P).T,
        "bkc": w["L1_xattn_bk"].reshape(KC, P).T,
        "ctx_n": ctx.reshape(TT, P, D).transpose(1, 0, 2),
    }
    inter, ng = NG * MC, NG * P
    gate, ch, bm, cm, wdt = np.split(w["L1_attn_in_proj_w"], np.cumsum([inter, inter, ng, ng]))
    n = KC, P

    def conv_rows(m):
        ch, bm, cm = np.split(m, np.cumsum([inter, ng]))
        return np.concatenate([v.reshape(NG, -1, *v.shape[1:]) for v in (bm, cm, ch)], 1)

    wx = np.concatenate([v.reshape(NG, -1, D) for v in (bm, cm, ch)], 1)
    a |= {
        "m_wx": wx.reshape(NG, NCH * P, *n).transpose(0, 3, 2, 1),
        "m_wg": by_group(gate, NG),
        "m_wo": w["L1_attn_out_proj_w"].T.reshape(NG, MCC, P, D).transpose(0, 2, 1, 3),
        "m_wdt": in_rows(wdt),
        "m_dtb": w["L1_attn_dt_bias"],
        "m_d": w["L1_attn_D"],
        "m_a": -np.arange(1, NG * MH + 1, dtype=np.float32),
        "m_taps": conv_rows(w["L1_attn_conv_w"][:, 0, :]).reshape(NG, NCH, P, TAPS).transpose(2, 0, 1, 3)
        .reshape(P, -1),
        "m_cb": conv_rows(w["L1_attn_conv_b"]).reshape(NG, NCH, P).transpose(2, 0, 1).reshape(P, -1),
        "m_nw": w["L1_attn_norm_w"].reshape(NG, MCC, P).transpose(2, 0, 1),
        "gw": w["L1_ffn_gate_w"].reshape(KC, P, NE).transpose(1, 0, 2),
        "ew": w["L1_ffn_expert_w"].reshape(NE, KC, P, D).transpose(0, 2, 1, 3),
    }
    return a
```
